# Optimizing a Trainium2 kernel written in Bass

```python
import numpy as np
import jax
import jax.numpy as jnp

def _softmax(x, axis=-1):
    return jax.nn.softmax(x, axis=axis)

def _gelu(x):
    return jax.nn.gelu(x, approximate=True)

def _silu(x):
    return jax.nn.silu(x)

def _sigmoid(x):
    return jax.nn.sigmoid(x)

def _layernorm(x, axis=-1, eps=1e-05):
    m = jnp.mean(x, axis=axis, keepdims=True)
    v = jnp.var(x, axis=axis, keepdims=True)
    return (x - m) / jnp.sqrt(v + eps)

def _scatter_add(tgt, idx, src, axis=0):
    return tgt.at[idx].add(src)

def _segment_sum(src, seg, n):
    return jax.ops.segment_sum(src, seg, n)
kernel_name = 'mk_gnn_resnorm_d4_gnn_r32_d36c5a'

def setup_inputs(seed: int=0):
    np.random.seed(seed)
    _w = jnp.asarray

    def _rec_inputs():
        import jax
        import jax.numpy as jnp
        _gk = jax.random.key(seed)
        x = -0.0005121 + 1.001 * jax.random.normal(jax.random.fold_in(_gk, 1), (3125, 160), jnp.float32)
        src = jax.random.randint(jax.random.fold_in(_gk, 2), (100000,), 0, 3125, jnp.int32)
        dst = jax.random.randint(jax.random.fold_in(_gk, 3), (100000,), 0, 3125, jnp.int32)
        _o = jnp.argsort(dst, stable=True)
        src = src[_o]
        dst = dst[_o]
        edge_attr_16 = jax.random.uniform(jax.random.fold_in(_gk, 12), (100000, 16), jnp.float32, 0.0, 1)
        edge_attr_4 = 0.000898722 + 1.00012 * jax.random.normal(jax.random.fold_in(_gk, 13), (100000, 4), jnp.float32)
        edge_attr_8 = 0.000398945 + 1.00003 * jax.random.normal(jax.random.fold_in(_gk, 14), (100000, 8), jnp.float32)
        node_vec1 = jax.random.uniform(jax.random.fold_in(_gk, 16), (3125, 1), jnp.float32, 0.0, 1)
        return (x, src, dst, edge_attr_16, edge_attr_4, edge_attr_8, node_vec1)
    x, src, dst, edge_attr_16, edge_attr_4, edge_attr_8, node_vec1 = _rec_inputs()

    def _L0_gnn_setup():
        import jax, jax.numpy as jnp
        import numpy as np
        N, E = (625, 10000)
        CS, CV = (64, 32)
        AS_, AV, H = (16, 8, 4)
        NB = 16
        SQRT3 = 1.7320508075688772
        SQRT2 = 1.4142135623730951
        EPS = 1e-05

        def _cg_tp(s, v, y0, y1, w_ss, w_sv, w_vs, w_vv0, w_vv1):
            out_s = jnp.concatenate([w_ss * s * y0[:, None], w_vv0 * (jnp.einsum('eci,ei->ec', v, y1) / SQRT3)], axis=-1)
            out_v = jnp.concatenate([(w_sv * s)[:, :, None] * y1[:, None, :], (w_vs * jnp.ones_like(v[..., 0]))[..., None] * v * y0[:, None, None], (w_vv1 * jnp.ones_like(v[..., 0]))[..., None] * (jnp.cross(v, y1[:, None, :]) / SQRT2)], axis=1)
            return (out_s, out_v)

        def _equiv_layernorm(s, v, gamma_s, beta_s, gamma_v):
            mu = jnp.mean(s, axis=-1, keepdims=True)
            var = jnp.var(s, axis=-1, keepdims=True)
            s_n = (s - mu) * jax.lax.rsqrt(var + EPS) * gamma_s + beta_s
            rms = jnp.sqrt(jnp.mean(jnp.sum(v * v, axis=-1), axis=-1, keepdims=True) + EPS)
            v_n = v / rms[..., None] * gamma_v[None, :, None]
            return (s_n, v_n)
        key = jax.random.key(seed)
        ks = jax.random.split(key, 26)

        def rn(k, shape, fan):
            return jax.random.normal(k, shape, jnp.float32) / np.sqrt(fan)
        D1S, D1V = (CS + CV, CS + 2 * CV)
        WN = 2 * CS + 3 * CV
        inp = {'node': jax.random.normal(ks[0], (N, CS + 3 * CV), jnp.float32), 'edge_index': jax.random.randint(ks[1], (2, E), 0, N, jnp.int64 if jax.config.jax_enable_x64 else jnp.int32), 'rbf': jax.random.uniform(ks[2], (E, NB), jnp.float32), 'rsh': jax.random.normal(ks[3], (E, 4), jnp.float32), 'gamma_s': jnp.ones((CS,), jnp.float32), 'beta_s': jnp.zeros((CS,), jnp.float32), 'gamma_v': jnp.ones((CV,), jnp.float32), 'Ws_src': rn(ks[4], (CS, CS), CS), 'Wv_src': rn(ks[5], (CV, CV), CV), 'Ws_dst': rn(ks[6], (CS, CS), CS), 'Wv_dst': rn(ks[7], (CV, CV), CV), 'W_rbf': rn(ks[8], (NB, WN), NB), 'W_alpha': rn(ks[9], (D1S, H * AS_), D1S), 'alpha_dot': rn(ks[10], (1, H, AS_), AS_), 'Ws_val': rn(ks[11], (D1S, CS), D1S), 'Wv_val': rn(ks[12], (D1V, CV), D1V), 'Wg': rn(ks[13], (CS, CV), CS), 'w2_ss': rn(ks[14], (CS,), 1), 'w2_sv': rn(ks[15], (CS,), 1), 'w2_vs': rn(ks[16], (CV,), 1), 'w2_vv0': rn(ks[17], (CV,), 1), 'w2_vv1': rn(ks[18], (CV,), 1), 'Ws_vlin': rn(ks[19], (D1S, H * AS_), D1S), 'Wv_vlin': rn(ks[20], (D1V, H * AV), D1V), 'Wps': rn(ks[21], (H * AS_, CS), H * AS_), 'Wpv': rn(ks[22], (H * AV, CV), H * AV)}
        return inp
    _L0_gnn_all = _L0_gnn_setup()
    _L0_gnn_in = {k: v for k, v in _L0_gnn_all.items() if k in ('gamma_s', 'beta_s', 'gamma_v', 'Ws_src', 'Wv_src', 'Ws_dst', 'Wv_dst', 'W_rbf', 'W_alpha', 'alpha_dot', 'Ws_val', 'Wv_val', 'Wg', 'w2_ss', 'w2_sv', 'w2_vs', 'w2_vv0', 'w2_vv1', 'Ws_vlin', 'Wv_vlin', 'Wps', 'Wpv')}
    del _L0_gnn_all

    def _L1_gnn_setup():
        import jax, jax.numpy as jnp
        import numpy as np
        INV3 = 1.0 / np.sqrt(3.0)

        def _fctp(x_s, x_v, attr, w0, w1):
            s = x_s @ w0 * (1.0 / np.sqrt(x_s.shape[-1])) * attr
            v = jnp.einsum('nud,uw->nwd', x_v, w1) * (1.0 / np.sqrt(x_v.shape[-2])) * attr[..., None]
            return (s, v)
        key = jax.random.key(seed)
        ks = jax.random.split(key, 16)
        N, E = (50000, 25000)
        inp = {'node_input': jax.random.normal(ks[0], (N, 160), jnp.float32), 'node_attr': jnp.ones((N, 1), jnp.float32), 'edge_attr': jax.random.normal(ks[1], (E, 4), jnp.float32), 'edge_scalars': jax.random.normal(ks[2], (E, 8), jnp.float32), 'sc_w0': jax.random.normal(ks[3], (64, 64), jnp.float32), 'sc_w1': jax.random.normal(ks[4], (32, 32), jnp.float32), 'lin1_w0': jax.random.normal(ks[5], (64, 64), jnp.float32), 'lin1_w1': jax.random.normal(ks[6], (32, 32), jnp.float32), 'fc_w1': jax.random.normal(ks[7], (8, 64), jnp.float32), 'fc_w2': jax.random.normal(ks[8], (64, 192), jnp.float32), 'lin2_w0': jax.random.normal(ks[9], (96, 64), jnp.float32), 'lin2_w1': jax.random.normal(ks[10], (96, 32), jnp.float32), 'lin3_w': jax.random.normal(ks[11], (96, 1), jnp.float32), 'edge_src': jax.random.randint(ks[12], (E,), 0, N), 'edge_dst': jax.random.randint(ks[13], (E,), 0, N), 'num_neighbors': 16}
        return inp
    _L1_gnn_all = _L1_gnn_setup()
    _L1_gnn_in = {k: v for k, v in _L1_gnn_all.items() if k in ('sc_w0', 'sc_w1', 'lin1_w0', 'lin1_w1', 'fc_w1', 'fc_w2', 'lin2_w0', 'lin2_w1', 'lin3_w')}
    del _L1_gnn_all

    def _L2_gnn_setup():
        import jax, jax.numpy as jnp
        import numpy as np
        import math
        N = 50000
        E = 15625
        MUL0 = 64
        MUL1 = 32
        MID = MUL0 + MUL1
        FC_IN = 16
        FC_H = 64
        WEIGHT_NUMEL = 2 * MUL0 + 2 * MUL1
        NUM_NEIGH = 10.0
        C_S = math.sin(math.pi / 8.0)
        C_X = math.cos(math.pi / 8.0)
        key = jax.random.key(seed)
        ks = jax.random.split(key, 14)
        f32 = jnp.float32
        return {'node_input': jax.random.normal(ks[0], (N, MUL0 + 3 * MUL1), f32), 'node_attr': jnp.ones((N, 1), f32), 'edge_src': jax.random.randint(ks[1], (E,), 0, N), 'edge_dst': jax.random.randint(ks[2], (E,), 0, N), 'edge_attr': jax.random.normal(ks[3], (E, 4), f32), 'edge_length_embedded': jax.random.uniform(ks[4], (E, FC_IN), dtype=f32), 'W_sc0': jax.random.normal(ks[5], (MUL0, MUL0), f32), 'W_sc1': jax.random.normal(ks[6], (MUL1, MUL1), f32), 'W_l1_0': jax.random.normal(ks[7], (MUL0, MUL0), f32), 'W_l1_1': jax.random.normal(ks[8], (MUL1, MUL1), f32), 'fc_W1': jax.random.normal(ks[9], (FC_IN, FC_H), f32), 'fc_W2': jax.random.normal(ks[10], (FC_H, WEIGHT_NUMEL), f32), 'W_l2_0': jax.random.normal(ks[11], (MID, MUL0), f32), 'W_l2_1': jax.random.normal(ks[12], (MID, MUL1), f32)}
    _L2_gnn_all = _L2_gnn_setup()
    _L2_gnn_in = {k: v for k, v in _L2_gnn_all.items() if k in ('W_sc0', 'W_sc1', 'W_l1_0', 'W_l1_1', 'fc_W1', 'fc_W2', 'W_l2_0', 'W_l2_1')}
    del _L2_gnn_all

    def _L3_gnn_setup():
        import jax, jax.numpy as jnp
        import numpy as np
        MUL0, MUL1 = (64, 32)
        INV_SQRT3 = 1.0 / np.sqrt(3.0)

        def _split(x):
            return (x[:, :MUL0], x[:, MUL0:].reshape(x.shape[0], MUL1, 3))

        def _merge(o0, o1):
            return jnp.concatenate([o0, o1.reshape(o1.shape[0], -1)], axis=-1)

        def _tp(x0, x1, y0, y1, w000, w011, w101, w110):
            fan0 = x0.shape[1] * y0.shape[1] + x1.shape[1] * y1.shape[1]
            fan1 = x0.shape[1] * y1.shape[1] + x1.shape[1] * y0.shape[1]
            out0 = (jnp.einsum('eu,ev,uvw->ew', x0, y0, w000) + INV_SQRT3 * jnp.einsum('euk,evk,uvw->ew', x1, y1, w110)) / np.sqrt(fan0)
            out1 = (jnp.einsum('eu,evk,uvw->ewk', x0, y1, w011) + jnp.einsum('euk,ev,uvw->ewk', x1, y0, w101)) / np.sqrt(fan1)
            return (out0, out1)

        def _lin(x0, x1, w0, w1):
            return (x0 @ w0 / np.sqrt(x0.shape[1]), jnp.einsum('euk,uv->evk', x1, w1) / np.sqrt(x1.shape[1]))
        key = jax.random.key(seed)
        ks = jax.random.split(key, 20)
        N, E = (50000, 15625)
        inp = {'node_features': jax.random.normal(ks[0], (N, MUL0 + 3 * MUL1), dtype=jnp.float32), 'edge_index': jax.random.randint(ks[1], (2, E), 0, N, dtype=jnp.int64), 'edge_attr_tensor': jax.random.normal(ks[2], (E, 4), dtype=jnp.float32), 'node_attr_scalar_raw': jax.random.normal(ks[3], (N, 1), dtype=jnp.float32), 'wm000': jax.random.normal(ks[4], (MUL0, 1, MUL0), dtype=jnp.float32), 'wm011': jax.random.normal(ks[5], (MUL0, 1, MUL1), dtype=jnp.float32), 'wm101': jax.random.normal(ks[6], (MUL1, 1, MUL1), dtype=jnp.float32), 'wm110': jax.random.normal(ks[7], (MUL1, 1, MUL0), dtype=jnp.float32), 'lm0': jax.random.normal(ks[8], (MUL0, MUL0), dtype=jnp.float32), 'lm1': jax.random.normal(ks[9], (MUL1, MUL1), dtype=jnp.float32), 'wu000': jax.random.normal(ks[10], (MUL0, MUL0, MUL0), dtype=jnp.float32), 'wu011': jax.random.normal(ks[11], (MUL0, MUL1, MUL1), dtype=jnp.float32), 'wu101': jax.random.normal(ks[12], (MUL1, MUL0, MUL1), dtype=jnp.float32), 'wu110': jax.random.normal(ks[13], (MUL1, MUL1, MUL0), dtype=jnp.float32), 'lu0': jax.random.normal(ks[14], (MUL0, MUL0), dtype=jnp.float32), 'lu1': jax.random.normal(ks[15], (MUL1, MUL1), dtype=jnp.float32)}
        return inp
    _L3_gnn_all = _L3_gnn_setup()
    _L3_gnn_in = {k: v for k, v in _L3_gnn_all.items() if k in ('wm000', 'wm011', 'wm101', 'wm110', 'lm0', 'lm1', 'wu000', 'wu011', 'wu101', 'wu110', 'lu0', 'lu1')}
    del _L3_gnn_all
    return {'x': x, 'src': src, 'dst': dst, 'edge_attr_16': edge_attr_16, 'edge_attr_4': edge_attr_4, 'edge_attr_8': edge_attr_8, 'node_vec1': node_vec1, 'L0_gnn_gamma_s': _L0_gnn_in['gamma_s'], 'L0_gnn_beta_s': _L0_gnn_in['beta_s'], 'L0_gnn_gamma_v': _L0_gnn_in['gamma_v'], 'L0_gnn_Ws_src': _L0_gnn_in['Ws_src'], 'L0_gnn_Wv_src': _L0_gnn_in['Wv_src'], 'L0_gnn_Ws_dst': _L0_gnn_in['Ws_dst'], 'L0_gnn_Wv_dst': _L0_gnn_in['Wv_dst'], 'L0_gnn_W_rbf': _L0_gnn_in['W_rbf'], 'L0_gnn_W_alpha': _L0_gnn_in['W_alpha'], 'L0_gnn_alpha_dot': _L0_gnn_in['alpha_dot'], 'L0_gnn_Ws_val': _L0_gnn_in['Ws_val'], 'L0_gnn_Wv_val': _L0_gnn_in['Wv_val'], 'L0_gnn_Wg': _L0_gnn_in['Wg'], 'L0_gnn_w2_ss': _L0_gnn_in['w2_ss'], 'L0_gnn_w2_sv': _L0_gnn_in['w2_sv'], 'L0_gnn_w2_vs': _L0_gnn_in['w2_vs'], 'L0_gnn_w2_vv0': _L0_gnn_in['w2_vv0'], 'L0_gnn_w2_vv1': _L0_gnn_in['w2_vv1'], 'L0_gnn_Ws_vlin': _L0_gnn_in['Ws_vlin'], 'L0_gnn_Wv_vlin': _L0_gnn_in['Wv_vlin'], 'L0_gnn_Wps': _L0_gnn_in['Wps'], 'L0_gnn_Wpv': _L0_gnn_in['Wpv'], 'L1_gnn_sc_w0': _L1_gnn_in['sc_w0'], 'L1_gnn_sc_w1': _L1_gnn_in['sc_w1'], 'L1_gnn_lin1_w0': _L1_gnn_in['lin1_w0'], 'L1_gnn_lin1_w1': _L1_gnn_in['lin1_w1'], 'L1_gnn_fc_w1': _L1_gnn_in['fc_w1'], 'L1_gnn_fc_w2': _L1_gnn_in['fc_w2'], 'L1_gnn_lin2_w0': _L1_gnn_in['lin2_w0'], 'L1_gnn_lin2_w1': _L1_gnn_in['lin2_w1'], 'L1_gnn_lin3_w': _L1_gnn_in['lin3_w'], 'L2_gnn_W_sc0': _L2_gnn_in['W_sc0'], 'L2_gnn_W_sc1': _L2_gnn_in['W_sc1'], 'L2_gnn_W_l1_0': _L2_gnn_in['W_l1_0'], 'L2_gnn_W_l1_1': _L2_gnn_in['W_l1_1'], 'L2_gnn_fc_W1': _L2_gnn_in['fc_W1'], 'L2_gnn_fc_W2': _L2_gnn_in['fc_W2'], 'L2_gnn_W_l2_0': _L2_gnn_in['W_l2_0'], 'L2_gnn_W_l2_1': _L2_gnn_in['W_l2_1'], 'L3_gnn_wm000': _L3_gnn_in['wm000'], 'L3_gnn_wm011': _L3_gnn_in['wm011'], 'L3_gnn_wm101': _L3_gnn_in['wm101'], 'L3_gnn_wm110': _L3_gnn_in['wm110'], 'L3_gnn_lm0': _L3_gnn_in['lm0'], 'L3_gnn_lm1': _L3_gnn_in['lm1'], 'L3_gnn_wu000': _L3_gnn_in['wu000'], 'L3_gnn_wu011': _L3_gnn_in['wu011'], 'L3_gnn_wu101': _L3_gnn_in['wu101'], 'L3_gnn_wu110': _L3_gnn_in['wu110'], 'L3_gnn_lu0': _L3_gnn_in['lu0'], 'L3_gnn_lu1': _L3_gnn_in['lu1']}

def reference(x, src, dst, edge_attr_16, edge_attr_4, edge_attr_8, node_vec1, L0_gnn_gamma_s, L0_gnn_beta_s, L0_gnn_gamma_v, L0_gnn_Ws_src, L0_gnn_Wv_src, L0_gnn_Ws_dst, L0_gnn_Wv_dst, L0_gnn_W_rbf, L0_gnn_W_alpha, L0_gnn_alpha_dot, L0_gnn_Ws_val, L0_gnn_Wv_val, L0_gnn_Wg, L0_gnn_w2_ss, L0_gnn_w2_sv, L0_gnn_w2_vs, L0_gnn_w2_vv0, L0_gnn_w2_vv1, L0_gnn_Ws_vlin, L0_gnn_Wv_vlin, L0_gnn_Wps, L0_gnn_Wpv, L1_gnn_sc_w0, L1_gnn_sc_w1, L1_gnn_lin1_w0, L1_gnn_lin1_w1, L1_gnn_fc_w1, L1_gnn_fc_w2, L1_gnn_lin2_w0, L1_gnn_lin2_w1, L1_gnn_lin3_w, L2_gnn_W_sc0, L2_gnn_W_sc1, L2_gnn_W_l1_0, L2_gnn_W_l1_1, L2_gnn_fc_W1, L2_gnn_fc_W2, L2_gnn_W_l2_0, L2_gnn_W_l2_1, L3_gnn_wm000, L3_gnn_wm011, L3_gnn_wm101, L3_gnn_wm110, L3_gnn_lm0, L3_gnn_lm1, L3_gnn_wu000, L3_gnn_wu011, L3_gnn_wu101, L3_gnn_wu110, L3_gnn_lu0, L3_gnn_lu1):
    import jax
    import jax.numpy as jnp

    def _L0_gnn_ref(node, rbf, rsh, gamma_s, beta_s, gamma_v, Ws_src, Wv_src, Ws_dst, Wv_dst, W_rbf, W_alpha, alpha_dot, Ws_val, Wv_val, Wg, w2_ss, w2_sv, w2_vs, w2_vv0, w2_vv1, Ws_vlin, Wv_vlin, Wps, Wpv, edge_index):
        import jax, jax.numpy as jnp
        import numpy as np
        N, E = (625, 10000)
        CS, CV = (64, 32)
        AS_, AV, H = (16, 8, 4)
        NB = 16
        SQRT3 = 1.7320508075688772
        SQRT2 = 1.4142135623730951
        EPS = 1e-05

        def _cg_tp(s, v, y0, y1, w_ss, w_sv, w_vs, w_vv0, w_vv1):
            out_s = jnp.concatenate([w_ss * s * y0[:, None], w_vv0 * (jnp.einsum('eci,ei->ec', v, y1) / SQRT3)], axis=-1)
            out_v = jnp.concatenate([(w_sv * s)[:, :, None] * y1[:, None, :], (w_vs * jnp.ones_like(v[..., 0]))[..., None] * v * y0[:, None, None], (w_vv1 * jnp.ones_like(v[..., 0]))[..., None] * (jnp.cross(v, y1[:, None, :]) / SQRT2)], axis=1)
            return (out_s, out_v)

        def _equiv_layernorm(s, v, gamma_s, beta_s, gamma_v):
            mu = jnp.mean(s, axis=-1, keepdims=True)
            var = jnp.var(s, axis=-1, keepdims=True)
            s_n = (s - mu) * jax.lax.rsqrt(var + EPS) * gamma_s + beta_s
            rms = jnp.sqrt(jnp.mean(jnp.sum(v * v, axis=-1), axis=-1, keepdims=True) + EPS)
            v_n = v / rms[..., None] * gamma_v[None, :, None]
            return (s_n, v_n)
        n = node.shape[0]
        e = rsh.shape[0]
        s = node[:, :CS]
        v = node[:, CS:].reshape(n, CV, 3)
        s_n, v_n = _equiv_layernorm(s, v, gamma_s, beta_s, gamma_v)
        src, dst = (edge_index[0], edge_index[1])
        msg_s = (s_n @ Ws_src)[src] + (s_n @ Ws_dst)[dst]
        msg_v = jnp.einsum('ncx,cd->ndx', v_n, Wv_src)[src] + jnp.einsum('ncx,cd->ndx', v_n, Wv_dst)[dst]
        y0, y1 = (rsh[:, 0], rsh[:, 1:4])
        w1 = rbf @ W_rbf
        m1_s, m1_v = _cg_tp(msg_s, msg_v, y0, y1, w1[:, :CS], w1[:, CS:2 * CS], w1[:, 2 * CS:2 * CS + CV], w1[:, 2 * CS + CV:2 * CS + 2 * CV], w1[:, 2 * CS + 2 * CV:])
        a = (m1_s @ W_alpha).reshape(e, H, AS_)
        a = jnp.where(a > 0, a, 0.2 * a)
        a = jnp.sum(a * alpha_dot, axis=-1, keepdims=True)
        amax = jax.ops.segment_max(a, dst, num_segments=n)
        amax = jnp.where(jnp.isfinite(amax), amax, 0.0)
        ex = jnp.exp(a - amax[dst])
        den = jax.ops.segment_sum(ex, dst, num_segments=n)
        alpha = ex / (den[dst] + 1e-16)
        val_s = m1_s @ Ws_val
        val_v = jnp.einsum('ecx,cd->edx', m1_v, Wv_val)
        val_v = val_v * jax.nn.sigmoid(val_s @ Wg)[..., None]
        val_s = jax.nn.sigmoid(val_s)
        m2_s, m2_v = _cg_tp(val_s, val_v, y0, y1, w2_ss, w2_sv, w2_vs, w2_vv0, w2_vv1)
        hs = (m2_s @ Ws_vlin).reshape(e, H, AS_)
        hv = jnp.einsum('ecx,cd->edx', m2_v, Wv_vlin).reshape(e, H, AV, 3)
        h = jnp.concatenate([hs, hv.reshape(e, H, AV * 3)], axis=-1)
        agg = jax.ops.segment_sum(alpha * h, dst, num_segments=n)
        agg_s = agg[:, :, :AS_].reshape(n, H * AS_)
        agg_v = agg[:, :, AS_:].reshape(n, H * AV, 3)
        out = node + jnp.concatenate([agg_s @ Wps, jnp.einsum('ncx,cd->ndx', agg_v, Wpv).reshape(n, CV * 3)], axis=-1)
        return out

    def _L1_gnn_ref(node_input, node_attr, edge_attr, edge_scalars, sc_w0, sc_w1, lin1_w0, lin1_w1, fc_w1, fc_w2, lin2_w0, lin2_w1, lin3_w, edge_src, edge_dst, num_neighbors):
        import jax, jax.numpy as jnp
        import numpy as np
        INV3 = 1.0 / np.sqrt(3.0)

        def _fctp(x_s, x_v, attr, w0, w1):
            s = x_s @ w0 * (1.0 / np.sqrt(x_s.shape[-1])) * attr
            v = jnp.einsum('nud,uw->nwd', x_v, w1) * (1.0 / np.sqrt(x_v.shape[-2])) * attr[..., None]
            return (s, v)
        N = node_input.shape[0]
        h = jax.nn.silu(edge_scalars @ fc_w1 * (1.0 / np.sqrt(8.0)))
        weight = h @ fc_w2 * (1.0 / np.sqrt(64.0))
        xs, xv = (node_input[:, :64], node_input[:, 64:].reshape(N, 32, 3))
        sc_s, sc_v = _fctp(xs, xv, node_attr, sc_w0, sc_w1)
        f_s, f_v = _fctp(xs, xv, node_attr, lin1_w0, lin1_w1)
        gs = f_s[edge_src]
        gv = f_v[edge_src]
        ys, yv = (edge_attr[:, :1], edge_attr[:, 1:])
        w1_, w2_ = (weight[:, :64], weight[:, 64:128])
        w3_, w4_ = (weight[:, 128:160], weight[:, 160:192])
        m0a = gs * ys * w1_
        m0b = jnp.sum(gv * yv[:, None, :], -1) * INV3 * w4_
        m1a = gs[..., None] * yv[:, None, :] * w2_[..., None]
        m1b = gv * ys[..., None] * w3_[..., None]
        E = m0a.shape[0]
        edge_feat = jnp.concatenate([m0a, m0b, m1a.reshape(E, 192), m1b.reshape(E, 96)], -1)
        mid = jax.ops.segment_sum(edge_feat, edge_dst, num_segments=N)
        mid = mid / np.sqrt(float(num_neighbors))
        mid_s, mid_v = (mid[:, :96], mid[:, 96:].reshape(N, 96, 3))
        c_s, c_v = _fctp(mid_s, mid_v, node_attr, lin2_w0, lin2_w1)
        conv = jnp.concatenate([c_s, c_v.reshape(N, -1)], -1)
        scfeat = jnp.concatenate([sc_s, sc_v.reshape(N, -1)], -1)
        angle = 0.1 * (mid_s @ lin3_w) * (1.0 / np.sqrt(96.0)) * node_attr
        return jnp.cos(angle) * scfeat + jnp.sin(angle) * conv

    def _L2_gnn_ref(node_input, node_attr, edge_src, edge_dst, edge_attr, edge_length_embedded, W_sc0, W_sc1, W_l1_0, W_l1_1, fc_W1, fc_W2, W_l2_0, W_l2_1):
        import jax, jax.numpy as jnp
        import numpy as np
        import math
        N = 50000
        E = 15625
        MUL0 = 64
        MUL1 = 32
        MID = MUL0 + MUL1
        FC_IN = 16
        FC_H = 64
        WEIGHT_NUMEL = 2 * MUL0 + 2 * MUL1
        NUM_NEIGH = 10.0
        C_S = math.sin(math.pi / 8.0)
        C_X = math.cos(math.pi / 8.0)
        n = node_input.shape[0]
        x0 = node_input[:, :MUL0]
        x1 = node_input[:, MUL0:].reshape(n, MUL1, 3)
        a = node_attr
        inv0 = 1.0 / math.sqrt(MUL0)
        inv1 = 1.0 / math.sqrt(MUL1)
        s0 = x0 @ W_sc0 * a * inv0
        s1 = jnp.einsum('nuc,uv->nvc', x1, W_sc1) * a[:, :, None] * inv1
        y0 = x0 @ W_l1_0 * a * inv0
        y1 = jnp.einsum('nuc,uv->nvc', x1, W_l1_1) * a[:, :, None] * inv1
        h = jax.nn.silu(edge_length_embedded @ fc_W1 * (1.0 / math.sqrt(FC_IN)))
        w = h @ fc_W2 * (1.0 / math.sqrt(FC_H))
        w_a = w[:, :MUL0]
        w_b = w[:, MUL0:2 * MUL0]
        w_c = w[:, 2 * MUL0:2 * MUL0 + MUL1]
        w_d = w[:, 2 * MUL0 + MUL1:]
        ys0 = y0[edge_src]
        ys1 = y1[edge_src]
        e0 = edge_attr[:, :1]
        e1 = edge_attr[:, 1:]
        mid_a = w_a * ys0 * e0
        mid_d = w_d * jnp.einsum('euc,ec->eu', ys1, e1) * (1.0 / math.sqrt(3.0))
        mid_b = (w_b * ys0)[:, :, None] * e1[:, None, :]
        mid_c = (w_c * e0)[:, :, None] * ys1
        mid0 = jnp.concatenate([mid_a, mid_d], axis=1)
        mid1 = jnp.concatenate([mid_b, mid_c], axis=1)
        inv_nb = 1.0 / math.sqrt(NUM_NEIGH)
        z0 = jnp.zeros((n, MID), mid0.dtype).at[edge_dst].add(mid0) * inv_nb
        z1 = jnp.zeros((n, MID, 3), mid1.dtype).at[edge_dst].add(mid1) * inv_nb
        inv_mid = 1.0 / math.sqrt(MID)
        o0 = z0 @ W_l2_0 * a * inv_mid
        o1 = jnp.einsum('nuc,uv->nvc', z1, W_l2_1) * a[:, :, None] * inv_mid
        out0 = C_S * s0 + C_X * o0
        out1 = C_S * s1 + C_X * o1
        return jnp.concatenate([out0, out1.reshape(n, MUL1 * 3)], axis=1)

    def _L3_gnn_ref(node_features, edge_index, edge_attr_tensor, node_attr_scalar_raw, wm000, wm011, wm101, wm110, lm0, lm1, wu000, wu011, wu101, wu110, lu0, lu1):
        import jax, jax.numpy as jnp
        import numpy as np
        MUL0, MUL1 = (64, 32)
        INV_SQRT3 = 1.0 / np.sqrt(3.0)

        def _split(x):
            return (x[:, :MUL0], x[:, MUL0:].reshape(x.shape[0], MUL1, 3))

        def _merge(o0, o1):
            return jnp.concatenate([o0, o1.reshape(o1.shape[0], -1)], axis=-1)

        def _tp(x0, x1, y0, y1, w000, w011, w101, w110):
            fan0 = x0.shape[1] * y0.shape[1] + x1.shape[1] * y1.shape[1]
            fan1 = x0.shape[1] * y1.shape[1] + x1.shape[1] * y0.shape[1]
            out0 = (jnp.einsum('eu,ev,uvw->ew', x0, y0, w000) + INV_SQRT3 * jnp.einsum('euk,evk,uvw->ew', x1, y1, w110)) / np.sqrt(fan0)
            out1 = (jnp.einsum('eu,evk,uvw->ewk', x0, y1, w011) + jnp.einsum('euk,ev,uvw->ewk', x1, y0, w101)) / np.sqrt(fan1)
            return (out0, out1)

        def _lin(x0, x1, w0, w1):
            return (x0 @ w0 / np.sqrt(x0.shape[1]), jnp.einsum('euk,uv->evk', x1, w1) / np.sqrt(x1.shape[1]))
        N = node_features.shape[0]
        row, col = (edge_index[0], edge_index[1])
        r_vec = edge_attr_tensor[:, :3]
        dist = edge_attr_tensor[:, 3:4]
        e0 = dist
        e1 = r_vec[:, None, :]
        xj0, xj1 = _split(node_features[col])
        m0, m1 = _tp(xj0, xj1, e0, e1, wm000, wm011, wm101, wm110)
        d0, d1 = _lin(xj0, xj1, lm0, lm1)
        msgs = _merge(m0 + d0, m1 + d1)
        agg = jax.ops.segment_sum(msgs, row, num_segments=N)
        a0, a1 = _split(agg)
        x0, x1 = _split(node_features)
        u0, u1 = _tp(x0, x1, a0, a1, wu000, wu011, wu101, wu110)
        ud0, ud1 = _lin(x0, x1, lu0, lu1)
        return node_features + _merge(u0 + ud0, u1 + ud1)
    edge_index = jnp.stack([src, dst])
    x = _layernorm(x + _L0_gnn_ref(x, edge_attr_16, edge_attr_4, L0_gnn_gamma_s, L0_gnn_beta_s, L0_gnn_gamma_v, L0_gnn_Ws_src, L0_gnn_Wv_src, L0_gnn_Ws_dst, L0_gnn_Wv_dst, L0_gnn_W_rbf, L0_gnn_W_alpha, L0_gnn_alpha_dot, L0_gnn_Ws_val, L0_gnn_Wv_val, L0_gnn_Wg, L0_gnn_w2_ss, L0_gnn_w2_sv, L0_gnn_w2_vs, L0_gnn_w2_vv0, L0_gnn_w2_vv1, L0_gnn_Ws_vlin, L0_gnn_Wv_vlin, L0_gnn_Wps, L0_gnn_Wpv, edge_index), axis=-1)
    x = _layernorm(x + _L1_gnn_ref(x, node_vec1, edge_attr_4, edge_attr_8, L1_gnn_sc_w0, L1_gnn_sc_w1, L1_gnn_lin1_w0, L1_gnn_lin1_w1, L1_gnn_fc_w1, L1_gnn_fc_w2, L1_gnn_lin2_w0, L1_gnn_lin2_w1, L1_gnn_lin3_w, src, dst, 16), axis=-1)
    x = _layernorm(x + _L2_gnn_ref(x, node_vec1, src, dst, edge_attr_4, edge_attr_16, L2_gnn_W_sc0, L2_gnn_W_sc1, L2_gnn_W_l1_0, L2_gnn_W_l1_1, L2_gnn_fc_W1, L2_gnn_fc_W2, L2_gnn_W_l2_0, L2_gnn_W_l2_1), axis=-1)
    x = _layernorm(x + _L3_gnn_ref(x, edge_index, edge_attr_4, node_vec1, L3_gnn_wm000, L3_gnn_wm011, L3_gnn_wm101, L3_gnn_wm110, L3_gnn_lm0, L3_gnn_lm1, L3_gnn_wu000, L3_gnn_wu011, L3_gnn_wu101, L3_gnn_wu110, L3_gnn_lu0, L3_gnn_lu1), axis=-1)
    return x

_drawn_inputs = setup_inputs


def setup_inputs(seed=0):
    import zlib

    import numpy as np

    out = dict(_drawn_inputs(seed))
    spreads = {'L0_gnn_gamma_s': (1.0, 0.2), 'L0_gnn_beta_s': (0.0, 0.319), 'L0_gnn_gamma_v': (1.0, 0.6)}
    factors = {'edge_attr_8': 4.32,
     'L0_gnn_w2_vv1': 3.09,
     'L1_gnn_lin1_w0': 4.559,
     'L1_gnn_lin1_w1': 5.607,
     'L1_gnn_fc_w1': 4.474,
     'L1_gnn_fc_w2': 4.287,
     'L1_gnn_lin2_w0': 5.185,
     'L1_gnn_lin2_w1': 7.136,
     'L1_gnn_lin3_w': 4.637,
     'L1_gnn_sc_w0': 3.958,
     'L1_gnn_sc_w1': 4.982}
    for name, (base, spread) in spreads.items():
        noise = np.random.default_rng([zlib.crc32(name.encode()), seed]).standard_normal(out[name].shape)
        drawn = base * np.exp(spread * noise) if base else spread * noise
        out[name] = jnp.asarray(drawn.astype(out[name].dtype))
    for name, factor in factors.items():
        out[name] = (out[name] * factor).astype(out[name].dtype)
    return out
```

```python
import math
from contextlib import ExitStack

import concourse.bass as bass
from concourse import mybir
from concourse.bass import IndirectOffsetOnAxis

F32 = mybir.dt.float32
I32 = mybir.dt.int32
ALU = mybir.AluOpType
ACT = mybir.ActivationFunctionType
AX = mybir.AxisListType
RMAX = bass.bass_isa.ReduceOp.max
ALL_ENGINES = [mybir.EngineType.Pool, mybir.EngineType.Activation, mybir.EngineType.PE,
               mybir.EngineType.DVE, mybir.EngineType.SP]

P = 128
NODES, EDGES = 3125, 100000
NT = -(-NODES // P)
NP = NT * P
TPC = 4
CH = -(-EDGES // (TPC * P))
W = 24
WS = 32
ROUNDS = -(-NODES // W)
S, V = 64, 32
D = S + 3 * V
NY = 5
EPS = 1e-5
PI = 3.1415925
NB = 4
ITERS = CH // NB
LAYERS = (0, 1, 2, 3)


def names(m, text, gpsimd_dmas=""):
    text, dmas = text.split(), gpsimd_dmas.split()
    assert len(text) <= len(m.sems) and len(dmas) <= len(m.dma_sems)
    return dict(list(zip(text, m.sems)) + list(zip(dmas, m.dma_sems)))


def linker(eng, sem):
    count = [0]

    def link(ins):
        count[0] += 1
        ins.then_inc(sem, 1)
        eng.wait_ge(sem, count[0])
    return link


def phase_end(nc, m):
    nc.gpsimd.dma_reset(m.dma_range)
    nc.all_engine_barrier(sems_to_clear=m.sem_range)


def setup_phase(nc, m, io):
    s = names(m, "loaded stored rounds_made ends_ready spans_ready linked")
    with nc.Block() as block:
        @block.sync
        def _(sp):
            loads = [(m.dst_i[:], io["dst"]), (m.y[:], io["y"]), (m.ident[:], io["ident"]), (m.iota[:], io["iota"]),
                     (m.rows[:], io["rows"]), (m.x[:], io["x"].rearrange("(p t) f -> p t f", t=NT)),
                     (m.attr[:], io["attr"]), (m.src[:], io["src"])]
            for to, what in loads:
                sp.dma_start(to, what).then_inc(s["loaded"], 16)
            sp.wait_ge(s["loaded"], 16 * len(loads))
            sp.wait_ge(s["rounds_made"], 1)
            sp.dma_start(m.rounds_dram, m.rounds_i[:]).then_inc(s["stored"], 16)
            sp.wait_ge(s["stored"], 16)

        @block.gpsimd
        def _(pool):
            pool.wait_ge(s["ends_ready"], 2)
            nc.gpsimd.partition_all_reduce(m.span[:], m.ends[:], P, RMAX).then_inc(s["spans_ready"], 1)

        @block.vector
        def _(dve):
            link = linker(dve, s["linked"])
            nc.vector.memset(m.zero[:], 0.0)
            nc.vector.memset(m.eps[:], EPS)
            nc.vector.memset(m.window_rows[:], 0)
            nc.vector.memset(m.rel[:], -1.0)
            dve.wait_ge(s["loaded"], 16 * 8)
            link(nc.vector.tensor_copy(m.dst_f[:], m.dst_i[:]))
            by_chunk = m.dst_f[:].rearrange("p (c t) -> p c t", t=TPC)
            nc.vector.tensor_reduce(m.ends[:, 0:CH], by_chunk, AX.X, ALU.min, negate=True).then_inc(s["ends_ready"], 1)
            nc.vector.tensor_reduce(m.ends[:, CH:2 * CH], by_chunk, AX.X, ALU.max).then_inc(s["ends_ready"], 1)
            dve.wait_ge(s["ends_ready"], 2)
            nc.vector.scalar_tensor_tensor(
                m.dst_f[:].unsqueeze(2), m.y[:, 0:CH * TPC * NY].rearrange("p (n k) -> p n k", k=NY)[:, :, NY - 1:NY],
                1e4, m.dst_f[:].unsqueeze(2), ALU.mult, ALU.add).then_inc(s["ends_ready"], 1)
            dve.wait_ge(s["ends_ready"], 3)
            nc.vector.tensor_scalar(m.dst_f[:], m.dst_f[:], -1e4, None, ALU.add)
            dve.wait_ge(s["spans_ready"], 1)
            link(nc.vector.tensor_tensor(m.ends[:, 0:CH], m.span[:, 0:CH], m.span[:, CH:2 * CH], ALU.add))
            link(nc.vector.tensor_reduce(m.fits[:], m.ends[:, 0:CH], AX.X, ALU.max))
            link(nc.vector.tensor_scalar(m.fits[:], m.fits[:], float(W - 1), None, ALU.is_le))
            nc.vector.tensor_scalar(m.base0[:], m.span[:, 0:CH], m.fits[:, 0:1], -1.0, ALU.mult, ALU.mult)
            nc.vector.tensor_scalar(m.rounds_i[:], m.fits[0:1, :], float(1 - ROUNDS), float(ROUNDS),
                                    ALU.mult, ALU.add).then_inc(s["rounds_made"], 1)
    phase_end(nc, m)


def window_phase(nc, m):
    s = names(m, "used")
    with nc.Block() as block:
        @block.vector
        def _(dve):
            rel = m.rel[:, 0:CH * TPC].rearrange("p (c t) -> p c t", t=TPC)
            dst = m.dst_f[:].rearrange("p (c t) -> p c t", t=TPC)
            nc.vector.tensor_tensor(rel, dst, m.base[:].unsqueeze(2).to_broadcast([P, CH, TPC]),
                                    ALU.subtract).then_inc(s["used"], 1)
            for j in range(2):
                nc.vector.tensor_scalar(m.window_rows[:, j, 0:CH], m.base[:], m.rows[:, j:j + 1], None,
                                        ALU.add).then_inc(s["used"], 1)
            dve.wait_ge(s["used"], 3)
            nc.vector.tensor_scalar(m.base[:], m.base[:], float(W), None, ALU.add)
    phase_end(nc, m)


def clear_phase(nc, m, rows):
    s = names(m, "cleared")
    with nc.Block() as block:
        @block.sync
        def _(sp):
            for k in range(rows):
                sp.dma_start(m.sums[k * NP:(k + 1) * NP, :].rearrange("(p t) f -> p (t f)", t=NT),
                             m.zero[:]).then_inc(s["cleared"], 16)
            sp.wait_ge(s["cleared"], 16 * rows)

        @block.vector
        def _(dve):
            nc.vector.tensor_copy(m.base[:], m.base0[:])
    phase_end(nc, m)


def edge_phase(nc, m, table, fc=None):
    NK, WN = (4, WS) if fc else (NY, W)
    KW = NK * WN
    WIDE = 2 * D if fc else D
    which = 0 if fc else 1
    s = names(m, "cols_ready landed turns summed acc_free partial_ready "
                 "onehot_ready weighted_ready scal0 scal1 scal2 scal3 hidden_psum hidden_ready weights_psum "
                 "messages_ready weights_free", "g0 g1 g2 g3 s0 s1 s2 s3")
    gathered, scattered = [s["g0"], s["g1"], s["g2"], s["g3"]], [s["s0"], s["s1"], s["s2"], s["s3"]]
    scal_loaded = [s["scal0"], s["scal1"], s["scal2"], s["scal3"]]
    with ExitStack() as ctx:
        sb = lambda name, shape, dt=F32, n=NB: [ctx.enter_context(nc.sbuf_tensor(m.tag + f"e_{name}{b}", shape, dt))
                                                for b in range(n)]
        ps = lambda name, shape, n: [ctx.enter_context(nc.psum_tensor(m.tag + f"e_{name}{b}", shape, F32)) for b in range(n)]
        src_cols = sb("src_cols", [P, TPC], I32)
        sum_rows = sb("sum_rows", [P, 1], I32)
        xj = sb("xj", [P, TPC, D])
        onehot = sb("onehot", [P, TPC, WN])
        weighted = sb("weighted", [P, TPC, NK, WN])
        partial = sb("partial", [P, D])
        acc = ps("acc", [P, 512], 2)
        if fc:
            scal_dram, K, w1, w2 = fc
            scal = sb("scal", [K, TPC * P])
            hidden = sb("hidden", [S, TPC * P], n=2)
            message = sb("message", [P, TPC, 2, D], n=2)
            hid_ps = ps("hid", [S, TPC * P], 2)
            wgt_ps = ps("wgt", [P, TPC, 256], 2)
        with nc.Block() as block:
            if fc:
                @block.sync
                def _(sp):
                    def load(c, b):
                        sp.dma_start(scal[b][:], scal_dram[:, bass.ds(c * TPC * P, TPC * P)]).then_inc(scal_loaded[b], 16)

                    for b in range(NB):
                        load(b, b)
                    with sp.Fori(0, ITERS) as i:
                        for b in range(NB):
                            sp.wait_ge(s["hidden_psum"], i * NB + b + 1)
                            load((i + 1) * NB + b, b)
                    for b in range(NB):
                        sp.wait_ge(scal_loaded[b], (ITERS + 1) * 16)

            @block.scalar
            def _(act):
                def columns(c, b):
                    nc.scalar.copy(src_cols[b][:], m.src[:, bass.ds(c * TPC, TPC)]).then_inc(s["cols_ready"], 1)

                def hide(c, b):
                    act.wait_ge(s["hidden_psum"], c + 1)
                    act.wait_ge(s["weights_psum"], c + 1)
                    nc.scalar.activation(hidden[b % 2][:], hid_ps[b % 2][:], ACT.Silu,
                                         scale=K ** -0.5).then_inc(s["hidden_ready"], 1)

                act.sem_inc(s["acc_free"], 2)
                for b in range(NB):
                    columns(b, b)
                if fc:
                    hide(0, 0)
                with act.Fori(0, ITERS) as i:
                    for b in range(NB):
                        c = i * NB + b
                        if fc:
                            hide(c + 1, b + 1)
                        act.wait_ge(s["summed"], c + 1 + NB)
                        act.wait_ge(s["landed"], c + 1)
                        nc.scalar.copy(sum_rows[b][:], m.window_rows[:, which, bass.ds(c, 1)]).then_inc(s["partial_ready"], 1)
                        if fc:
                            nc.scalar.copy(partial[b][0:96, :], acc[b % 2][0:96, D:2 * D]).then_inc(s["partial_ready"], 1)
                            nc.scalar.copy(partial[b][96:P, :], acc[b % 2][96:P, 0:D]).then_inc(s["partial_ready"], 1)
                        else:
                            nc.scalar.copy(partial[b][0:KW, :], acc[b % 2][0:KW, 0:D]).then_inc(s["partial_ready"], 2)
                        act.wait_ge(s["partial_ready"], (c + 1) * 3)
                        act.sem_inc(s["acc_free"], 1)
                        act.wait_ge(gathered[b], (i + 1) * 16 * TPC)
                        columns(c + NB, b)

            @block.gpsimd
            def _(pool):
                def gather(c, b):
                    pool.wait_ge(s["cols_ready"], c + 1)
                    pool.wait_ge(s["summed"], c + 1)
                    pool.sem_inc(s["turns"], 1)
                    for t in range(TPC):
                        nc.gpsimd.indirect_dma_start(
                            out=xj[b][:, t, :], out_offset=None, in_=table,
                            in_offset=IndirectOffsetOnAxis(ap=src_cols[b][:, t:t + 1], axis=0),
                        ).then_inc(gathered[b], 16)

                def scatter(c, b):
                    pool.wait_ge(s["partial_ready"], (c + 1) * 3)
                    pool.sem_inc(s["turns"], 1)
                    nc.gpsimd.indirect_dma_start(
                        out=m.sums, out_offset=IndirectOffsetOnAxis(ap=sum_rows[b][0:KW, :], axis=0),
                        in_=partial[b][0:KW, :], in_offset=None, compute_op=ALU.add,
                    ).then_inc(scattered[b], 16)

                def landed(i, b):
                    pool.wait_ge(scattered[b], (i + 1) * 16)
                    pool.sem_inc(s["landed"], 1)

                pool.sem_inc(s["landed"], NB)
                for b in range(NB):
                    gather(b, b)
                with pool.Fori(0, ITERS - 1) as i:
                    for b in range(NB):
                        scatter(i * NB + b, b)
                        gather((i + 1) * NB + b, b)
                        landed(i, b)
                for b in range(NB):
                    scatter((ITERS - 1) * NB + b, b)
                    landed(ITERS - 1, b)

            @block.vector
            def _(dve):
                if fc:
                    dve.sem_inc(s["weights_free"], 2)
                with dve.Fori(0, ITERS) as i:
                    for b in range(NB):
                        c = i * NB + b
                        dve.wait_ge(s["summed"], c + 1)
                        nc.vector.tensor_tensor(
                            onehot[b][:], m.iota[:, 0:WN].unsqueeze(1).to_broadcast([P, TPC, WN]),
                            m.rel[:, bass.ds(c * TPC, TPC)].unsqueeze(2).to_broadcast([P, TPC, WN]),
                            ALU.is_equal).then_inc(s["onehot_ready"], 1)
                        dve.wait_ge(s["onehot_ready"], c + 1)
                        y = m.y[:, bass.ds(c * TPC * NY, TPC * NY)].rearrange("p (t k) -> p t k", k=NY)[:, :, 0:NK]
                        nc.vector.tensor_tensor(
                            weighted[b][:], onehot[b][:].unsqueeze(2).to_broadcast([P, TPC, NK, WN]),
                            y.unsqueeze(3).to_broadcast([P, TPC, NK, WN]), ALU.mult).then_inc(s["weighted_ready"], 1)
                        if fc:
                            g, w, z = xj[b], wgt_ps[b % 2], message[b % 2]
                            dve.wait_ge(gathered[b], (i + 1) * 16 * TPC)
                            dve.wait_ge(s["weights_psum"], c + 1 + 2)
                            dve.wait_ge(s["summed"], c + 1 + NB - 2)
                            nc.vector.tensor_tensor(
                                z[:, :, :, 0:S], g[:, :, 0:S].unsqueeze(2).to_broadcast([P, TPC, 2, S]),
                                w[:, :, 0:2 * S].rearrange("p t (w c) -> p t w c", w=2), ALU.mult,
                            ).then_inc(s["messages_ready"], 1)
                            for j in range(2):
                                ins = nc.vector.tensor_tensor(
                                    z[:, :, j, S:D].rearrange("p t (d c) -> p t d c", d=3),
                                    g[:, :, S:D].rearrange("p t (d c) -> p t d c", d=3),
                                    w[:, :, 2 * S + V * j:2 * S + V * j + V].unsqueeze(2).to_broadcast([P, TPC, 3, V]),
                                    ALU.mult)
                                ins.then_inc(s["messages_ready"], 1)
                            dve.wait_ge(s["messages_ready"], (c + 1) * 3)
                            dve.sem_inc(s["weights_free"], 1)

            @block.tensor
            def _(pe):
                def hide(c, i, b):
                    pe.wait_ge(scal_loaded[b], (i + 1) * 16)
                    nc.tensor.matmul(hid_ps[b % 2][:], w1, scal[b][:], start=True, stop=True).then_inc(s["hidden_psum"], 1)

                def weights(c, b):
                    pe.wait_ge(s["hidden_ready"], c + 1)
                    pe.wait_ge(s["weights_free"], c + 1)
                    for t in range(TPC):
                        mm = nc.tensor.matmul(wgt_ps[b % 2][:, t, 0:192], hidden[b % 2][:, t * P:(t + 1) * P], w2,
                                              start=True, stop=True)
                    mm.then_inc(s["weights_psum"], 1)

                pe.sem_inc(s["summed"], NB)
                if fc:
                    pe.sem_inc(s["weights_psum"], 2)
                    hide(0, 0, 0)
                    hide(1, 0, 1)
                    weights(0, 0)
                with pe.Fori(0, ITERS) as i:
                    for b in range(NB):
                        c = i * NB + b
                        if fc:
                            ib, bb = (i, b + 2) if b + 2 < NB else (i + 1, b + 2 - NB)
                            hide(c + 2, ib, bb)
                            weights(c + 1, (b + 1) % NB)
                            pe.wait_ge(s["messages_ready"], (c + 1) * 3)
                        else:
                            pe.wait_ge(gathered[b], (i + 1) * 16 * TPC)
                        pe.wait_ge(s["weighted_ready"], c + 1)
                        pe.wait_ge(s["acc_free"], c + 1)
                        for t in range(TPC):
                            moving = message[b % 2][:, t, :, :].rearrange("p w c -> p (w c)") if fc else xj[b][:, t, :]
                            mm = nc.tensor.matmul(acc[b % 2][0:KW, 0:WIDE],
                                                  weighted[b][:, t, :, :].rearrange("p k n -> p (k n)"),
                                                  moving, start=(t == 0), stop=(t == TPC - 1))
                        mm.then_inc(s["summed"], 1)
    phase_end(nc, m)


def conv_weights_phase(nc, m, w, sc_scale, mid_scale, angle_scale):
    s = names(m, "zeroed loaded scaled")
    with nc.Block() as block:
        @block.vector
        def _(dve):
            nc.vector.memset(m.lin_a[:], 0.0).then_inc(s["zeroed"], 1)
            nc.vector.memset(m.lin_b[:], 0.0).then_inc(s["zeroed"], 1)

        @block.sync
        def _(sp):
            sp.wait_ge(s["zeroed"], 2)
            loads = [(m.fc1[0:w.K, :], w.fc1), (m.fc2[:], w.fc2), (m.out_s[:, 0:S], w.out_s), (m.out_v[:], w.out_v)]
            if w.angle is not None:
                loads.append((m.out_s[:, S:S + 1], w.angle))
            for j, (ws, wv) in enumerate([(w.sc_s, w.sc_v), (w.lin_s, w.lin_v)]):
                loads += [(m.lin_a[0:S, j * D:j * D + S], ws),
                          (m.lin_a[S:S + V, j * D + S:j * D + S + V], wv),
                          (m.lin_a[S + V:P, j * D + S + V:j * D + P], wv),
                          (m.lin_b[:, j * D + P:(j + 1) * D], wv)]
            for to, what in loads:
                sp.dma_start(to, what).then_inc(s["loaded"], 16)
            m.n_loads = len(loads)

        @block.scalar
        def _(act):
            act.wait_ge(s["loaded"], 16 * m.n_loads)
            for j, c in enumerate([sc_scale, 1.0]):
                nc.scalar.mul(m.lin_a[0:S, j * D:(j + 1) * D], m.lin_a[0:S, j * D:(j + 1) * D], c * S ** -0.5)
                nc.scalar.mul(m.lin_a[S:P, j * D:(j + 1) * D], m.lin_a[S:P, j * D:(j + 1) * D], c * V ** -0.5)
                nc.scalar.mul(m.lin_b[:, j * D:(j + 1) * D], m.lin_b[:, j * D:(j + 1) * D], c * V ** -0.5)
            nc.scalar.mul(m.fc2[:], m.fc2[:], S ** -0.5)
            n = 1
            scales = [mid_scale] + ([angle_scale] if w.angle is not None else [])
            for (a, b), c in zip([(0, S), (S, S + 1)], scales):
                nc.scalar.mul(m.out_s[0:S, a:b], m.out_s[0:S, a:b], c)
                nc.scalar.mul(m.out_s[S:96, a:b], m.out_s[S:96, a:b], c * 3 ** -0.5)
            nc.scalar.mul(m.out_v[:], m.out_v[:], mid_scale)
    phase_end(nc, m)


def node_linear_phase(nc, m, source, attr, own_table=None):
    s = names(m, "x_copied turned turned_copied mapped done stored")
    with ExitStack() as ctx:
        x1 = ctx.enter_context(nc.sbuf_tensor(m.tag + "nl_x", [P, D], F32))
        xT = ctx.enter_context(nc.sbuf_tensor(m.tag + "nl_xT", [P, 2 * P], F32))
        f = ctx.enter_context(nc.sbuf_tensor(m.tag + "nl_f", [P, NT, D], F32))
        pT = ctx.enter_context(nc.psum_tensor(m.tag + "nl_pT", [P, 512], F32))
        po = ctx.enter_context(nc.psum_tensor(m.tag + "nl_po", [P, 512], F32))
        with nc.Block() as block:
            @block.scalar
            def _(act):
                with act.Fori(0, NT) as t:
                    act.wait_ge(s["turned"], 2 * t + 2)
                    nc.scalar.copy(x1[:], source[:, bass.ds(t, 1), :].rearrange("p o f -> p (o f)")).then_inc(s["x_copied"], 1)
                    act.wait_ge(s["turned"], 2 * t + 4)
                    act.wait_ge(s["mapped"], t + 1)
                    nc.scalar.copy(xT[:, 0:P], pT[:, 0:P]).then_inc(s["turned_copied"], 1)
                    nc.scalar.copy(xT[0:V, P:2 * P], pT[0:V, P:2 * P]).then_inc(s["turned_copied"], 1)

            @block.tensor
            def _(pe):
                pe.sem_inc(s["turned"], 2)
                pe.sem_inc(s["mapped"], 1)
                with pe.Fori(0, NT) as t:
                    pe.wait_ge(s["x_copied"], t + 1)
                    nc.tensor.transpose(pT[:, 0:P], x1[:, 0:P], m.ident[:]).then_inc(s["turned"], 1)
                    nc.tensor.transpose(pT[0:V, P:2 * P], x1[:, P:D], m.ident[:]).then_inc(s["turned"], 1)
                    pe.wait_ge(s["turned_copied"], 2 * t + 2)
                    pe.wait_ge(s["done"], 2 * t + 2)
                    nc.tensor.matmul(po[:, 0:2 * D], xT[:, 0:P], m.lin_a[:], start=True, stop=False)
                    nc.tensor.matmul(po[:, 0:2 * D], xT[0:V, P:2 * P], m.lin_b[:], start=False,
                                     stop=True).then_inc(s["mapped"], 1)

            @block.vector
            def _(dve):
                dve.sem_inc(s["done"], 2)
                with dve.Fori(0, NT) as t:
                    dve.wait_ge(s["mapped"], t + 2)
                    a = attr[:, bass.ds(t, 1)]
                    for j, to in enumerate([m.own, f]):
                        nc.vector.tensor_scalar(to[:, bass.ds(t, 1), :].rearrange("p o f -> p (o f)"),
                                                po[:, j * D:(j + 1) * D], a, None, ALU.mult).then_inc(s["done"], 1)

            @block.sync
            def _(sp):
                sp.wait_ge(s["done"], 2 * NT + 2)
                sp.dma_start(m.table.rearrange("(p t) f -> p t f", t=NT), f[:]).then_inc(s["stored"], 16)
                if own_table is not None:
                    sp.dma_start(own_table.rearrange("(p t) f -> p t f", t=NT), m.own[:]).then_inc(s["stored"], 16)
                sp.wait_ge(s["stored"], 32 if own_table is not None else 16)
    phase_end(nc, m)


def conv_node_phase(nc, m, with_angle):
    s = names(m, "loaded gathered_mid turned turned_copied mapped done linked waved linked2")
    with ExitStack() as ctx:
        sb = lambda name, shape: ctx.enter_context(nc.sbuf_tensor(m.tag + "cn_" + name, shape, F32))
        ps = lambda name, shape: ctx.enter_context(nc.psum_tensor(m.tag + "cn_" + name, shape, F32))
        sums = sb("sums", [P, 4, NT, D])
        mid = sb("mid", [P, 4, 96])
        midT = sb("midT", [96, 4 * P])
        pT = ps("pT", [96, 4 * P])
        po = ps("po", [P, 512])
        angle = sb("angle", [P, NT, 1])
        turn = sb("turn", [P, NT, 1])
        wave = [sb("sin", [P, NT, 1]), sb("cos", [P, NT, 1])]
        with nc.Block() as block:
            @block.sync
            def _(sp):
                for k in range(4):
                    sp.dma_start(sums[:, k, :, :], m.sums[k * NP:(k + 1) * NP, :].rearrange("(p t) f -> p t f", t=NT)
                                 ).then_inc(s["loaded"], 16)

            @block.vector
            def _(dve):
                dve.wait_ge(s["loaded"], 64)
                dve.sem_inc(s["done"], 2)
                with dve.Fori(0, NT) as t:
                    one = lambda k, a, b: sums[:, k, bass.ds(t, 1), a:b]
                    dve.wait_ge(s["turned"], t + 1)
                    dot = mid[:, 3, S:96].unsqueeze(1)
                    nc.vector.tensor_tensor(dot, one(0, S, S + V), one(1, S + V, S + 2 * V), ALU.add).then_inc(s["linked"], 1)
                    dve.wait_ge(s["linked"], 2 * t + 1)
                    nc.vector.tensor_tensor(dot, dot, one(2, S + 2 * V, D), ALU.add).then_inc(s["linked"], 1)
                    nc.vector.tensor_copy(mid[:, 3, 0:S].unsqueeze(1), one(3, 0, S)).then_inc(s["gathered_mid"], 1)
                    nc.vector.tensor_copy(mid[:, 0:3, S:96], one(3, S, D).rearrange("p o (d c) -> p (o d) c", d=3)
                                          ).then_inc(s["gathered_mid"], 1)
                    nc.vector.tensor_copy(mid[:, 0:3, 0:S].unsqueeze(2), sums[:, 0:3, bass.ds(t, 1), 0:S]
                                          ).then_inc(s["gathered_mid"], 1)
                    dve.wait_ge(s["mapped"], t + 2)
                    a = m.attr[:, bass.ds(t, 1)]
                    nc.vector.tensor_scalar(m.h[:, bass.ds(t, 1), :].rearrange("p o f -> p (o f)"), po[:, 0:D], a, None,
                                            ALU.mult).then_inc(s["done"], 1)
                    if with_angle:
                        nc.vector.tensor_scalar(angle[:, bass.ds(t, 1), :].rearrange("p o f -> p (o f)"), po[:, D:D + 1],
                                                a, None, ALU.mult).then_inc(s["done"], 1)
                    else:
                        dve.sem_inc(s["done"], 1)
                dve.wait_ge(s["done"], 2 * NT + 2)
                link = linker(dve, s["linked2"])
                tt = nc.vector.tensor_tensor
                if with_angle:
                    big, two_pi = 1.5 * 2 ** 23, 2 * math.pi
                    hi = math.floor(two_pi * 2 ** 9) / 2 ** 9
                    for j in range(2):
                        a = wave[j]
                        link(nc.vector.tensor_scalar(a[:], angle[:], 0.5 * math.pi * j, None, ALU.add))
                        link(nc.vector.tensor_scalar(turn[:], a[:], 1 / two_pi, big, ALU.mult, ALU.add))
                        link(nc.vector.tensor_scalar(turn[:], turn[:], big, None, ALU.subtract))
                        link(nc.vector.scalar_tensor_tensor(a[:], turn[:], -hi, a[:], ALU.mult, ALU.add))
                        link(nc.vector.scalar_tensor_tensor(a[:], turn[:], hi - two_pi, a[:], ALU.mult, ALU.add))
                        link(nc.vector.tensor_scalar(a[:], a[:], PI, -PI, ALU.min, ALU.max))
                    dve.wait_ge(s["waved"], 2)
                    link(tt(m.h[:], m.h[:], wave[0][:].to_broadcast([P, NT, D]), ALU.mult))
                    link(tt(m.own[:], m.own[:], wave[1][:].to_broadcast([P, NT, D]), ALU.mult))
                link(tt(m.h[:], m.h[:], m.own[:], ALU.add))
                link(tt(m.h[:], m.h[:], m.x[:], ALU.add))

            @block.scalar
            def _(act):
                with act.Fori(0, NT) as t:
                    act.wait_ge(s["turned"], t + 2)
                    act.wait_ge(s["mapped"], t + 1)
                    nc.scalar.copy(midT[:], pT[:]).then_inc(s["turned_copied"], 1)
                if with_angle:
                    act.wait_ge(s["linked2"], 12)
                    for j in range(2):
                        nc.scalar.activation(wave[j][:], wave[j][:], ACT.Sin).then_inc(s["waved"], 1)

            @block.tensor
            def _(pe):
                pe.sem_inc(s["turned"], 1)
                pe.sem_inc(s["mapped"], 1)
                with pe.Fori(0, NT) as t:
                    pe.wait_ge(s["gathered_mid"], 3 * t + 3)
                    pe.wait_ge(s["linked"], 2 * t + 2)
                    for k in range(4):
                        mm = nc.tensor.transpose(pT[:, k * P:(k + 1) * P], mid[:, k, :], m.ident[:])
                    mm.then_inc(s["turned"], 1)
                    pe.wait_ge(s["turned_copied"], t + 1)
                    pe.wait_ge(s["done"], 2 * t + 2)
                    at = lambda k: midT[:, k * P:(k + 1) * P]
                    nc.tensor.matmul(po[:, 0:S], at(3), m.out_s[:, 0:S], start=True, stop=True)
                    if with_angle:
                        nc.tensor.matmul(po[:, D:D + 1], at(3), m.out_s[:, S:S + 1], start=True, stop=True)
                    for k in range(3):
                        mm = nc.tensor.matmul(po[:, S + k * V:S + (k + 1) * V], at(k), m.out_v[:], start=True, stop=True)
                    mm.then_inc(s["mapped"], 1)
    phase_end(nc, m)


def layernorm_phase(nc, m):
    s = names(m, "linked squared rooted")
    with ExitStack() as ctx:
        sb = lambda name, shape: ctx.enter_context(nc.sbuf_tensor(m.tag + "ln_" + name, shape, F32))
        mean, var = sb("mean", [P, NT]), sb("var", [P, NT])
        square = sb("square", [P, NT, D])
        wide = lambda a: a[:].unsqueeze(2).to_broadcast([P, NT, D])
        with nc.Block() as block:
            @block.vector
            def _(dve):
                link = linker(dve, s["linked"])
                link(nc.vector.tensor_reduce(mean[:], m.h[:], AX.X, ALU.add))
                link(nc.vector.tensor_scalar(mean[:], mean[:], 1.0 / D, None, ALU.mult))
                link(nc.vector.tensor_tensor(m.h[:], m.h[:], wide(mean), ALU.subtract))
                dve.wait_ge(s["squared"], 1)
                link(nc.vector.tensor_reduce(var[:], square[:], AX.X, ALU.add))
                dve.wait_ge(s["rooted"], 1)
                link(nc.vector.reciprocal(var[:], var[:]))
                nc.vector.tensor_tensor(m.x[:], m.h[:], wide(var), ALU.mult)

            @block.scalar
            def _(act):
                act.wait_ge(s["linked"], 3)
                nc.scalar.activation(square[:], m.h[:], ACT.Square).then_inc(s["squared"], 1)
                act.wait_ge(s["linked"], 4)
                nc.scalar.activation(var[:], var[:], ACT.Sqrt, bias=m.eps[:, 0:1], scale=1.0 / D).then_inc(s["rooted"], 1)
    phase_end(nc, m)


def conv_layer(nc, m, io, w, scal, sc_scale, mid_scale, angle_scale, rounds):
    with ExitStack() as ctx:
        sb = lambda name, shape: ctx.enter_context(nc.sbuf_tensor(m.tag + "cl_" + name, shape, F32))
        m.lin_a, m.lin_b = sb("lin_a", [P, 2 * D]), sb("lin_b", [V, 2 * D])
        m.fc1, m.fc2 = sb("fc1", [16, S]), sb("fc2", [S, 192])
        m.out_s, m.out_v = sb("out_s", [96, S + 1]), sb("out_v", [96, V])
        m.own = sb("own", [P, NT, D])
        conv_weights_phase(nc, m, w, sc_scale, mid_scale, angle_scale)
        node_linear_phase(nc, m, m.x, m.attr)
        clear_phase(nc, m, 4)
        with nc.Fori(0, rounds):
            window_phase(nc, m)
            edge_phase(nc, m, m.table, (scal, w.K, m.fc1[0:w.K, :], m.fc2[:]))
        m.h = sb("h", [P, NT, D])
        conv_node_phase(nc, m, w.angle is not None)
        layernorm_phase(nc, m)


class Memory:
    pass


KX, KDIST, KONE = (3, 0, 1), 2, 4


def update_weights_phase(nc, m, io):
    s = names(m, "loaded", "g0")
    c_msg, c_u0, c_u1 = (S + V) ** -0.5, (S * S + V * V) ** -0.5, (2 * S * V) ** -0.5
    parts = [(m.ms[:, 0:S], io["L3_gnn_lm0"], S ** -0.5), (m.ms[:, S:2 * S], io["L3_gnn_wm000"], c_msg),
             (m.ms[:, 2 * S:], io["L3_gnn_wm011"], c_msg),
             (m.mv[:, 0:V], io["L3_gnn_lm1"], V ** -0.5), (m.mv[:, V:2 * V], io["L3_gnn_wm101"], c_msg),
             (m.mv[:, 2 * V:], io["L3_gnn_wm110"], c_msg * 3 ** -0.5),
             (m.u000[:], io["L3_gnn_wu000"], c_u0), (m.u110[:], io["L3_gnn_wu110"], c_u0 * 3 ** -0.5),
             (m.u011[:], io["L3_gnn_wu011"], c_u1), (m.u101[:], io["L3_gnn_wu101"], c_u1),
             (m.lu0[:], io["L3_gnn_lu0"], S ** -0.5), (m.lu1[:], io["L3_gnn_lu1"], V ** -0.5)]
    with nc.Block() as block:
        @block.gpsimd
        def _(pool):
            pool.dma_start(m.lower[:], io["lower"]).then_inc(s["g0"], 16)
            pool.wait_ge(s["g0"], 16)

        @block.sync
        def _(sp):
            for to, what, _ in parts:
                sp.dma_start(to, what).then_inc(s["loaded"], 16)

        @block.scalar
        def _(act):
            act.wait_ge(s["loaded"], 16 * len(parts))
            for to, _, c in parts:
                nc.scalar.mul(to, to, c)
    phase_end(nc, m)


def update_tables_phase(nc, m):
    s = names(m, "zeroed x_copied turned turned_copied mapped kept stored")
    with ExitStack() as ctx:
        sb = lambda name, shape: ctx.enter_context(nc.sbuf_tensor(m.tag + "ut_" + name, shape, F32))
        ps = lambda name: ctx.enter_context(nc.psum_tensor(m.tag + "ut_" + name, [P, 512], F32))
        tables, x1, xT = sb("tables", [P, NY, NT, D]), sb("x", [P, D]), sb("xT", [S, 4 * P])
        pT, p_s, p_v = ps("pT"), ps("s"), ps("v")
        with nc.Block() as block:
            @block.gpsimd
            def _(pool):
                nc.gpsimd.memset(tables[:], 0.0).then_inc(s["zeroed"], 1)

            @block.scalar
            def _(act):
                with act.Fori(0, NT) as t:
                    act.wait_ge(s["turned"], 2 * t + 2)
                    nc.scalar.copy(x1[:].unsqueeze(1), m.x[:, bass.ds(t, 1), :]).then_inc(s["x_copied"], 1)
                    act.wait_ge(s["turned"], 2 * t + 4)
                    act.wait_ge(s["mapped"], t + 1)
                    nc.scalar.copy(xT[:, 0:P], pT[0:S, 0:P]).then_inc(s["turned_copied"], 1)
                    nc.scalar.copy(xT[0:V, P:4 * P], pT[0:V, P:4 * P]).then_inc(s["turned_copied"], 1)

            @block.tensor
            def _(pe):
                pe.sem_inc(s["turned"], 2)
                pe.sem_inc(s["mapped"], 1)
                with pe.Fori(0, NT) as t:
                    pe.wait_ge(s["x_copied"], t + 1)
                    pe.sem_inc(s["turned"], 1)
                    nc.tensor.transpose(pT[0:S, 0:P], x1[:, 0:S], m.ident[:])
                    for d in range(3):
                        mm = nc.tensor.transpose(pT[0:V, (1 + d) * P:(2 + d) * P], x1[:, S + d * V:S + (d + 1) * V],
                                                 m.ident[:])
                    mm.then_inc(s["turned"], 1)
                    pe.wait_ge(s["turned_copied"], 2 * t + 2)
                    pe.wait_ge(s["kept"], 8 * t + 1)
                    nc.tensor.matmul(p_s[:, 0:D], xT[:, 0:P], m.ms[:], start=True, stop=True)
                    for d in range(3):
                        mm = nc.tensor.matmul(p_v[:, d * P:(d + 1) * P], xT[0:V, (1 + d) * P:(2 + d) * P], m.mv[:],
                                              start=True, stop=True)
                    mm.then_inc(s["mapped"], 1)

            @block.vector
            def _(dve):
                dve.sem_inc(s["kept"], 1)
                dve.wait_ge(s["zeroed"], 1)
                with dve.Fori(0, NT) as t:
                    dve.wait_ge(s["mapped"], t + 2)
                    for n, k in enumerate((KONE, KDIST)):
                        nc.vector.tensor_copy(tables[:, k, bass.ds(t, 1), 0:S], p_s[:, n * S:(n + 1) * S].unsqueeze(1)
                                              ).then_inc(s["kept"], 1)
                        nc.vector.tensor_copy(
                            tables[:, k, bass.ds(t, 1), S:D].rearrange("p o (d c) -> p (o d) c", d=3),
                            p_v[:, 0:3 * P].rearrange("p (d c) -> p d c", d=3)[:, :, n * V:(n + 1) * V],
                        ).then_inc(s["kept"], 1)
                    for d in range(3):
                        nc.vector.tensor_copy(tables[:, KX[d], bass.ds(t, 1), 0:S],
                                              p_v[:, d * P + 2 * V:(d + 1) * P].unsqueeze(1)).then_inc(s["kept"], 1)
                    for d in range(3):
                        ins = nc.vector.tensor_copy(tables[:, KX[d], bass.ds(t, 1), S + d * V:S + (d + 1) * V],
                                                    p_s[:, 2 * S:D].unsqueeze(1))
                        if d == 2:
                            ins.then_inc(s["kept"], 1)

            @block.sync
            def _(sp):
                sp.wait_ge(s["kept"], 8 * NT + 1)
                for k in range(NY):
                    sp.dma_start(m.sums[k * NP:(k + 1) * NP, :].rearrange("(p t) f -> p t f", t=NT),
                                 tables[:, k, :, :]).then_inc(s["stored"], 16)
                sp.wait_ge(s["stored"], 16 * NY)
    phase_end(nc, m)


def update_clear_phase(nc, m):
    s = names(m, "cleared src_made")
    with nc.Block() as block:
        @block.sync
        def _(sp):
            for t in range(TPC):
                sp.dma_start(m.by_src[t][0:NP, :].rearrange("(p t) f -> p (t f)", t=NT), m.zero[:]).then_inc(s["cleared"], 16)
                sp.dma_start(m.by_src[t][NP:NP + P, :], m.zero[:, 0:D]).then_inc(s["cleared"], 16)
            sp.wait_ge(s["cleared"], 16 * 2 * TPC)

        @block.vector
        def _(dve):
            nc.vector.tensor_copy(m.base[:], m.base0[:])
            nc.vector.tensor_copy(m.src_f[:], m.src[:, 0:CH * TPC]).then_inc(s["src_made"], 1)
            dve.wait_ge(s["src_made"], 1)
            nc.vector.tensor_scalar(m.to_spare[:], m.src_f[:], m.rows[:, 2:3], -1.0, ALU.subtract, ALU.mult)
    phase_end(nc, m)


def edge_phase_3(nc, m, io):
    KW = NY * W
    s = names(m, "rows_copied landed turns used weighted_ready same_ready row0 row1 row2 row3 mixed mixed_copied "
                 "messages_psum messages_ready chained index_ready",
              "t0 t1 t2 t3 w0 w1 w2 w3 w4 w5 w6 w7")
    row_loaded = [s["row0"], s["row1"], s["row2"], s["row3"]]
    gathered = [s["t0"], s["t1"], s["t2"], s["t3"]]
    scattered = [[s["w0"], s["w1"], s["w2"], s["w3"]], [s["w4"], s["w5"], s["w6"], s["w7"]]]
    with ExitStack() as ctx:
        sb = lambda name, shape, dt=F32, n=NB: [ctx.enter_context(nc.sbuf_tensor(m.tag + f"e3_{name}{b}", shape, dt))
                                                for b in range(n)]
        ps = lambda name, shape: [ctx.enter_context(nc.psum_tensor(m.tag + f"e3_{name}{b}", shape, F32)) for b in range(2)]
        window_rows = sb("window_rows", [P, 1], I32)
        window = sb("window", [P, D])
        src_row = sb("src_row", [P, TPC * P], I32)
        onehot = sb("onehot", [P, TPC, W], n=2)
        weighted = sb("weighted", [P, TPC, NY, W], n=2)
        same = sb("same", [P, TPC, P], n=2)
        before = sb("before", [P, TPC, P], n=1)[0]
        count, moved = sb("count", [P, TPC], n=1)[0], sb("moved", [P, TPC], n=1)[0]
        index = sb("index", [P, TPC], I32)
        mixed_sb = sb("mixed_sb", [P, TPC * P], n=2)
        message = sb("message", [P, TPC, D])
        mixed_ps = ps("mixed", [P, TPC * P])
        mess_ps = ps("mess", [P, TPC, 256])
        with nc.Block() as block:
            @block.sync
            def _(sp):
                def load(c, b):
                    sp.dma_start(src_row[b][:], io["src_rows"][bass.ds(c, 1), :].to_broadcast([P, TPC * P])
                                 ).then_inc(row_loaded[b], 16)

                for b in range(NB):
                    load(b, b)
                with sp.Fori(0, ITERS) as i:
                    for b in range(NB):
                        sp.wait_ge(s["same_ready"], i * NB + b + 1)
                        load((i + 1) * NB + b, b)
                for b in range(NB):
                    sp.wait_ge(row_loaded[b], (ITERS + 1) * 16)

            @block.scalar
            def _(act):
                def rows(c, b):
                    nc.scalar.copy(window_rows[b][:], m.window_rows[:, 1, bass.ds(c, 1)]).then_inc(s["rows_copied"], 1)

                def mixed(c, b):
                    act.wait_ge(s["mixed"], c + 1 + 2)
                    act.wait_ge(s["messages_psum"], c + 3)
                    nc.scalar.copy(mixed_sb[b % 2][0:KW, :], mixed_ps[b % 2][0:KW, :]).then_inc(s["mixed_copied"], 1)

                def messages(c, i, b):
                    act.wait_ge(s["messages_psum"], c + 1 + NB)
                    act.wait_ge(s["landed"], c + 1)
                    nc.scalar.copy(message[b][:], mess_ps[b % 2][:, :, 0:D]).then_inc(s["messages_ready"], 1)
                    act.wait_ge(gathered[b], (i + 1) * 16)
                    rows(c + NB, b)

                act.sem_inc(s["mixed_copied"], 2)
                act.sem_inc(s["messages_ready"], 2)
                for b in range(NB):
                    rows(b, b)
                mixed(0, 0)
                for b in range(1, NB):
                    mixed(b, b)
                    messages(b - 1, 0, b - 1)
                with act.Fori(1, ITERS) as i:
                    for b in range(NB):
                        mixed(i * NB + b, b)
                        messages(i * NB + b - 1, *((i, b - 1) if b else (i - 1, NB - 1)))
                messages(CH - 1, ITERS - 1, NB - 1)

            @block.gpsimd
            def _(pool):
                def gather(c, b):
                    pool.wait_ge(s["rows_copied"], c + 1)
                    pool.wait_ge(s["messages_psum"], c + 1)
                    pool.sem_inc(s["turns"], 1)
                    nc.gpsimd.indirect_dma_start(
                        out=window[b][0:KW, :], out_offset=None, in_=m.sums,
                        in_offset=IndirectOffsetOnAxis(ap=window_rows[b][0:KW, :], axis=0),
                    ).then_inc(gathered[b], 16)

                def scatter(c, b, turns_before):
                    pool.wait_ge(s["messages_ready"], c + 1 + 2)
                    pool.wait_ge(s["index_ready"], c + 1)
                    for t in range(TPC):
                        if turns_before is not None:
                            pool.wait_ge(scattered[(b + 1) % 2][t], turns_before * 16)
                        pool.sem_inc(s["turns"], 1)
                        nc.gpsimd.indirect_dma_start(
                            out=m.by_src[t], out_offset=IndirectOffsetOnAxis(ap=index[b][:, t:t + 1], axis=0),
                            in_=message[b][:, t, :], in_offset=None, compute_op=ALU.add,
                        ).then_inc(scattered[b % 2][t], 16)
                    pool.sem_inc(s["landed"], 1)

                def turn(i, first):
                    for b in range(NB):
                        before_b = (i * 2 if b == 0 else i * 2 + 1 if b in (1, 2) else i * 2 + 2)
                        scatter(i * NB + b, b, None if first and b == 0 else before_b)
                        yield b

                pool.sem_inc(s["landed"], NB - 1)
                for b in range(NB):
                    pool.wait_ge(s["rows_copied"], b + 1)
                    nc.gpsimd.indirect_dma_start(
                        out=window[b][0:KW, :], out_offset=None, in_=m.sums,
                        in_offset=IndirectOffsetOnAxis(ap=window_rows[b][0:KW, :], axis=0),
                    ).then_inc(gathered[b], 16)
                for b in turn(0, True):
                    gather(NB + b, b)
                with pool.Fori(1, ITERS - 1) as i:
                    for b in turn(i, False):
                        gather((i + 1) * NB + b, b)
                for b in turn(ITERS - 1, False):
                    pass
                for parity in range(2):
                    for t in range(TPC):
                        pool.wait_ge(scattered[parity][t], 16 * CH // 2)

            @block.vector
            def _(dve):
                with dve.Fori(0, ITERS) as i:
                    for b in range(NB):
                        c, b2 = i * NB + b, b % 2
                        dve.wait_ge(s["mixed"], c + 1)
                        nc.vector.tensor_tensor(
                            onehot[b2][:], m.iota[:, 0:W].unsqueeze(1).to_broadcast([P, TPC, W]),
                            m.rel[:, bass.ds(c * TPC, TPC)].unsqueeze(2).to_broadcast([P, TPC, W]),
                            ALU.is_equal).then_inc(s["chained"], 1)
                        dve.wait_ge(row_loaded[b], (i + 1) * 16)
                        src = m.src_f[:, bass.ds(c * TPC, TPC)]
                        nc.vector.tensor_tensor(
                            same[b2][:], src_row[b][:].rearrange("p (t e) -> p t e", t=TPC),
                            src.unsqueeze(2).to_broadcast([P, TPC, P]), ALU.is_equal).then_inc(s["same_ready"], 1)
                        dve.wait_ge(s["chained"], c * 4 + 1)
                        y = m.y[:, bass.ds(c * TPC * NY, TPC * NY)].rearrange("p (t k) -> p t k", k=NY)
                        nc.vector.tensor_tensor(
                            weighted[b2][:], onehot[b2][:].unsqueeze(2).to_broadcast([P, TPC, NY, W]),
                            y.unsqueeze(3).to_broadcast([P, TPC, NY, W]), ALU.mult).then_inc(s["weighted_ready"], 1)
                        dve.wait_ge(s["same_ready"], c + 1)
                        nc.vector.tensor_tensor(before[:], same[b2][:], m.lower[:].unsqueeze(1).to_broadcast([P, TPC, P]),
                                                ALU.mult).then_inc(s["chained"], 1)
                        dve.wait_ge(s["chained"], c * 4 + 2)
                        nc.vector.tensor_reduce(count[:], before[:], AX.X, ALU.add).then_inc(s["chained"], 1)
                        dve.wait_ge(s["chained"], c * 4 + 3)
                        nc.vector.scalar_tensor_tensor(moved[:], count[:], 0.5, m.to_spare[:, bass.ds(c * TPC, TPC)],
                                                       ALU.is_gt, ALU.mult).then_inc(s["chained"], 1)
                        dve.wait_ge(s["chained"], c * 4 + 4)
                        dve.wait_ge(s["landed"], c + 1)
                        nc.vector.tensor_tensor(index[b][:], moved[:], src, ALU.add).then_inc(s["index_ready"], 1)

            @block.tensor
            def _(pe):
                def mix(c, b):
                    pe.wait_ge(s["weighted_ready"], c + 1)
                    pe.wait_ge(s["same_ready"], c + 1)
                    pe.wait_ge(s["mixed_copied"], c + 1)
                    for t in range(TPC):
                        mm = nc.tensor.matmul(mixed_ps[b % 2][0:KW, t * P:(t + 1) * P],
                                              weighted[b % 2][:, t, :, :].rearrange("p k n -> p (k n)"),
                                              same[b % 2][:, t, :], start=True, stop=True)
                    mm.then_inc(s["mixed"], 1)

                def messages(c, i, b):
                    pe.wait_ge(s["mixed_copied"], c + 1 + 2)
                    pe.wait_ge(gathered[b], (i + 1) * 16)
                    pe.wait_ge(s["messages_ready"], c + 1)
                    for t in range(TPC):
                        mm = nc.tensor.matmul(mess_ps[b % 2][:, t, 0:D], mixed_sb[b % 2][0:KW, t * P:(t + 1) * P],
                                              window[b][0:KW, :], start=True, stop=True)
                    mm.then_inc(s["messages_psum"], 1)

                pe.sem_inc(s["mixed"], 2)
                pe.sem_inc(s["messages_psum"], NB)
                mix(0, 0)
                for b in range(1, NB):
                    mix(b, b)
                    messages(b - 1, 0, b - 1)
                with pe.Fori(1, ITERS) as i:
                    for b in range(NB):
                        mix(i * NB + b, b)
                        messages(i * NB + b - 1, *((i, b - 1) if b else (i - 1, NB - 1)))
                messages(CH - 1, ITERS - 1, NB - 1)
    phase_end(nc, m)


def update_node_phase(nc, m):
    s = names(m, "loaded x_copied turned turned_copied a_copied a_turned a_turned_copied y_psum "
                 "products h_done linked pe_turns linear_psum added")
    N0, N1 = 20, 4
    with ExitStack() as ctx:
        sb = lambda name, shape: ctx.enter_context(nc.sbuf_tensor(m.tag + "un_" + name, shape, F32))
        ps = lambda name: ctx.enter_context(nc.psum_tensor(m.tag + "un_ps_" + name, [P, 512], F32))
        sums, xs = sb("sums", [P, TPC, D]), sb("xs", [P, D])
        p_x, p_a, p_out = ps("x"), ps("a"), ps("out")
        p_y = [ps(f"y{n}") for n in range(3)]
        x_T = sb("x_T", [S, 4 * P])
        halves = sb("halves", [P, 2, D])
        a = sb("a", [P, D])
        a0T = sb("a0T", [S, P])
        prod0, prod1 = sb("prod0", [P, N0, 8, S]), sb("prod1", [P, 3, S, V])
        out0, out1 = sb("out0", [P, S]), sb("out1", [P, 3, V])
        xT = [x_T[:, 0:P]] + [x_T[0:V, d * P:(d + 1) * P] for d in (1, 2, 3)]
        with nc.Block() as block:
            @block.sync
            def _(sp):
                rows = [one[0:NP, :].rearrange("(p t) f -> p t f", t=NT) for one in m.by_src]
                with sp.Fori(0, NT) as t:
                    sp.wait_ge(s["added"], 2 * t + 2)
                    for k in range(TPC):
                        sp.dma_start(sums[:, k, :].unsqueeze(1), rows[k][:, bass.ds(t, 1), :]).then_inc(s["loaded"], 16)

            @block.scalar
            def _(act):
                with act.Fori(0, NT) as t:
                    act.wait_ge(s["h_done"], t + 1)
                    nc.scalar.copy(xs[:].unsqueeze(1), m.x[:, bass.ds(t, 1), :]).then_inc(s["x_copied"], 1)
                    act.wait_ge(s["turned"], t + 1)
                    nc.scalar.copy(x_T[:, 0:P], p_x[0:S, 0:P]).then_inc(s["turned_copied"], 1)
                    nc.scalar.copy(x_T[0:V, P:4 * P], p_x[0:V, P:4 * P]).then_inc(s["turned_copied"], 1)
                    act.wait_ge(s["a_turned"], t + 1)
                    nc.scalar.copy(a0T[:], p_a[0:S, 0:P]).then_inc(s["a_turned_copied"], 1)

            @block.tensor
            def _(pe):
                with pe.Fori(0, NT) as t:
                    turn, mm = nc.tensor.transpose, nc.tensor.matmul
                    pe.wait_ge(s["x_copied"], t + 1)
                    pe.sem_inc(s["pe_turns"], 1)
                    turn(p_x[0:S, 0:P], xs[:, 0:S], m.ident[:])
                    for d in range(3):
                        last = turn(p_x[0:V, (1 + d) * P:(2 + d) * P], xs[:, S + d * V:S + (d + 1) * V], m.ident[:])
                    last.then_inc(s["turned"], 1)
                    pe.wait_ge(s["turned_copied"], (t + 1) * 2)
                    mm(p_out[:, 0:S], xT[0], m.lu0[:], start=True, stop=True)
                    for d in range(3):
                        last = mm(p_out[:, S + d * V:S + (d + 1) * V], xT[1 + d], m.lu1[:], start=True, stop=True)
                    last.then_inc(s["linear_psum"], 1)
                    pe.wait_ge(s["a_copied"], t + 1)
                    pe.sem_inc(s["pe_turns"], 1)
                    turn(p_a[0:S, 0:P], a[:, 0:S], m.ident[:]).then_inc(s["a_turned"], 1)
                    blocks = [(xT[0], m.u000, j) for j in range(8)]
                    blocks += [(xT[1 + d], m.u110, j) for d in range(3) for j in range(4)]
                    blocks += [(xT[0], m.u011, 0), (xT[0], m.u011, 1), (a0T[:], m.u101, 0), (a0T[:], m.u101, 1)]
                    for n, (fixed, u, j) in enumerate(blocks):
                        pe.wait_ge(s["products"], t * (N0 + N1) + n + 1)
                        if n == N0 + 2:
                            pe.wait_ge(s["a_turned_copied"], t + 1)
                        mm(p_y[n % 3][:], fixed, u[:, j * 512:(j + 1) * 512], start=True, stop=True).then_inc(s["y_psum"], 1)

            @block.vector
            def _(dve):
                dve.sem_inc(s["products"], 3)
                dve.sem_inc(s["h_done"], 1)
                dve.sem_inc(s["added"], 2)
                tt = nc.vector.tensor_tensor
                with dve.Fori(0, NT) as t:
                    dve.wait_ge(s["loaded"], (t + 1) * 16 * TPC)
                    tt(halves[:], sums[:, 0:2, :], sums[:, 2:4, :], ALU.add).then_inc(s["added"], 1)
                    dve.wait_ge(s["added"], 2 * t + 3)
                    tt(a[:], halves[:, 0, :], halves[:, 1, :], ALU.add).then_inc(s["a_copied"], 1)
                    dve.wait_ge(s["a_copied"], t + 1)
                    dve.sem_inc(s["added"], 1)
                    for n in range(N0 + N1):
                        dve.wait_ge(s["y_psum"], t * (N0 + N1) + n + 1)
                        y = p_y[n % 3]
                        if n < N0:
                            v0 = 8 * n if n < 8 else S + (n - 8) * 8
                            tt(prod0[:, n, :, :], y[:].rearrange("p (v w) -> p v w", w=S),
                               a[:, v0:v0 + 8].unsqueeze(2).to_broadcast([P, 8, S]), ALU.mult).then_inc(s["products"], 1)
                        else:
                            other, j = (a, n - N0) if n < N0 + 2 else (xs, n - N0 - 2)
                            f = other[:, S:D].rearrange("p (d v) -> p d v", d=3)[:, :, 16 * j:16 * j + 16]
                            at = 16 * j + (0 if other is a else V)
                            tt(prod1[:, :, at:at + 16, :],
                               y[:].rearrange("p (v w) -> p v w", w=V).unsqueeze(1).to_broadcast([P, 3, 16, V]),
                               f.unsqueeze(3).to_broadcast([P, 3, 16, V]), ALU.mult).then_inc(s["products"], 1)
                    dve.wait_ge(s["products"], (t + 1) * (N0 + N1) + 3)
                    nc.vector.tensor_reduce(out0[:], prod0[:].rearrange("p n v w -> p w (n v)"), AX.X,
                                            ALU.add).then_inc(s["linked"], 1)
                    nc.vector.tensor_reduce(out1[:], prod1[:].rearrange("p d v w -> p d w v"), AX.X,
                                            ALU.add).then_inc(s["linked"], 1)
                    dve.wait_ge(s["linear_psum"], t + 1)
                    h = m.h[:, bass.ds(t, 1), :]
                    nc.vector.scalar_tensor_tensor(h, xs[:].unsqueeze(1), 2.0, p_out[:, 0:D].unsqueeze(1),
                                                   ALU.mult, ALU.add).then_inc(s["linked"], 1)
                    dve.wait_ge(s["linked"], t * 5 + 3)
                    tt(h[:, :, 0:S], h[:, :, 0:S], out0[:].unsqueeze(1), ALU.add).then_inc(s["linked"], 1)
                    tt(h[:, :, S:D], h[:, :, S:D], out1[:].rearrange("p d w -> p (d w)").unsqueeze(1),
                       ALU.add).then_inc(s["linked"], 1)
                    dve.wait_ge(s["linked"], t * 5 + 5)
                    dve.sem_inc(s["h_done"], 1)
    phase_end(nc, m)


def update_layer(nc, m, io, rounds):
    with ExitStack() as ctx:
        sb = lambda name, shape: ctx.enter_context(nc.sbuf_tensor(m.tag + "ul_" + name, shape, F32))
        m.ms, m.mv = sb("ms", [S, D]), sb("mv", [V, P])
        m.lower, m.src_f, m.to_spare = sb("lower", [P, P]), sb("src_f", [P, CH * TPC]), sb("to_spare", [P, CH * TPC])
        m.u000, m.u110 = sb("u000", [S, S * S]), sb("u110", [V, V * S])
        m.u011, m.u101 = sb("u011", [S, V * V]), sb("u101", [S, V * V])
        m.lu0, m.lu1 = sb("lu0", [S, S]), sb("lu1", [V, V])
        update_weights_phase(nc, m, io)
        update_tables_phase(nc, m)
        update_clear_phase(nc, m)
        with nc.Fori(0, rounds):
            window_phase(nc, m)
            edge_phase_3(nc, m, io)
        m.h = sb("h", [P, NT, D])
        update_node_phase(nc, m)
        layernorm_phase(nc, m)


H, AS, AV = 4, 16, 8
BIG = 1e30
ROW0 = H * D + H


def attention_weights_phase(nc, m, io):
    s = names(m, "zeroed loaded scaled gate_psum gate_kept head_psum head_kept")
    with ExitStack() as ctx:
        sb = lambda name, shape: ctx.enter_context(nc.sbuf_tensor(m.tag + "aw_" + name, shape, F32))
        valT, wg = sb("valT", [S, 96]), sb("wg", [S, V])
        slT, ps_w = sb("slT", [AS, H * 96]), sb("ps_w", [AS, H * S])
        vlT, pv_w = sb("vlT", [AV, H * P]), sb("pv_w", [AV, H * V])
        w2 = sb("w2", [P, 2])
        p_gate = ctx.enter_context(nc.psum_tensor(m.tag + "aw_pg", [P, 512], F32))
        p_s = ctx.enter_context(nc.psum_tensor(m.tag + "aw_ps", [P, 512], F32))
        p_v = ctx.enter_context(nc.psum_tensor(m.tag + "aw_pv", [P, 512], F32))
        loads = [(m.rbf[:, a:b], io["L0_gnn_W_rbf"][:, c:d]) for a, b, c, d in
                 ((0, 64, 0, 64), (64, 96, 160, 192), (96, 160, 64, 128), (160, 192, 128, 160), (192, 224, 192, 224))]
        loads += [(m.att[0:96, 0:S], io["L0_gnn_W_alpha"]), (m.att[0:96, S:2 * S], io["L0_gnn_Ws_val"]),
                  (m.val_v[:], io["L0_gnn_Wv_val"]), (m.alpha[:], io["alpha_rows"]),
                  (m.gamma_s[:], io["gamma_s_rows"]), (m.beta_s[:], io["beta_s_rows"]), (m.gamma_v[:], io["gamma_v_rows"]),
                  (m.head_mask[:], io["head_mask"]), (m.repeat[:], io["repeat"]),
                  (valT[:], io["valT"]), (wg[:], io["L0_gnn_Wg"]), (slT[:], io["slT"]), (ps_w[:], io["ps_w"]),
                  (vlT[:], io["vlT"]), (pv_w[:], io["pv_w"]),
                  (w2[0:S, 0:1], io["w2_ss"]), (w2[S:96, 0:1], io["w2_vv0"]),
                  (w2[0:S, 1:2], io["w2_sv"]), (w2[S:96, 1:2], io["w2_vs"]), (w2[96:P, 1:2], io["w2_vv1"])]
        for j, (ws, wv) in enumerate([(io["L0_gnn_Ws_dst"], io["L0_gnn_Wv_dst"]), (io["L0_gnn_Ws_src"], io["L0_gnn_Wv_src"])]):
            loads += [(m.lin_a[0:S, j * D:j * D + S], ws),
                      (m.lin_a[S:S + V, j * D + S:j * D + S + V], wv),
                      (m.lin_a[S + V:P, j * D + S + V:j * D + P], wv),
                      (m.lin_b[:, j * D + P:(j + 1) * D], wv)]
        with nc.Block() as block:
            @block.vector
            def _(dve):
                nc.vector.memset(m.lin_a[:], 0.0).then_inc(s["zeroed"], 1)
                nc.vector.memset(m.lin_b[:], 0.0).then_inc(s["zeroed"], 1)
                nc.vector.memset(m.att[:], 0.0).then_inc(s["zeroed"], 1)
                nc.vector.memset(m.out_s[:], 0.0).then_inc(s["zeroed"], 1)
                nc.vector.memset(w2[:], 0.0).then_inc(s["zeroed"], 1)
                nc.vector.memset(m.ones[:], 1.0)

            @block.sync
            def _(sp):
                sp.wait_ge(s["zeroed"], 5)
                for to, what in loads:
                    sp.dma_start(to, what).then_inc(s["loaded"], 16)

            @block.tensor
            def _(pe):
                pe.wait_ge(s["loaded"], 16 * len(loads))
                nc.tensor.matmul(p_gate[0:96, 0:V], valT[:], wg[:], start=True, stop=True).then_inc(s["gate_psum"], 1)
                for h in range(H):
                    nc.tensor.matmul(p_s[0:96, h * S:(h + 1) * S], slT[:, h * 96:(h + 1) * 96],
                                     ps_w[:, h * S:(h + 1) * S], start=True, stop=True)
                    mm = nc.tensor.matmul(p_v[:, h * V:(h + 1) * V], vlT[:, h * P:(h + 1) * P],
                                          pv_w[:, h * V:(h + 1) * V], start=True, stop=True)
                mm.then_inc(s["head_psum"], 1)

            @block.scalar
            def _(act):
                act.wait_ge(s["loaded"], 16 * len(loads))
                nc.scalar.mul(m.rbf[:, 64:96], m.rbf[:, 64:96], 3 ** -0.5)
                nc.scalar.mul(m.rbf[:, 192:224], m.rbf[:, 192:224], 2 ** -0.5)
                nc.scalar.mul(w2[S:96, 0:1], w2[S:96, 0:1], 3 ** -0.5).then_inc(s["scaled"], 1)
                nc.scalar.mul(w2[96:P, 1:2], w2[96:P, 1:2], 2 ** -0.5).then_inc(s["scaled"], 1)
                act.wait_ge(s["gate_psum"], 1)
                nc.scalar.copy(m.att[0:96, 2 * S:D], p_gate[0:96, 0:V])
                act.wait_ge(s["scaled"], 2)
                act.wait_ge(s["head_psum"], 1)
                nc.scalar.activation(m.out_s[0:96, :], p_s[0:96, 0:H * S], ACT.Copy, scale=w2[0:96, 0:1])
                nc.scalar.activation(m.out_v[:], p_v[:, 0:H * V], ACT.Copy, scale=w2[:, 1:2])
    phase_end(nc, m)


def equivariant_norm_phase(nc, m):
    s = names(m, "linked squared rooted vec_squared vec_rooted")
    with ExitStack() as ctx:
        sb = lambda name, shape: ctx.enter_context(nc.sbuf_tensor(m.tag + "en_" + name, shape, F32))
        mean, var, power = sb("mean", [P, NT]), sb("var", [P, NT]), sb("power", [P, NT])
        square, vsquare = sb("square", [P, NT, S]), sb("vsquare", [P, NT, 3 * V])
        wide = lambda a, n: a[:].unsqueeze(2).to_broadcast([P, NT, n])
        over = lambda a, n: a[:].unsqueeze(1).to_broadcast([P, NT, n])
        sn = m.xn[:, :, 0:S]
        with nc.Block() as block:
            @block.vector
            def _(dve):
                link = linker(dve, s["linked"])
                tt = nc.vector.tensor_tensor
                link(nc.vector.tensor_reduce(mean[:], m.x[:, :, 0:S], AX.X, ALU.add))
                link(nc.vector.tensor_scalar(mean[:], mean[:], 1.0 / S, None, ALU.mult))
                link(tt(sn, m.x[:, :, 0:S], wide(mean, S), ALU.subtract))
                dve.wait_ge(s["squared"], 1)
                link(nc.vector.tensor_reduce(var[:], square[:], AX.X, ALU.add))
                dve.wait_ge(s["vec_squared"], 1)
                link(nc.vector.tensor_reduce(power[:], vsquare[:], AX.X, ALU.add))
                dve.wait_ge(s["rooted"], 2)
                link(nc.vector.reciprocal(var[:], var[:]))
                link(nc.vector.reciprocal(power[:], power[:]))
                link(tt(sn, sn, wide(var, S), ALU.mult))
                link(tt(sn, sn, over(m.gamma_s, S), ALU.mult))
                link(tt(sn, sn, over(m.beta_s, S), ALU.add))
                for d in range(3):
                    v = slice(S + d * V, S + (d + 1) * V)
                    link(tt(m.xn[:, :, v], m.x[:, :, v], wide(power, V), ALU.mult))
                    link(tt(m.xn[:, :, v], m.xn[:, :, v], over(m.gamma_v, V), ALU.mult))

            @block.scalar
            def _(act):
                nc.scalar.activation(vsquare[:], m.x[:, :, S:D], ACT.Square).then_inc(s["vec_squared"], 1)
                act.wait_ge(s["linked"], 3)
                nc.scalar.activation(square[:], sn, ACT.Square).then_inc(s["squared"], 1)
                act.wait_ge(s["linked"], 5)
                nc.scalar.activation(var[:], var[:], ACT.Sqrt, bias=m.eps[:, 0:1], scale=1.0 / S).then_inc(s["rooted"], 1)
                nc.scalar.activation(power[:], power[:], ACT.Sqrt, bias=m.eps[:, 0:1], scale=1.0 / V).then_inc(s["rooted"], 1)
    phase_end(nc, m)


def attention_clear_phase(nc, m, io):
    s = names(m, "low_ready cleared")
    with ExitStack() as ctx:
        low = ctx.enter_context(nc.sbuf_tensor(m.tag + "ac_low", [P, NT * D], F32))
        with nc.Block() as block:
            @block.vector
            def _(dve):
                nc.vector.memset(low[:], -BIG).then_inc(s["low_ready"], 1)
                nc.vector.tensor_copy(m.base[:], m.base0[:])
                nc.vector.memset(m.node_rows[:], 0)
                nc.vector.memset(m.maxima_rows[:], 0)
                nc.vector.memset(m.all_max[:], 0.0)

            @block.sync
            def _(sp):
                sp.dma_start(m.chunk_rows[:], io["chunk_rows"]).then_inc(s["cleared"], 16)
                n = 1
                flat = m.att_sums.rearrange("r f -> (r f)").rearrange("(p x) -> p x", p=P)
                width = flat.shape[1]
                for a in range(0, width, NT * D):
                    b = min(a + NT * D, width)
                    sp.dma_start(flat[:, a:b], m.zero[:, 0:b - a]).then_inc(s["cleared"], 16)
                    n += 1
                sp.wait_ge(s["low_ready"], 1)
                flat = m.maxima.rearrange("r h -> (r h)").rearrange("(p x) -> p x", p=P)
                width = flat.shape[1]
                for a in range(0, width, NT * D):
                    b = min(a + NT * D, width)
                    sp.dma_start(flat[:, a:b], low[:, 0:b - a]).then_inc(s["cleared"], 16)
                    n += 1
                sp.wait_ge(s["cleared"], 16 * n)
    phase_end(nc, m)


def attention_window_phase(nc, m):
    s = names(m, "made")
    with nc.Block() as block:
        @block.vector
        def _(dve):
            nc.vector.tensor_scalar(m.node_rows_f[:], m.base[:], m.rows[:, 3:4], -float(W), ALU.add,
                                    ALU.add).then_inc(s["made"], 1)
            dve.wait_ge(s["made"], 1)
            nc.vector.tensor_copy(m.node_rows[:, 0:CH], m.node_rows_f[:])
            nc.vector.tensor_tensor(m.maxima_rows[:, 0:CH], m.node_rows_f[:], m.chunk_rows[:], ALU.add)
    phase_end(nc, m)


class Chain:

    def __init__(self, eng, sem):
        self.eng, self.sem, self.base, self.n = eng, sem, 0, 0

    def add(self, ins):
        self.n += 1
        ins.then_inc(self.sem, 1)

    def wait(self):
        self.eng.wait_ge(self.sem, self.base + self.n)

    def start(self):
        self.prologue = self.n

    def turn(self, c, each):
        self.base, self.n, self.each = c * each + self.prologue, 0, each

    def end(self):
        assert self.n == self.each, self.n


def attention_edge_phase(nc, m, io):
    NV = 24
    s = names(m, "cols_ready turns onehot_ready onehotT_psum onehotT_ready dst_psum dst_added weights_psum "
                 "products_ready turned turned_copied values_psum leak_ready values_ready mask_ready mask_psum "
                 "max_taken max_spread repeat_psum shift_psum shifted exp_ready attended_ready summed "
                 "staged chained scal0 scal1 scal2 scal3 stored0 stored1 maxima_ready keeping maxima_landed turns_pe",
              "g0 g1 g2 g3 w0 w1 w2 w3")
    gathered, scal_loaded = [s["g0"], s["g1"], s["g2"], s["g3"]], [s["scal0"], s["scal1"], s["scal2"], s["scal3"]]
    maxima_out, stored = [s["w0"], s["w1"], s["w2"], s["w3"]], [s["stored0"], s["stored1"]]
    with ExitStack() as ctx:
        sb = lambda name, shape, n=1, dt=F32: [ctx.enter_context(nc.sbuf_tensor(m.tag + f"ae_{name}{b}", shape, dt))
                                               for b in range(n)]
        ps = lambda name, shape: ctx.enter_context(nc.psum_tensor(m.tag + "ae_ps_" + name, shape, F32))
        src_cols, win_col, max_col = sb("src_cols", [P, TPC], NB, I32), sb("win", [P, 1], NB, I32), sb("maxc", [P, 1], NB, I32)
        xj = sb("xj", [P, TPC, D], NB)
        dst_win = sb("dst_win", [WS, D], NB)
        scal = sb("scal", [16, TPC * P], NB)
        onehot, onehotT = sb("onehot", [P, TPC, WS], 2), sb("onehotT", [WS, TPC * P], 2)
        msg, x, tmp = sb("msg", [P, TPC, D])[0], sb("x", [P, TPC, 4, P])[0], sb("tmp", [P, TPC, 3, V])[0]
        xT = sb("xT", [P, 4 * P], 2)
        leak, leak2 = sb("leak", [P, TPC, S], 2), sb("leak2", [P, TPC, S])[0]
        score, low = sb("score", [P, TPC, H], 2), sb("low", [P, TPC, WS])[0]
        masked = sb("masked", [P, TPC, H, WS])[0]
        mx, by_head = sb("mx", [P, 1])[0], sb("by_head", [P, H])[0]
        win_max = sb("win_max", [P, H], NB)
        ex_in, ex = sb("ex_in", [P, TPC, H])[0], sb("ex", [P, TPC, H], 2)
        z, gate, vv = sb("z", [P, TPC, D], 2), sb("gate", [P, TPC, V], 2), sb("vv", [P, TPC, 3, V], 2)
        ye, attended = sb("ye", [P, TPC, H, 4])[0], sb("attended", [P, TPC, H * 4, WS], 2)
        stage = sb("stage", [P, ROW0], 2)
        p_dst, p_w, p_val = ps("dst", [P, 512]), ps("w", [P, TPC, 256]), ps("val", [P, TPC, 256])
        p_turn, p_a, p_b = ps("turn", [P, 512]), ps("a", [P, 512]), ps("b", [P, 512])
        p_onehotT, p_den, p_repeat, p_shift = p_turn[0:WS, :], p_b[0:WS, 320:324], p_dst[:, 320:324], p_dst[:, 324:340]
        tt, ts, red = nc.vector.tensor_tensor, nc.vector.tensor_scalar, nc.vector.tensor_reduce
        with nc.Block() as block:
            @block.sync
            def _(sp):
                def load(c, b):
                    sp.dma_start(scal[b][:], io["a16"][:, bass.ds(c * TPC * P, TPC * P)]).then_inc(scal_loaded[b], 16)

                for one in stored:
                    sp.sem_inc(one, 16)
                for b in range(NB):
                    load(b, b)
                with sp.Fori(0, ITERS) as i:
                    for b in range(NB):
                        c = i * NB + b
                        sp.wait_ge(s["weights_psum"], c + 1)
                        load(c + NB, b)
                        sp.wait_ge(s["staged"], c + 1 + 1)
                        sp.dma_start(m.chunk_sums[bass.ds(c, 1), :, :].rearrange("o p f -> p (o f)"),
                                     stage[b % 2][:]).then_inc(stored[b % 2], 16)
                for b in range(NB):
                    sp.wait_ge(scal_loaded[b], (ITERS + 1) * 16)
                for b in range(2):
                    sp.wait_ge(stored[b], (ITERS * 2 + 1) * 16)

            @block.gpsimd
            def _(pool):
                def gather(c, b):
                    pool.wait_ge(s["cols_ready"], c * 3 + 3)
                    pool.wait_ge(s["products_ready"], c + 1)
                    pool.sem_inc(s["turns"], 1)
                    nc.gpsimd.indirect_dma_start(
                        out=dst_win[b][:], out_offset=None, in_=m.dst_table,
                        in_offset=IndirectOffsetOnAxis(ap=win_col[b][0:WS, :], axis=0)).then_inc(gathered[b], 16)
                    for t in range(TPC):
                        nc.gpsimd.indirect_dma_start(
                            out=xj[b][:, t, :], out_offset=None, in_=m.table,
                            in_offset=IndirectOffsetOnAxis(ap=src_cols[b][:, t:t + 1], axis=0)).then_inc(gathered[b], 16)

                pool.sem_inc(s["maxima_landed"], NB)
                for b in range(NB):
                    gather(b, b)
                with pool.Fori(0, ITERS) as i:
                    for b in range(NB):
                        c = i * NB + b
                        pool.wait_ge(s["maxima_ready"], c + 1)
                        pool.sem_inc(s["turns"], 1)
                        nc.gpsimd.indirect_dma_start(
                            out=m.maxima, out_offset=IndirectOffsetOnAxis(ap=max_col[b][0:WS, :], axis=0),
                            in_=win_max[b][0:WS, :], in_offset=None).then_inc(maxima_out[b], 16)
                        pool.wait_ge(maxima_out[b], (i + 1) * 16)
                        pool.sem_inc(s["maxima_landed"], 1)
                        gather(c + NB, b)
                for b in range(NB):
                    pool.wait_ge(gathered[b], (ITERS + 1) * 16 * 5)

            @block.scalar
            def _(act):
                def columns(c, b):
                    nc.scalar.copy(src_cols[b][:], m.src[:, bass.ds(c * TPC, TPC)]).then_inc(s["cols_ready"], 1)
                    nc.scalar.copy(win_col[b][:], m.node_rows[:, bass.ds(c, 1)]).then_inc(s["cols_ready"], 1)
                    nc.scalar.copy(max_col[b][:], m.maxima_rows[:, bass.ds(c, 1)]).then_inc(s["cols_ready"], 1)

                def turn_onehot(c, b):
                    act.wait_ge(s["onehotT_psum"], c + 1)
                    act.wait_ge(s["shift_psum"], c + 1)
                    nc.scalar.copy(onehotT[b % 2][:], p_onehotT).then_inc(s["onehotT_ready"], 1)

                def products(c, b):
                    for t in range(TPC):
                        act.wait_ge(s["turned"], c * TPC + t + 1)
                        act.wait_ge(s["values_psum"], c * TPC + t + 1)
                        nc.scalar.copy(xT[t % 2][:], p_turn[:]).then_inc(s["turned_copied"], 1)

                def values(c, b):
                    act.wait_ge(s["values_psum"], (c + 1) * TPC + 2)
                    act.wait_ge(s["summed"], c + 1)
                    nc.scalar.copy(leak[b % 2][:], p_val[:, :, 0:S]).then_inc(s["leak_ready"], 1)
                    nc.scalar.activation(z[b % 2][:, :, 0:S], p_val[:, :, S:2 * S], ACT.Tanh, scale=0.5
                                         ).then_inc(s["values_ready"], 1)
                    nc.scalar.activation(gate[b % 2][:], p_val[:, :, 2 * S:D], ACT.Tanh, scale=0.5
                                         ).then_inc(s["values_ready"], 1)
                    nc.scalar.copy(vv[b % 2][:].rearrange("p t d c -> p t (d c)"), p_val[:, :, D:256]
                                   ).then_inc(s["values_ready"], 1)

                def exponentials(c, b):
                    act.wait_ge(s["shifted"], c + 1)
                    nc.scalar.activation(ex[b % 2][:], ex_in[:], ACT.Exp).then_inc(s["exp_ready"], 1)

                def keep(c, i, b):
                    act.wait_ge(s["summed"], c + 1 + 2)
                    act.wait_ge(stored[b % 2], (i * 2 + b // 2 + 1) * 16)
                    st = stage[b % 2]
                    nc.scalar.copy(st[:, 0:2 * D], p_a[:, 0:2 * D]).then_inc(s["keeping"], 1)
                    nc.scalar.copy(st[:, 2 * D:4 * D], p_b[:, 0:2 * D]).then_inc(s["keeping"], 1)
                    nc.scalar.copy(st[0:WS, 4 * D:ROW0], p_den).then_inc(s["keeping"], 1)
                    act.wait_ge(s["keeping"], (c + 1) * 3)
                    act.sem_inc(s["staged"], 1)

                act.sem_inc(s["staged"], 1)
                for b in range(2):
                    nc.scalar.copy(stage[b][:, 4 * D:ROW0], m.zero[:, 0:H])
                for b in range(NB):
                    columns(b, b)
                turn_onehot(0, 0)
                products(0, 0)
                values(0, 0)
                with act.Fori(0, ITERS) as i:
                    for b in range(NB):
                        c = i * NB + b
                        turn_onehot(c + 1, b + 1)
                        exponentials(c, b)
                        products(c + 1, b + 1)
                        values(c + 1, b + 1)
                        keep(c, i, b)
                        act.wait_ge(gathered[b], (i + 1) * 16 * 5)
                        act.wait_ge(s["maxima_landed"], c + 1 + NB)
                        columns(c + NB, b)

            @block.vector
            def _(dve):
                link = Chain(dve, s["chained"])

                def y_of(c):
                    return m.y[:, bass.ds(c * TPC * NY, TPC * NY)].rearrange("p (t k) -> p t k", k=NY)

                def find(c, b):
                    dve.wait_ge(s["summed"], c + 1)
                    tt(onehot[b % 2][:], m.iota[:].unsqueeze(1).to_broadcast([P, TPC, WS]),
                       m.rel[:, bass.ds(c * TPC, TPC)].unsqueeze(2).to_broadcast([P, TPC, WS]),
                       ALU.is_equal).then_inc(s["onehot_ready"], 1)

                def message(c, i, b):
                    y = y_of(c)
                    dve.wait_ge(gathered[b], (i + 1) * 16 * 5)
                    for half in range(2):
                        dve.wait_ge(s["dst_psum"], 2 * c + half + 1)
                        tt(msg[:, 2 * half:2 * half + 2, :], xj[b][:, 2 * half:2 * half + 2, :],
                           p_dst[:, 0:2 * D].rearrange("p (t f) -> p t f", f=D), ALU.add).then_inc(s["dst_added"], 1)
                    dve.wait_ge(s["dst_added"], 2 * c + 2 + 1)
                    link.add(tt(x[:, :, 3, 0:S], msg[:, :, 0:S], y[:, :, 3:4].to_broadcast([P, TPC, S]), ALU.mult))
                    link.add(tt(tmp[:], msg[:, :, S:D].rearrange("p t (d c) -> p t d c", d=3),
                            y[:, :, 0:3].unsqueeze(3).to_broadcast([P, TPC, 3, V]), ALU.mult))
                    link.wait()
                    link.add(red(x[:, :, 3, S:96], tmp[:].rearrange("p t d c -> p t c d"), AX.X, ALU.add))

                def outer(c):
                    y = y_of(c)
                    link.add(tt(x[:, :, 0:3, 0:S], msg[:, :, 0:S].unsqueeze(2).to_broadcast([P, TPC, 3, S]),
                            y[:, :, 0:3].unsqueeze(3).to_broadcast([P, TPC, 3, S]), ALU.mult))
                    link.add(tt(x[:, :, 0:3, S:96], msg[:, :, S:D].rearrange("p t (d c) -> p t d c", d=3),
                            y[:, :, 3:4].unsqueeze(3).to_broadcast([P, TPC, 3, V]), ALU.mult))

                def cross(c):
                    y = y_of(c)
                    link.wait()
                    for d in range(3):
                        for to, v, w in ((x[:, :, d, 96:P], (d + 1) % 3, (d + 2) % 3), (tmp[:, :, d, :], (d + 2) % 3, (d + 1) % 3)):
                            link.add(tt(to, msg[:, :, S + v * V:S + (v + 1) * V],
                                    y[:, :, w:w + 1].to_broadcast([P, TPC, V]), ALU.mult))
                    link.wait()
                    link.add(tt(x[:, :, 0:3, 96:P], x[:, :, 0:3, 96:P], tmp[:], ALU.subtract))

                def weigh(c):
                    link.wait()
                    dve.wait_ge(s["weights_psum"], c + 1)
                    link.add(tt(x[:, :, 0:3, :], x[:, :, 0:3, :], p_w[:, :, 96:224].unsqueeze(2).to_broadcast([P, TPC, 3, P]),
                            ALU.mult))
                    link.add(tt(x[:, :, 3, 0:96], x[:, :, 3, 0:96], p_w[:, :, 0:96], ALU.mult))
                    link.wait()
                    dve.sem_inc(s["products_ready"], 1)

                def scores(c, b):
                    dve.wait_ge(s["leak_ready"], c + 1)
                    link.add(nc.vector.scalar_tensor_tensor(leak2[:], leak[b % 2][:], 0.2, leak[b % 2][:], ALU.mult, ALU.max))
                    link.add(ts(low[:], onehot[b % 2][:], BIG, -BIG, ALU.mult, ALU.add))
                    link.wait()
                    link.add(tt(leak2[:], leak2[:], m.alpha[:].unsqueeze(1).to_broadcast([P, TPC, S]), ALU.mult))
                    link.wait()
                    link.add(red(score[b % 2][:], leak2[:].rearrange("p t (h a) -> p t h a", h=H), AX.X, ALU.add))
                    link.wait()
                    tt(masked[:], low[:].unsqueeze(2).to_broadcast([P, TPC, H, WS]),
                       score[b % 2][:].unsqueeze(3).to_broadcast([P, TPC, H, WS]), ALU.add).then_inc(s["mask_ready"], 1)

                def maxima(c):
                    dve.wait_ge(s["mask_psum"], c + 1)
                    red(mx[:], p_turn[:], AX.X, ALU.max).then_inc(s["max_taken"], 1)
                    dve.wait_ge(s["max_taken"], c + 1)
                    ts(by_head[:], m.head_mask[:], mx[:, 0:1], None, ALU.mult).then_inc(s["max_spread"], 1)

                def spread(c, b):
                    dve.wait_ge(s["repeat_psum"], c + 1)
                    dve.wait_ge(s["maxima_landed"], c + 1)
                    nc.vector.tensor_copy(win_max[b][:], p_repeat).then_inc(s["maxima_ready"], 1)
                    dve.wait_ge(s["maxima_ready"], c + 1)
                    link.add(nc.vector.tensor_copy(m.all_max[:, bass.ds(c, 1), :], win_max[b][:].unsqueeze(1)))

                def shift(c, b):
                    dve.wait_ge(s["shift_psum"], c + 1 + 2)
                    link.add(tt(ex_in[:], score[b % 2][:], p_shift.rearrange("p (t h) -> p t h", h=H), ALU.subtract))
                    link.wait()
                    ts(ex_in[:], ex_in[:], 0.0, None, ALU.min).then_inc(s["shifted"], 1)

                def attend(c, b):
                    zz = z[b % 2]
                    dve.wait_ge(s["values_ready"], 3 * c + 3)
                    link.add(ts(zz[:, :, 0:S], zz[:, :, 0:S], 0.5, 0.5, ALU.mult, ALU.add))
                    link.add(ts(gate[b % 2][:], gate[b % 2][:], 0.5, 0.5, ALU.mult, ALU.add))
                    link.wait()
                    link.add(tt(zz[:, :, S:D].rearrange("p t (d c) -> p t d c", d=3), vv[b % 2][:],
                            gate[b % 2][:].unsqueeze(2).to_broadcast([P, TPC, 3, V]), ALU.mult))
                    dve.wait_ge(s["exp_ready"], c + 1)
                    link.add(tt(ye[:], ex[b % 2][:].unsqueeze(3).to_broadcast([P, TPC, H, 4]),
                            y_of(c)[:, :, 0:4].unsqueeze(2).to_broadcast([P, TPC, H, 4]), ALU.mult))
                    link.wait()
                    tt(attended[b % 2][:], ye[:].rearrange("p t h k -> p t (h k)").unsqueeze(3).to_broadcast([P, TPC, 16, WS]),
                       onehot[b % 2][:].unsqueeze(2).to_broadcast([P, TPC, 16, WS]), ALU.mult).then_inc(s["attended_ready"], 1)

                nc.vector.memset(x[:, :, 3, 96:P], 0.0)
                dve.sem_inc(s["products_ready"], NB)
                dve.sem_inc(s["dst_added"], 1)
                find(0, 0)
                message(0, 0, 0)
                outer(0)
                cross(0)
                weigh(0)
                link.start()
                with dve.Fori(0, ITERS) as i:
                    for b in range(NB):
                        c = i * NB + b
                        nb, ni = (b + 1, i) if b + 1 < NB else (0, i + 1)
                        link.turn(c, NV)
                        find(c + 1, b + 1)
                        scores(c, b)
                        message(c + 1, ni, nb)
                        maxima(c)
                        outer(c + 1)
                        spread(c, b)
                        cross(c + 1)
                        shift(c, b)
                        weigh(c + 1)
                        attend(c, b)
                        link.end()

            @block.tensor
            def _(pe):
                turn, mm = nc.tensor.transpose, nc.tensor.matmul

                def turn_onehot(c, b):
                    pe.wait_ge(s["onehot_ready"], c + 1)
                    pe.sem_inc(s["turns_pe"], 1)
                    for t in range(TPC):
                        last = turn(p_onehotT[:, t * P:(t + 1) * P], onehot[b % 2][:, t, :], m.ident[:])
                    last.then_inc(s["onehotT_psum"], 1)

                def dst_part(c, i, b, half):
                    if half == 0:
                        pe.wait_ge(s["onehotT_ready"], c + 1)
                        pe.wait_ge(gathered[b % NB], (i + 1) * 16 * 5)
                    pe.wait_ge(s["dst_added"], 2 * c + half + 1)
                    for j in range(2):
                        t = 2 * half + j
                        last = mm(p_dst[:, j * D:(j + 1) * D], onehotT[b % 2][:, t * P:(t + 1) * P], dst_win[b % NB][:],
                                  start=True, stop=True)
                    last.then_inc(s["dst_psum"], 1)

                def weights(c, i, b):
                    pe.wait_ge(scal_loaded[b % NB], (i + 1) * 16)
                    pe.wait_ge(s["products_ready"], c + NB)
                    for t in range(TPC):
                        last = mm(p_w[:, t, 0:224], scal[b % NB][:, t * P:(t + 1) * P], m.rbf[:], start=True, stop=True)
                    last.then_inc(s["weights_psum"], 1)

                def values(c, b, first=False):
                    pe.wait_ge(s["products_ready"], c + 1 + NB)
                    if not first:
                        pe.wait_ge(s["max_taken"], c)
                        pe.wait_ge(s["values_ready"], 3 * c)

                    def turn_tile(t):
                        for j in range(4):
                            last = turn(p_turn[:, j * P:(j + 1) * P], x[:, t, j, :], m.ident[:])
                        last.then_inc(s["turned"], 1)

                    turn_tile(0)
                    for t in range(TPC):
                        pe.wait_ge(s["turned_copied"], c * TPC + t + 1)
                        if t + 1 < TPC:
                            turn_tile(t + 1)
                        xt = xT[t % 2]
                        mm(p_val[:, t, 0:D], xt[:, 3 * P:4 * P], m.att[:], start=True, stop=True)
                        for d in range(3):
                            last = mm(p_val[:, t, D + d * V:D + (d + 1) * V], xt[:, d * P:(d + 1) * P], m.val_v[:],
                                      start=True, stop=True)
                        last.then_inc(s["values_psum"], 1)

                def turn_mask(c):
                    pe.wait_ge(s["mask_ready"], c + 1)
                    pe.wait_ge(s["onehotT_ready"], c + 2)
                    for t in range(TPC):
                        last = turn(p_turn[:, t * P:(t + 1) * P], masked[:, t, :, :].rearrange("p h n -> p (h n)"), m.ident[:])
                    last.then_inc(s["mask_psum"], 1)

                def repeat(c):
                    pe.wait_ge(s["max_spread"], c + 1)
                    mm(p_repeat, m.repeat[:], by_head[:], start=True, stop=True).then_inc(s["repeat_psum"], 1)

                def shifts(c, b):
                    pe.wait_ge(s["maxima_ready"], c + 1)
                    for t in range(TPC):
                        last = mm(p_shift[:, t * H:(t + 1) * H], onehotT[b % 2][:, t * P:(t + 1) * P],
                                  win_max[b][0:WS, :], start=True, stop=True)
                    last.then_inc(s["shift_psum"], 1)

                def sums(c, b):
                    pe.wait_ge(s["attended_ready"], c + 1)
                    pe.wait_ge(s["staged"], c + 1)
                    for h in range(H):
                        to = (p_a if h < 2 else p_b)[:, (h % 2) * D:(h % 2 + 1) * D]
                        for t in range(TPC):
                            mm(to, attended[b % 2][:, t, 4 * h:4 * h + 4, :].rearrange("p k n -> p (k n)"),
                               z[b % 2][:, t, :], start=(t == 0), stop=(t == TPC - 1))
                    for t in range(TPC):
                        last = mm(p_den, onehot[b % 2][:, t, :], ex[b % 2][:, t, :], start=(t == 0), stop=(t == TPC - 1))
                    last.then_inc(s["summed"], 1)

                pe.sem_inc(s["summed"], 2)
                pe.sem_inc(s["shift_psum"], 2)
                pe.sem_inc(s["values_psum"], 2)
                turn_onehot(0, 0)
                dst_part(0, 0, 0, 0)
                dst_part(0, 0, 0, 1)
                weights(0, 0, 0)
                values(0, 0, first=True)
                with pe.Fori(0, ITERS) as i:
                    for b in range(NB):
                        c = i * NB + b
                        ni = i if b + 1 < NB else i + 1
                        turn_onehot(c + 1, b + 1)
                        turn_mask(c)
                        dst_part(c + 1, ni, b + 1, 0)
                        dst_part(c + 1, ni, b + 1, 1)
                        weights(c + 1, ni, b + 1)
                        repeat(c)
                        shifts(c, b)
                        values(c + 1, b + 1)
                        sums(c, b)
    phase_end(nc, m)


def attention_maximum_phase(nc, m):
    s = names(m, "piece0 piece1 reduced stored")
    PIECES = 4
    per = CH // PIECES
    with ExitStack() as ctx:
        sb = lambda name, shape: ctx.enter_context(nc.sbuf_tensor(m.tag + "am_" + name, shape, F32))
        piece = [sb(f"piece{b}", [P, per, NT * H]) for b in range(2)]
        best, top = sb("best", [P, PIECES, NT * H]), sb("top", [P, NT * H])
        loaded = [s["piece0"], s["piece1"]]
        with nc.Block() as block:
            @block.sync
            def _(sp):
                by_chunk = m.maxima.rearrange("(c p t) h -> p c (t h)", p=P, t=NT)
                for n in range(PIECES):
                    if n >= 2:
                        sp.wait_ge(s["reduced"], n - 1)
                    sp.dma_start(piece[n % 2][:], by_chunk[:, n * per:(n + 1) * per, :]).then_inc(loaded[n % 2], 16)
                sp.wait_ge(s["reduced"], PIECES + 1)
                sp.dma_start(m.amax.rearrange("(p t) h -> p (t h)", t=NT), top[:]).then_inc(s["stored"], 16)
                sp.wait_ge(s["stored"], 16)

            @block.vector
            def _(dve):
                for n in range(PIECES):
                    dve.wait_ge(loaded[n % 2], 16 * (n // 2 + 1))
                    nc.vector.tensor_reduce(best[:, n, :], piece[n % 2][:].rearrange("p c x -> p x c"), AX.X,
                                            ALU.max).then_inc(s["reduced"], 1)
                dve.wait_ge(s["reduced"], PIECES)
                nc.vector.tensor_reduce(top[:], best[:].rearrange("p n x -> p x n"), AX.X, ALU.max).then_inc(s["reduced"], 1)
    phase_end(nc, m)


def attention_add_phase(nc, m):
    s = names(m, "win_ready row_ready turns diffed shifted exp_ready scaled_ready landed l0 l1 l2 l3",
              "g0 g1 g2 g3 s0 s1 s2 s3")
    gathered, scattered = [s["g0"], s["g1"], s["g2"], s["g3"]], [s["s0"], s["s1"], s["s2"], s["s3"]]
    loaded = [s["l0"], s["l1"], s["l2"], s["l3"]]
    with ExitStack() as ctx:
        sb = lambda name, shape, dt=F32: [ctx.enter_context(nc.sbuf_tensor(m.tag + f"aa_{name}{b}", shape, dt)) for b in range(NB)]
        win_col, row_col = sb("win", [P, 1], I32), sb("row", [P, 1], I32)
        raw, scaled = sb("raw", [P, ROW0]), sb("scaled", [P, ROW0])
        top, diff, factor = sb("top", [P, H]), sb("diff", [P, H]), sb("factor", [P, H])
        with nc.Block() as block:
            @block.sync
            def _(sp):
                def load(c, b):
                    sp.dma_start(raw[b][:], m.chunk_sums[bass.ds(c, 1), :, :].rearrange("o p f -> p (o f)")
                                 ).then_inc(loaded[b], 16)

                for b in range(NB):
                    load(b, b)
                with sp.Fori(0, ITERS - 1) as i:
                    for b in range(NB):
                        sp.wait_ge(s["scaled_ready"], (i * NB + b + 1) * 2 + 2 * NB)
                        load((i + 1) * NB + b, b)

            @block.scalar
            def _(act):
                def window_column(c, b):
                    nc.scalar.copy(win_col[b][:], m.node_rows[:, bass.ds(c, 1)]).then_inc(s["win_ready"], 1)

                for b in range(NB):
                    window_column(b, b)
                with act.Fori(0, ITERS) as i:
                    for b in range(NB):
                        c = i * NB + b
                        act.wait_ge(s["landed"], c + 1)
                        nc.scalar.copy(row_col[b][:], m.window_rows[:, 0, bass.ds(c, 1)]).then_inc(s["row_ready"], 1)
                        act.wait_ge(s["shifted"], c + 1)
                        act.wait_ge(s["scaled_ready"], (c + 1) * 2)
                        nc.scalar.activation(factor[b][:], diff[b][:], ACT.Exp).then_inc(s["exp_ready"], 1)
                        act.wait_ge(gathered[b], (i + 1) * 16)
                        window_column(c + NB, b)

            @block.gpsimd
            def _(pool):
                def gather(c, b):
                    pool.wait_ge(s["win_ready"], c + 1)
                    pool.wait_ge(s["diffed"], c + 1)
                    pool.sem_inc(s["turns"], 1)
                    nc.gpsimd.indirect_dma_start(
                        out=top[b][:], out_offset=None, in_=m.amax,
                        in_offset=IndirectOffsetOnAxis(ap=win_col[b][:], axis=0)).then_inc(gathered[b], 16)

                pool.sem_inc(s["landed"], NB)
                for b in range(NB):
                    gather(b, b)
                with pool.Fori(0, ITERS) as i:
                    for b in range(NB):
                        c = i * NB + b
                        pool.wait_ge(s["scaled_ready"], (c + 1) * 2 + 2 * NB)
                        pool.wait_ge(s["row_ready"], c + 1)
                        pool.sem_inc(s["turns"], 1)
                        nc.gpsimd.indirect_dma_start(
                            out=m.att_sums, out_offset=IndirectOffsetOnAxis(ap=row_col[b][:], axis=0),
                            in_=scaled[b][:], in_offset=None, compute_op=ALU.add).then_inc(scattered[b], 16)
                        gather(c + NB, b)
                        pool.wait_ge(scattered[b], (i + 1) * 16)
                        pool.sem_inc(s["landed"], 1)
                for b in range(NB):
                    pool.wait_ge(gathered[b], (ITERS + 1) * 16)

            @block.vector
            def _(dve):
                tt = nc.vector.tensor_tensor

                def shift(c, i, b):
                    dve.wait_ge(gathered[b], (i + 1) * 16)
                    tt(diff[b][:].unsqueeze(1), m.all_max[:, bass.ds(c, 1), :], top[b][:].unsqueeze(1),
                       ALU.subtract).then_inc(s["diffed"], 1)
                    dve.wait_ge(s["diffed"], c + 1 + NB)
                    nc.vector.tensor_scalar(diff[b][:], diff[b][:], -1e4, None, ALU.max).then_inc(s["shifted"], 1)

                dve.sem_inc(s["diffed"], NB)
                dve.sem_inc(s["scaled_ready"], 2 * NB)
                shift(0, 0, 0)
                with dve.Fori(0, ITERS) as i:
                    for b in range(NB):
                        c = i * NB + b
                        shift(c + 1, *((i, b + 1) if b + 1 < NB else (i + 1, 0)))
                        dve.wait_ge(s["exp_ready"], c + 1)
                        dve.wait_ge(loaded[b], (i + 1) * 16)
                        dve.wait_ge(s["landed"], c + 1)
                        tt(scaled[b][:, 0:H * D].rearrange("p (h f) -> p h f", h=H),
                           raw[b][:, 0:H * D].rearrange("p (h f) -> p h f", h=H),
                           factor[b][:].unsqueeze(2).to_broadcast([P, H, D]), ALU.mult).then_inc(s["scaled_ready"], 1)
                        tt(scaled[b][:, H * D:ROW0], raw[b][:, H * D:ROW0], factor[b][:], ALU.mult).then_inc(s["scaled_ready"], 1)
    phase_end(nc, m)


def attention_node_phase(nc, m):
    s = names(m, "l0 l1 assembled linked turned turned_copied projected kept")
    loaded = [s["l0"], s["l1"]]
    NL, NA = 8, 5
    with ExitStack() as ctx:
        sb = lambda name, shape: [ctx.enter_context(nc.sbuf_tensor(m.tag + f"an_{name}{b}", shape, F32)) for b in range(2)]
        sums, mid = sb("sums", [P, 4, ROW0]), sb("mid", [P, H, 4, P])
        rden = sb("rden", [P, H])
        midT = sb("midT", [P, H * P])
        p_turn = [ctx.enter_context(nc.psum_tensor(m.tag + f"an_pt{b}", [P, 512], F32)) for b in range(2)]
        p_out = ctx.enter_context(nc.psum_tensor(m.tag + "an_po", [P, 512], F32))
        tt, ts = nc.vector.tensor_tensor, nc.vector.tensor_scalar

        def tiles(eng, body):
            with eng.Fori(0, NT // 2) as i:
                for b in range(2):
                    body(i * 2 + b, b, i)
            body(NT - 1, 0, NT // 2)

        with nc.Block() as block:
            @block.sync
            def _(sp):
                rows = m.att_sums.rearrange("(k p t) f -> k p t f", k=4, t=NT)

                def load(t, b, i):
                    sp.wait_ge(s["assembled"], (t + 1) * NA)
                    for k in range(4):
                        sp.dma_start(sums[b][:, k, :].unsqueeze(1), rows[k][:, bass.ds(t, 1), :]).then_inc(loaded[b], 16)
                tiles(sp, load)

            @block.vector
            def _(dve):
                def assemble(t, b, i):
                    T, M = sums[b][:, :, 0:H * D].rearrange("p k (h f) -> p h k f", h=H), mid[b]
                    v = lambda k, d: T[:, :, k, S + d * V:S + (d + 1) * V]
                    r = lambda n: rden[b][:].unsqueeze(2).to_broadcast([P, H, n])
                    r3 = lambda n: rden[b][:].unsqueeze(2).unsqueeze(3).to_broadcast([P, H, 3, n])
                    dve.wait_ge(loaded[b], (i + 1) * 64)
                    dve.wait_ge(s["turned"], t * 4 + 4)
                    ts(rden[b][:], sums[b][:, 0, H * D:ROW0], 1e-16, None, ALU.add).then_inc(s["linked"], 1)
                    for d in range(3):
                        tt(M[:, :, d, 96:P], v((d + 2) % 3, (d + 1) % 3), v((d + 1) % 3, (d + 2) % 3),
                           ALU.subtract).then_inc(s["linked"], 1)
                    tt(M[:, :, 3, S:96], v(0, 0), v(1, 1), ALU.add).then_inc(s["linked"], 1)
                    dve.wait_ge(s["linked"], t * NL + 5)
                    tt(M[:, :, 3, S:96], M[:, :, 3, S:96], v(2, 2), ALU.add).then_inc(s["linked"], 1)
                    nc.vector.reciprocal(rden[b][:], rden[b][:]).then_inc(s["linked"], 1)
                    dve.wait_ge(s["linked"], t * NL + 7)
                    for d in range(3):
                        last = tt(M[:, :, d, 0:S], T[:, :, d, 0:S], r(S), ALU.mult)
                        last.then_inc(s["assembled"], 1) if d == 2 else None
                    for d in range(3):
                        last = tt(M[:, :, d, S:96], v(3, d), r(V), ALU.mult)
                        last.then_inc(s["assembled"], 1) if d == 2 else None
                    for d in range(3):
                        last = tt(M[:, :, d, 96:P], M[:, :, d, 96:P], r(V), ALU.mult)
                        last.then_inc(s["assembled"], 1) if d == 2 else None
                    tt(M[:, :, 3, 0:S], T[:, :, 3, 0:S], r(S), ALU.mult).then_inc(s["assembled"], 1)
                    tt(M[:, :, 3, S:96], M[:, :, 3, S:96], r(V), ALU.mult).then_inc(s["linked"], 1)
                    dve.wait_ge(s["linked"], t * NL + 8)
                    dve.sem_inc(s["assembled"], 1)

                dve.sem_inc(s["assembled"], 2 * NA)
                for b in range(2):
                    nc.vector.memset(mid[b][:, :, 3, 96:P], 0.0)
                tiles(dve, assemble)
                dve.wait_ge(s["kept"], NT + 1)
                h = m.h
                nc.vector.scalar_tensor_tensor(h[:], m.x[:], 2.0, h[:], ALU.mult, ALU.add)

            @block.tensor
            def _(pe):
                def project(t, b, i):
                    pe.wait_ge(s["assembled"], (t + 1) * NA + 2 * NA)

                    def turn(j):
                        pe.wait_ge(s["turned_copied"], t * 4 + j + 1)
                        for h in range(H):
                            last = nc.tensor.transpose(p_turn[j % 2][:, h * P:(h + 1) * P], mid[b][:, h, j, :], m.ident[:])
                        last.then_inc(s["turned"], 1)

                    turn(0)
                    pe.wait_ge(s["kept"], t + 1)
                    for j in range(4):
                        if j < 3:
                            turn(j + 1)
                        pe.wait_ge(s["turned_copied"], t * 4 + j + 3)
                        to, w, n = (p_out[:, 0:S], m.out_s, S) if j == 3 else (p_out[:, S + j * V:S + (j + 1) * V], m.out_v, V)
                        for h in range(H):
                            last = nc.tensor.matmul(to, midT[j % 2][:, h * P:(h + 1) * P], w[:, h * n:(h + 1) * n],
                                                    start=(h == 0), stop=(h == H - 1))
                        last.then_inc(s["projected"], 1)

                pe.sem_inc(s["turned"], 8)
                pe.sem_inc(s["projected"], 2)
                tiles(pe, project)

            @block.scalar
            def _(act):
                def keep(t, b, i):
                    for j in range(4):
                        act.wait_ge(s["turned"], t * 4 + j + 1 + 8)
                        act.wait_ge(s["projected"], t * 4 + j + 1)
                        nc.scalar.copy(midT[j % 2][:], p_turn[j % 2][:]).then_inc(s["turned_copied"], 1)
                    act.wait_ge(s["projected"], t * 4 + 4 + 2)
                    nc.scalar.copy(m.h[:, bass.ds(t, 1), :].rearrange("p o f -> p (o f)"), p_out[:, 0:D]).then_inc(s["kept"], 1)

                act.sem_inc(s["turned_copied"], 2)
                act.sem_inc(s["kept"], 1)
                tiles(act, keep)
    phase_end(nc, m)


def attention_layer(nc, m, io, rounds):
    with ExitStack() as ctx:
        sb = lambda name, shape, dt=F32: ctx.enter_context(nc.sbuf_tensor(m.tag + "al_" + name, shape, dt))
        m.rbf, m.att, m.val_v = sb("rbf", [16, 224]), sb("att", [P, D]), sb("val_v", [P, V])
        m.alpha, m.gamma_s, m.beta_s, m.gamma_v = [sb(name, [P, n]) for name, n in
                                                    (("alpha", S), ("gamma_s", S), ("beta_s", S), ("gamma_v", V))]
        m.head_mask, m.repeat = sb("head_mask", [P, H]), sb("repeat", [P, P])
        m.out_s, m.out_v = sb("out_s", [P, H * S]), sb("out_v", [P, H * V])
        m.lin_a, m.lin_b = sb("lin_a", [P, 2 * D]), sb("lin_b", [V, 2 * D])
        m.ones = sb("ones", [P, NT])
        attention_weights_phase(nc, m, io)
        with ExitStack() as inner:
            m.xn = inner.enter_context(nc.sbuf_tensor(m.tag + "al_xn", [P, NT, D], F32))
            m.own = inner.enter_context(nc.sbuf_tensor(m.tag + "al_own", [P, NT, D], F32))
            equivariant_norm_phase(nc, m)
            node_linear_phase(nc, m, m.xn, m.ones, m.dst_table)
        m.node_rows_f, m.node_rows = sb("node_rows_f", [P, CH]), sb("node_rows", [P, CH + NB], I32)
        m.maxima_rows, m.chunk_rows = sb("maxima_rows", [P, CH + NB], I32), sb("chunk_rows", [P, CH])
        m.all_max = sb("all_max", [P, CH + NB, H])
        attention_clear_phase(nc, m, io)
        with nc.Fori(0, rounds):
            window_phase(nc, m)
            attention_window_phase(nc, m)
            attention_edge_phase(nc, m, io)
            attention_maximum_phase(nc, m)
            attention_add_phase(nc, m)
        m.h = sb("h", [P, NT, D])
        attention_node_phase(nc, m)
        layernorm_phase(nc, m)


def build(nc, io, out, layers=(0, 1, 2, 3)):
    m = Memory()
    with ExitStack() as ctx:
        sb = lambda name, shape, dt=F32: ctx.enter_context(nc.sbuf_tensor(name, shape, dt))
        m.sems = [ctx.enter_context(nc.semaphore(f"phase{n}")) for n in range(36)]
        m.dma_sems = [ctx.enter_context(nc.semaphore(f"gpsimd_dma{n}")) for n in range(20)]
        nums = [sem.num for sem in m.sems + m.dma_sems]
        assert nums == list(range(nums[0], nums[0] + len(nums)))
        m.sem_range = range(nums[0], nums[-1] + 1)
        m.dma_range = range(m.dma_sems[0].num, nums[-1] + 1)
        m.dst_i = sb("dst_i", [P, CH * TPC], I32)
        m.src = sb("src", [P, (CH + NB) * TPC], I32)
        m.dst_f = sb("dst_f", [P, CH * TPC])
        m.rel = sb("rel", [P, (CH + NB) * TPC])
        m.y = sb("y", [P, (CH + NB) * TPC * NY])
        m.ident = sb("ident", [P, P])
        m.iota = sb("iota", [P, WS])
        m.rows = sb("rows", [P, 4])
        m.attr = sb("attr", [P, NT])
        m.x = sb("x", [P, NT, D])
        m.zero = sb("zero", [P, NT * D])
        m.eps = sb("eps", [P, 1])
        m.ends = sb("ends", [P, 2 * CH])
        m.span = sb("span", [P, 2 * CH])
        m.fits = sb("fits", [P, 1])
        m.base0 = sb("base0", [P, CH])
        m.base = sb("base", [P, CH])
        m.window_rows = sb("window_rows", [P, 2, CH + NB], I32)
        m.rounds_i = sb("rounds_i", [1, 1], I32)
        m.rounds_dram = nc.dram_tensor("rounds", (1, 1), I32, kind="Internal").ap()
        m.sums = nc.dram_tensor("sums", (NY * NP, D), F32, kind="Internal").ap()
        m.by_src = [nc.dram_tensor(f"by_src{t}", (NP + P, D), F32, kind="Internal").ap() for t in range(TPC)]
        m.table = nc.dram_tensor("table", (NP, D), F32, kind="Internal").ap()
        setup_phase(nc, m, io)
        rounds = nc.values_load(m.rounds_dram, min_val=1, max_val=ROUNDS)
        if 0 in layers:
            m.tag = "L0_"
            m.dst_table = nc.dram_tensor("dst_table", (NP, D), F32, kind="Internal").ap()
            m.maxima = nc.dram_tensor("maxima", (CH * NP, H), F32, kind="Internal").ap()
            m.amax = nc.dram_tensor("amax", (NP, H), F32, kind="Internal").ap()
            m.chunk_sums = nc.dram_tensor("chunk_sums", (CH, P, ROW0), F32, kind="Internal").ap()
            m.att_sums = nc.dram_tensor("att_sums", (4 * NP, ROW0), F32, kind="Internal").ap()
            attention_layer(nc, m, io, rounds)
        if 1 in layers:
            m.tag = "L1_"
            w = Memory()
            w.K, w.fc1, w.fc2 = 8, io["L1_gnn_fc_w1"], io["L1_gnn_fc_w2"]
            w.sc_s, w.sc_v, w.lin_s, w.lin_v = io["L1_gnn_sc_w0"], io["L1_gnn_sc_w1"], io["L1_gnn_lin1_w0"], io["L1_gnn_lin1_w1"]
            w.out_s, w.out_v, w.angle = io["L1_gnn_lin2_w0"], io["L1_gnn_lin2_w1"], io["L1_gnn_lin3_w"]
            conv_layer(nc, m, io, w, io["a8"], 1.0, 0.25 * 96 ** -0.5, 0.1 * 0.25 * 96 ** -0.5, rounds)
        if 2 in layers:
            m.tag = "L2_"
            w = Memory()
            w.K, w.fc1, w.fc2 = 16, io["L2_gnn_fc_W1"], io["L2_gnn_fc_W2"]
            w.sc_s, w.sc_v, w.lin_s, w.lin_v = io["L2_gnn_W_sc0"], io["L2_gnn_W_sc1"], io["L2_gnn_W_l1_0"], io["L2_gnn_W_l1_1"]
            w.out_s, w.out_v, w.angle = io["L2_gnn_W_l2_0"], io["L2_gnn_W_l2_1"], None
            conv_layer(nc, m, io, w, io["a16"], math.sin(math.pi / 8), math.cos(math.pi / 8) * 10 ** -0.5 * 96 ** -0.5,
                       None, rounds)
        if 3 in layers:
            m.tag = "L3_"
            update_layer(nc, m, io, rounds)
        s = names(m, "stored")
        with nc.Block() as block:
            @block.sync
            def _(sp):
                sp.dma_start(out.rearrange("(p t) f -> p t f", t=NT), m.x[:]).then_inc(s["stored"], 16)
                sp.wait_ge(s["stored"], 16)


def kernel(**inputs):
    import numpy as np
    import concourse.bacc as _bacc
    from concourse import mybir as _mybir
    from concourse.bass_utils import run_bass_kernel_spmd as _run

    epad = CH * TPC * P - EDGES

    def by_edge(a, fill="edge"):
        a = np.pad(a, [(0, epad)] + [(0, 0)] * (a.ndim - 1), mode=fill)
        return np.ascontiguousarray(np.moveaxis(a.reshape(CH * TPC, P, *a.shape[1:]), 0, 1))

    def d_major(a):
        return np.concatenate([a[:, :S], a[:, S:].reshape(-1, V, 3).transpose(0, 2, 1).reshape(-1, 3 * V)], 1)

    g = {k: np.asarray(v) for k, v in inputs.items()}
    attr4 = by_edge(g["edge_attr_4"], "constant")
    valid = by_edge(np.ones((EDGES, 1), np.float32), "constant")
    n = np.arange(P)
    iota = np.where(np.arange(WS) < W, np.arange(WS), -7).astype(np.float32)
    arrays = {
        "x": np.pad(d_major(g["x"]), [(0, NP - NODES), (0, 0)]),
        "attr": np.pad(g["node_vec1"][:, 0], (0, NP - NODES)).reshape(P, NT),
        "src": np.pad(by_edge(g["src"]), [(0, 0), (0, NB * TPC)]),
        "dst": by_edge(g["dst"]),
        "y": np.pad(np.concatenate([attr4[:, :, 1:4], attr4[:, :, 0:1], valid], 2), [(0, 0), (0, NB * TPC), (0, 0)]).reshape(P, -1),
        "a8": np.pad(g["edge_attr_8"].T, [(0, 0), (0, epad + NB * TPC * P)]),
        "a16": np.pad(g["edge_attr_16"].T, [(0, 0), (0, epad + NB * TPC * P)]),
        "ident": np.eye(P, dtype=np.float32),
        "lower": np.tril(np.ones((P, P), np.float32), -1),
        "src_rows": np.pad(g["src"], (0, epad + NB * TPC * P), mode="edge").reshape(CH + NB, TPC * P),
        "iota": np.tile(iota, (P, 1)),
        "rows": np.stack([n // WS * NP + n % WS, np.minimum(n // W, NY - 1) * NP + n % W, NP + n, n % WS], 1).astype(np.float32),
    }
    arrays.update({k: v for k, v in g.items() if k.startswith("L")})
    for k in ("wm000", "wm011", "wm101", "wm110", "wu000", "wu011", "wu110"):
        arrays["L3_gnn_" + k] = g["L3_gnn_" + k].reshape(g["L3_gnn_" + k].shape[0], -1)
    arrays["L3_gnn_wu101"] = g["L3_gnn_wu101"].transpose(1, 0, 2).reshape(S, -1)
    L0 = lambda k: g["L0_gnn_" + k]
    by_head = lambda a, n: a.reshape(a.shape[0], H, n)
    row = lambda a: np.tile(a.reshape(1, -1), (P, 1))
    arrays.update({
        "alpha_rows": row(L0("alpha_dot")), "gamma_s_rows": row(L0("gamma_s")), "beta_s_rows": row(L0("beta_s")),
        "gamma_v_rows": row(L0("gamma_v")),
        "head_mask": (n[:, None] // WS == np.arange(H)).astype(np.float32),
        "repeat": (n[:, None] % WS == n % WS).astype(np.float32),
        "chunk_rows": row(np.arange(CH) * NP).astype(np.float32),
        "valT": L0("Ws_val").T,
        "slT": by_head(L0("Ws_vlin"), AS).transpose(2, 1, 0).reshape(AS, -1),
        "ps_w": L0("Wps").reshape(H, AS, S).transpose(1, 0, 2).reshape(AS, -1),
        "vlT": by_head(L0("Wv_vlin"), AV).transpose(2, 1, 0).reshape(AV, -1),
        "pv_w": L0("Wpv").reshape(H, AV, V).transpose(1, 0, 2).reshape(AV, -1),
    })
    arrays.update({k: L0(k).reshape(-1, 1) for k in ("w2_ss", "w2_sv", "w2_vs", "w2_vv0", "w2_vv1")})
    nc = _bacc.Bacc("TRN2", target_bir_lowering=False, num_devices=1)
    arrays = {k: np.ascontiguousarray(v) for k, v in arrays.items()}
    io = {
        k: nc.dram_tensor(f"in_{k}", v.shape, _mybir.dt.from_np(v.dtype), kind="ExternalInput").ap()
        for k, v in arrays.items()}
    out = nc.dram_tensor("out", (NP, D), F32, kind="ExternalOutput").ap()
    build(nc, io, out, LAYERS)
    r = _run(nc, [{f"in_{k}": v for k, v in arrays.items()}], core_ids=[0]).results[0]["out"]
    r = r[:NODES]
    return np.concatenate([r[:, :S], r[:, S:].reshape(-1, 3, V).transpose(0, 2, 1).reshape(-1, 3 * V)], 1)
```

```python
import math
from contextlib import ExitStack

import concourse.bass as bass
from concourse import mybir
from concourse.bass import IndirectOffsetOnAxis

F32 = mybir.dt.float32
I32 = mybir.dt.int32
ALU = mybir.AluOpType
ACT = mybir.ActivationFunctionType
AX = mybir.AxisListType
RMAX = bass.bass_isa.ReduceOp.max
ALL_ENGINES = [mybir.EngineType.Pool, mybir.EngineType.Activation, mybir.EngineType.PE,
               mybir.EngineType.DVE, mybir.EngineType.SP]

P = 128
NODES, EDGES = 3125, 100000
NT = -(-NODES // P)
NP = NT * P
TPC = 4
CH = -(-EDGES // (TPC * P))
W = 24
WS = 32
ROUNDS = -(-NODES // W)
S, V = 64, 32
D = S + 3 * V
NY = 5
EPS = 1e-5
PI = 3.1415925
NB = 4
ITERS = CH // NB
LAYERS = (0, 1, 2, 3)


def names(m, text, gpsimd_dmas=""):
    text, dmas = text.split(), gpsimd_dmas.split()
    assert len(text) <= len(m.sems) and len(dmas) <= len(m.dma_sems)
    return dict(list(zip(text, m.sems)) + list(zip(dmas, m.dma_sems)))


def linker(eng, sem):
    count = [0]

    def link(ins):
        count[0] += 1
        ins.then_inc(sem, 1)
        eng.wait_ge(sem, count[0])
    return link


def phase_end(nc, m):
    nc.gpsimd.dma_reset(m.dma_range)
    nc.all_engine_barrier(sems_to_clear=m.sem_range)


def setup_phase(nc, m, io):
    s = names(m, "loaded stored rounds_made ends_ready spans_ready linked")
    with nc.Block() as block:
        @block.sync
        def _(sp):
            loads = [(m.dst_i[:], io["dst"]), (m.y[:], io["y"]), (m.ident[:], io["ident"]), (m.iota[:], io["iota"]),
                     (m.rows[:], io["rows"]), (m.x[:], io["x"].rearrange("(p t) f -> p t f", t=NT)),
                     (m.attr[:], io["attr"]), (m.src[:], io["src"])]
            for to, what in loads:
                sp.dma_start(to, what).then_inc(s["loaded"], 16)
            sp.wait_ge(s["loaded"], 16 * len(loads))
            sp.wait_ge(s["rounds_made"], 1)
            sp.dma_start(m.rounds_dram, m.rounds_i[:]).then_inc(s["stored"], 16)
            sp.wait_ge(s["stored"], 16)

        @block.gpsimd
        def _(pool):
            pool.wait_ge(s["ends_ready"], 2)
            nc.gpsimd.partition_all_reduce(m.span[:], m.ends[:], P, RMAX).then_inc(s["spans_ready"], 1)

        @block.vector
        def _(dve):
            link = linker(dve, s["linked"])
            nc.vector.memset(m.zero[:], 0.0)
            nc.vector.memset(m.eps[:], EPS)
            nc.vector.memset(m.window_rows[:], 0)
            nc.vector.memset(m.rel[:], -1.0)
            dve.wait_ge(s["loaded"], 16 * 8)
            link(nc.vector.tensor_copy(m.dst_f[:], m.dst_i[:]))
            by_chunk = m.dst_f[:].rearrange("p (c t) -> p c t", t=TPC)
            nc.vector.tensor_reduce(m.ends[:, 0:CH], by_chunk, AX.X, ALU.min, negate=True).then_inc(s["ends_ready"], 1)
            nc.vector.tensor_reduce(m.ends[:, CH:2 * CH], by_chunk, AX.X, ALU.max).then_inc(s["ends_ready"], 1)
            dve.wait_ge(s["ends_ready"], 2)
            nc.vector.scalar_tensor_tensor(
                m.dst_f[:].unsqueeze(2), m.y[:, 0:CH * TPC * NY].rearrange("p (n k) -> p n k", k=NY)[:, :, NY - 1:NY],
                1e4, m.dst_f[:].unsqueeze(2), ALU.mult, ALU.add).then_inc(s["ends_ready"], 1)
            dve.wait_ge(s["ends_ready"], 3)
            nc.vector.tensor_scalar(m.dst_f[:], m.dst_f[:], -1e4, None, ALU.add)
            dve.wait_ge(s["spans_ready"], 1)
            link(nc.vector.tensor_tensor(m.ends[:, 0:CH], m.span[:, 0:CH], m.span[:, CH:2 * CH], ALU.add))
            link(nc.vector.tensor_reduce(m.fits[:], m.ends[:, 0:CH], AX.X, ALU.max))
            link(nc.vector.tensor_scalar(m.fits[:], m.fits[:], float(W - 1), None, ALU.is_le))
            nc.vector.tensor_scalar(m.base0[:], m.span[:, 0:CH], m.fits[:, 0:1], -1.0, ALU.mult, ALU.mult)
            nc.vector.tensor_scalar(m.rounds_i[:], m.fits[0:1, :], float(1 - ROUNDS), float(ROUNDS),
                                    ALU.mult, ALU.add).then_inc(s["rounds_made"], 1)
    phase_end(nc, m)


def window_phase(nc, m):
    s = names(m, "used")
    with nc.Block() as block:
        @block.vector
        def _(dve):
            rel = m.rel[:, 0:CH * TPC].rearrange("p (c t) -> p c t", t=TPC)
            dst = m.dst_f[:].rearrange("p (c t) -> p c t", t=TPC)
            nc.vector.tensor_tensor(rel, dst, m.base[:].unsqueeze(2).to_broadcast([P, CH, TPC]),
                                    ALU.subtract).then_inc(s["used"], 1)
            for j in range(2):
                nc.vector.tensor_scalar(m.window_rows[:, j, 0:CH], m.base[:], m.rows[:, j:j + 1], None,
                                        ALU.add).then_inc(s["used"], 1)
            dve.wait_ge(s["used"], 3)
            nc.vector.tensor_scalar(m.base[:], m.base[:], float(W), None, ALU.add)
    phase_end(nc, m)


def clear_phase(nc, m, rows):
    s = names(m, "cleared")
    with nc.Block() as block:
        @block.sync
        def _(sp):
            for k in range(rows):
                sp.dma_start(m.sums[k * NP:(k + 1) * NP, :].rearrange("(p t) f -> p (t f)", t=NT),
                             m.zero[:]).then_inc(s["cleared"], 16)
            sp.wait_ge(s["cleared"], 16 * rows)

        @block.vector
        def _(dve):
            nc.vector.tensor_copy(m.base[:], m.base0[:])
    phase_end(nc, m)


def edge_phase(nc, m, table, fc=None):
    NK, WN = (4, WS) if fc else (NY, W)
    KW = NK * WN
    WIDE = 2 * D if fc else D
    which = 0 if fc else 1
    s = names(m, "cols_ready landed turns summed acc_free partial_ready "
                 "onehot_ready weighted_ready scal0 scal1 scal2 scal3 hidden_psum hidden_ready weights_psum "
                 "messages_ready weights_free", "g0 g1 g2 g3 s0 s1 s2 s3")
    gathered, scattered = [s["g0"], s["g1"], s["g2"], s["g3"]], [s["s0"], s["s1"], s["s2"], s["s3"]]
    scal_loaded = [s["scal0"], s["scal1"], s["scal2"], s["scal3"]]
    with ExitStack() as ctx:
        sb = lambda name, shape, dt=F32, n=NB: [ctx.enter_context(nc.sbuf_tensor(m.tag + f"e_{name}{b}", shape, dt))
                                                for b in range(n)]
        ps = lambda name, shape, n: [ctx.enter_context(nc.psum_tensor(m.tag + f"e_{name}{b}", shape, F32)) for b in range(n)]
        src_cols = sb("src_cols", [P, TPC], I32)
        sum_rows = sb("sum_rows", [P, 1], I32)
        xj = sb("xj", [P, TPC, D])
        onehot = sb("onehot", [P, TPC, WN])
        weighted = sb("weighted", [P, TPC, NK, WN])
        partial = sb("partial", [P, D])
        acc = ps("acc", [P, 512], 2)
        if fc:
            scal_dram, K, w1, w2 = fc
            scal = sb("scal", [K, TPC * P])
            hidden = sb("hidden", [S, TPC * P], n=2)
            message = sb("message", [P, TPC, 2, D], n=2)
            hid_ps = ps("hid", [S, TPC * P], 2)
            wgt_ps = ps("wgt", [P, TPC, 256], 2)
        with nc.Block() as block:
            if fc:
                @block.sync
                def _(sp):
                    def load(c, b):
                        sp.dma_start(scal[b][:], scal_dram[:, bass.ds(c * TPC * P, TPC * P)]).then_inc(scal_loaded[b], 16)

                    for b in range(NB):
                        load(b, b)
                    with sp.Fori(0, ITERS) as i:
                        for b in range(NB):
                            sp.wait_ge(s["hidden_psum"], i * NB + b + 1)
                            load((i + 1) * NB + b, b)
                    for b in range(NB):
                        sp.wait_ge(scal_loaded[b], (ITERS + 1) * 16)

            @block.scalar
            def _(act):
                def columns(c, b):
                    nc.scalar.copy(src_cols[b][:], m.src[:, bass.ds(c * TPC, TPC)]).then_inc(s["cols_ready"], 1)

                def hide(c, b):
                    act.wait_ge(s["hidden_psum"], c + 1)
                    act.wait_ge(s["weights_psum"], c + 1)
                    nc.scalar.activation(hidden[b % 2][:], hid_ps[b % 2][:], ACT.Silu,
                                         scale=K ** -0.5).then_inc(s["hidden_ready"], 1)

                act.sem_inc(s["acc_free"], 2)
                for b in range(NB):
                    columns(b, b)
                if fc:
                    hide(0, 0)
                with act.Fori(0, ITERS) as i:
                    for b in range(NB):
                        c = i * NB + b
                        if fc:
                            hide(c + 1, b + 1)
                        act.wait_ge(s["summed"], c + 1 + NB)
                        act.wait_ge(s["landed"], c + 1)
                        nc.scalar.copy(sum_rows[b][:], m.window_rows[:, which, bass.ds(c, 1)]).then_inc(s["partial_ready"], 1)
                        if fc:
                            nc.scalar.copy(partial[b][0:96, :], acc[b % 2][0:96, D:2 * D]).then_inc(s["partial_ready"], 1)
                            nc.scalar.copy(partial[b][96:P, :], acc[b % 2][96:P, 0:D]).then_inc(s["partial_ready"], 1)
                        else:
                            nc.scalar.copy(partial[b][0:KW, :], acc[b % 2][0:KW, 0:D]).then_inc(s["partial_ready"], 2)
                        act.wait_ge(s["partial_ready"], (c + 1) * 3)
                        act.sem_inc(s["acc_free"], 1)
                        act.wait_ge(gathered[b], (i + 1) * 16 * TPC)
                        columns(c + NB, b)

            @block.gpsimd
            def _(pool):
                def gather(c, b):
                    pool.wait_ge(s["cols_ready"], c + 1)
                    pool.wait_ge(s["summed"], c + 1)
                    pool.sem_inc(s["turns"], 1)
                    for t in range(TPC):
                        nc.gpsimd.indirect_dma_start(
                            out=xj[b][:, t, :], out_offset=None, in_=table,
                            in_offset=IndirectOffsetOnAxis(ap=src_cols[b][:, t:t + 1], axis=0),
                        ).then_inc(gathered[b], 16)

                def scatter(c, b):
                    pool.wait_ge(s["partial_ready"], (c + 1) * 3)
                    pool.sem_inc(s["turns"], 1)
                    nc.gpsimd.indirect_dma_start(
                        out=m.sums, out_offset=IndirectOffsetOnAxis(ap=sum_rows[b][0:KW, :], axis=0),
                        in_=partial[b][0:KW, :], in_offset=None, compute_op=ALU.add,
                    ).then_inc(scattered[b], 16)

                def landed(i, b):
                    pool.wait_ge(scattered[b], (i + 1) * 16)
                    pool.sem_inc(s["landed"], 1)

                pool.sem_inc(s["landed"], NB)
                for b in range(NB):
                    gather(b, b)
                with pool.Fori(0, ITERS - 1) as i:
                    for b in range(NB):
                        scatter(i * NB + b, b)
                        gather((i + 1) * NB + b, b)
                        landed(i, b)
                for b in range(NB):
                    scatter((ITERS - 1) * NB + b, b)
                    landed(ITERS - 1, b)

            @block.vector
            def _(dve):
                if fc:
                    dve.sem_inc(s["weights_free"], 2)
                with dve.Fori(0, ITERS) as i:
                    for b in range(NB):
                        c = i * NB + b
                        dve.wait_ge(s["summed"], c + 1)
                        nc.vector.tensor_tensor(
                            onehot[b][:], m.iota[:, 0:WN].unsqueeze(1).to_broadcast([P, TPC, WN]),
                            m.rel[:, bass.ds(c * TPC, TPC)].unsqueeze(2).to_broadcast([P, TPC, WN]),
                            ALU.is_equal).then_inc(s["onehot_ready"], 1)
                        dve.wait_ge(s["onehot_ready"], c + 1)
                        y = m.y[:, bass.ds(c * TPC * NY, TPC * NY)].rearrange("p (t k) -> p t k", k=NY)[:, :, 0:NK]
                        nc.vector.tensor_tensor(
                            weighted[b][:], onehot[b][:].unsqueeze(2).to_broadcast([P, TPC, NK, WN]),
                            y.unsqueeze(3).to_broadcast([P, TPC, NK, WN]), ALU.mult).then_inc(s["weighted_ready"], 1)
                        if fc:
                            g, w, z = xj[b], wgt_ps[b % 2], message[b % 2]
                            dve.wait_ge(gathered[b], (i + 1) * 16 * TPC)
                            dve.wait_ge(s["weights_psum"], c + 1 + 2)
                            dve.wait_ge(s["summed"], c + 1 + NB - 2)
                            nc.vector.tensor_tensor(
                                z[:, :, :, 0:S], g[:, :, 0:S].unsqueeze(2).to_broadcast([P, TPC, 2, S]),
                                w[:, :, 0:2 * S].rearrange("p t (w c) -> p t w c", w=2), ALU.mult,
                            ).then_inc(s["messages_ready"], 1)
                            for j in range(2):
                                ins = nc.vector.tensor_tensor(
                                    z[:, :, j, S:D].rearrange("p t (d c) -> p t d c", d=3),
                                    g[:, :, S:D].rearrange("p t (d c) -> p t d c", d=3),
                                    w[:, :, 2 * S + V * j:2 * S + V * j + V].unsqueeze(2).to_broadcast([P, TPC, 3, V]),
                                    ALU.mult)
                                ins.then_inc(s["messages_ready"], 1)
                            dve.wait_ge(s["messages_ready"], (c + 1) * 3)
                            dve.sem_inc(s["weights_free"], 1)

            @block.tensor
            def _(pe):
                def hide(c, i, b):
                    pe.wait_ge(scal_loaded[b], (i + 1) * 16)
                    nc.tensor.matmul(hid_ps[b % 2][:], w1, scal[b][:], start=True, stop=True).then_inc(s["hidden_psum"], 1)

                def weights(c, b):
                    pe.wait_ge(s["hidden_ready"], c + 1)
                    pe.wait_ge(s["weights_free"], c + 1)
                    for t in range(TPC):
                        mm = nc.tensor.matmul(wgt_ps[b % 2][:, t, 0:192], hidden[b % 2][:, t * P:(t + 1) * P], w2,
                                              start=True, stop=True)
                    mm.then_inc(s["weights_psum"], 1)

                pe.sem_inc(s["summed"], NB)
                if fc:
                    pe.sem_inc(s["weights_psum"], 2)
                    hide(0, 0, 0)
                    hide(1, 0, 1)
                    weights(0, 0)
                with pe.Fori(0, ITERS) as i:
                    for b in range(NB):
                        c = i * NB + b
                        if fc:
                            ib, bb = (i, b + 2) if b + 2 < NB else (i + 1, b + 2 - NB)
                            hide(c + 2, ib, bb)
                            weights(c + 1, (b + 1) % NB)
                            pe.wait_ge(s["messages_ready"], (c + 1) * 3)
                        else:
                            pe.wait_ge(gathered[b], (i + 1) * 16 * TPC)
                        pe.wait_ge(s["weighted_ready"], c + 1)
                        pe.wait_ge(s["acc_free"], c + 1)
                        for t in range(TPC):
                            moving = message[b % 2][:, t, :, :].rearrange("p w c -> p (w c)") if fc else xj[b][:, t, :]
                            mm = nc.tensor.matmul(acc[b % 2][0:KW, 0:WIDE],
                                                  weighted[b][:, t, :, :].rearrange("p k n -> p (k n)"),
                                                  moving, start=(t == 0), stop=(t == TPC - 1))
                        mm.then_inc(s["summed"], 1)
    phase_end(nc, m)


def conv_weights_phase(nc, m, w, sc_scale, mid_scale, angle_scale):
    s = names(m, "zeroed loaded scaled")
    with nc.Block() as block:
        @block.vector
        def _(dve):
            nc.vector.memset(m.lin_a[:], 0.0).then_inc(s["zeroed"], 1)
            nc.vector.memset(m.lin_b[:], 0.0).then_inc(s["zeroed"], 1)

        @block.sync
        def _(sp):
            sp.wait_ge(s["zeroed"], 2)
            loads = [(m.fc1[0:w.K, :], w.fc1), (m.fc2[:], w.fc2), (m.out_s[:, 0:S], w.out_s), (m.out_v[:], w.out_v)]
            if w.angle is not None:
                loads.append((m.out_s[:, S:S + 1], w.angle))
            for j, (ws, wv) in enumerate([(w.sc_s, w.sc_v), (w.lin_s, w.lin_v)]):
                loads += [(m.lin_a[0:S, j * D:j * D + S], ws),
                          (m.lin_a[S:S + V, j * D + S:j * D + S + V], wv),
                          (m.lin_a[S + V:P, j * D + S + V:j * D + P], wv),
                          (m.lin_b[:, j * D + P:(j + 1) * D], wv)]
            for to, what in loads:
                sp.dma_start(to, what).then_inc(s["loaded"], 16)
            m.n_loads = len(loads)

        @block.scalar
        def _(act):
            act.wait_ge(s["loaded"], 16 * m.n_loads)
            for j, c in enumerate([sc_scale, 1.0]):
                nc.scalar.mul(m.lin_a[0:S, j * D:(j + 1) * D], m.lin_a[0:S, j * D:(j + 1) * D], c * S ** -0.5)
                nc.scalar.mul(m.lin_a[S:P, j * D:(j + 1) * D], m.lin_a[S:P, j * D:(j + 1) * D], c * V ** -0.5)
                nc.scalar.mul(m.lin_b[:, j * D:(j + 1) * D], m.lin_b[:, j * D:(j + 1) * D], c * V ** -0.5)
            nc.scalar.mul(m.fc2[:], m.fc2[:], S ** -0.5)
            n = 1
            scales = [mid_scale] + ([angle_scale] if w.angle is not None else [])
            for (a, b), c in zip([(0, S), (S, S + 1)], scales):
                nc.scalar.mul(m.out_s[0:S, a:b], m.out_s[0:S, a:b], c)
                nc.scalar.mul(m.out_s[S:96, a:b], m.out_s[S:96, a:b], c * 3 ** -0.5)
            nc.scalar.mul(m.out_v[:], m.out_v[:], mid_scale)
    phase_end(nc, m)


def node_linear_phase(nc, m, source, attr, own_table=None):
    s = names(m, "x_copied turned turned_copied mapped done stored")
    with ExitStack() as ctx:
        x1 = ctx.enter_context(nc.sbuf_tensor(m.tag + "nl_x", [P, D], F32))
        xT = ctx.enter_context(nc.sbuf_tensor(m.tag + "nl_xT", [P, 2 * P], F32))
        f = ctx.enter_context(nc.sbuf_tensor(m.tag + "nl_f", [P, NT, D], F32))
        pT = ctx.enter_context(nc.psum_tensor(m.tag + "nl_pT", [P, 512], F32))
        po = ctx.enter_context(nc.psum_tensor(m.tag + "nl_po", [P, 512], F32))
        with nc.Block() as block:
            @block.scalar
            def _(act):
                with act.Fori(0, NT) as t:
                    act.wait_ge(s["turned"], 2 * t + 2)
                    nc.scalar.copy(x1[:], source[:, bass.ds(t, 1), :].rearrange("p o f -> p (o f)")).then_inc(s["x_copied"], 1)
                    act.wait_ge(s["turned"], 2 * t + 4)
                    act.wait_ge(s["mapped"], t + 1)
                    nc.scalar.copy(xT[:, 0:P], pT[:, 0:P]).then_inc(s["turned_copied"], 1)
                    nc.scalar.copy(xT[0:V, P:2 * P], pT[0:V, P:2 * P]).then_inc(s["turned_copied"], 1)

            @block.tensor
            def _(pe):
                pe.sem_inc(s["turned"], 2)
                pe.sem_inc(s["mapped"], 1)
                with pe.Fori(0, NT) as t:
                    pe.wait_ge(s["x_copied"], t + 1)
                    nc.tensor.transpose(pT[:, 0:P], x1[:, 0:P], m.ident[:]).then_inc(s["turned"], 1)
                    nc.tensor.transpose(pT[0:V, P:2 * P], x1[:, P:D], m.ident[:]).then_inc(s["turned"], 1)
                    pe.wait_ge(s["turned_copied"], 2 * t + 2)
                    pe.wait_ge(s["done"], 2 * t + 2)
                    nc.tensor.matmul(po[:, 0:2 * D], xT[:, 0:P], m.lin_a[:], start=True, stop=False)
                    nc.tensor.matmul(po[:, 0:2 * D], xT[0:V, P:2 * P], m.lin_b[:], start=False,
                                     stop=True).then_inc(s["mapped"], 1)

            @block.vector
            def _(dve):
                dve.sem_inc(s["done"], 2)
                with dve.Fori(0, NT) as t:
                    dve.wait_ge(s["mapped"], t + 2)
                    a = attr[:, bass.ds(t, 1)]
                    for j, to in enumerate([m.own, f]):
                        nc.vector.tensor_scalar(to[:, bass.ds(t, 1), :].rearrange("p o f -> p (o f)"),
                                                po[:, j * D:(j + 1) * D], a, None, ALU.mult).then_inc(s["done"], 1)

            @block.sync
            def _(sp):
                sp.wait_ge(s["done"], 2 * NT + 2)
                sp.dma_start(m.table.rearrange("(p t) f -> p t f", t=NT), f[:]).then_inc(s["stored"], 16)
                if own_table is not None:
                    sp.dma_start(own_table.rearrange("(p t) f -> p t f", t=NT), m.own[:]).then_inc(s["stored"], 16)
                sp.wait_ge(s["stored"], 32 if own_table is not None else 16)
    phase_end(nc, m)


def conv_node_phase(nc, m, with_angle):
    s = names(m, "loaded gathered_mid turned turned_copied mapped done linked waved linked2")
    with ExitStack() as ctx:
        sb = lambda name, shape: ctx.enter_context(nc.sbuf_tensor(m.tag + "cn_" + name, shape, F32))
        ps = lambda name, shape: ctx.enter_context(nc.psum_tensor(m.tag + "cn_" + name, shape, F32))
        sums = sb("sums", [P, 4, NT, D])
        mid = sb("mid", [P, 4, 96])
        midT = sb("midT", [96, 4 * P])
        pT = ps("pT", [96, 4 * P])
        po = ps("po", [P, 512])
        angle = sb("angle", [P, NT, 1])
        turn = sb("turn", [P, NT, 1])
        wave = [sb("sin", [P, NT, 1]), sb("cos", [P, NT, 1])]
        with nc.Block() as block:
            @block.sync
            def _(sp):
                for k in range(4):
                    sp.dma_start(sums[:, k, :, :], m.sums[k * NP:(k + 1) * NP, :].rearrange("(p t) f -> p t f", t=NT)
                                 ).then_inc(s["loaded"], 16)

            @block.vector
            def _(dve):
                dve.wait_ge(s["loaded"], 64)
                dve.sem_inc(s["done"], 2)
                with dve.Fori(0, NT) as t:
                    one = lambda k, a, b: sums[:, k, bass.ds(t, 1), a:b]
                    dve.wait_ge(s["turned"], t + 1)
                    dot = mid[:, 3, S:96].unsqueeze(1)
                    nc.vector.tensor_tensor(dot, one(0, S, S + V), one(1, S + V, S + 2 * V), ALU.add).then_inc(s["linked"], 1)
                    dve.wait_ge(s["linked"], 2 * t + 1)
                    nc.vector.tensor_tensor(dot, dot, one(2, S + 2 * V, D), ALU.add).then_inc(s["linked"], 1)
                    nc.vector.tensor_copy(mid[:, 3, 0:S].unsqueeze(1), one(3, 0, S)).then_inc(s["gathered_mid"], 1)
                    nc.vector.tensor_copy(mid[:, 0:3, S:96], one(3, S, D).rearrange("p o (d c) -> p (o d) c", d=3)
                                          ).then_inc(s["gathered_mid"], 1)
                    nc.vector.tensor_copy(mid[:, 0:3, 0:S].unsqueeze(2), sums[:, 0:3, bass.ds(t, 1), 0:S]
                                          ).then_inc(s["gathered_mid"], 1)
                    dve.wait_ge(s["mapped"], t + 2)
                    a = m.attr[:, bass.ds(t, 1)]
                    nc.vector.tensor_scalar(m.h[:, bass.ds(t, 1), :].rearrange("p o f -> p (o f)"), po[:, 0:D], a, None,
                                            ALU.mult).then_inc(s["done"], 1)
                    if with_angle:
                        nc.vector.tensor_scalar(angle[:, bass.ds(t, 1), :].rearrange("p o f -> p (o f)"), po[:, D:D + 1],
                                                a, None, ALU.mult).then_inc(s["done"], 1)
                    else:
                        dve.sem_inc(s["done"], 1)
                dve.wait_ge(s["done"], 2 * NT + 2)
                link = linker(dve, s["linked2"])
                tt = nc.vector.tensor_tensor
                if with_angle:
                    big, two_pi = 1.5 * 2 ** 23, 2 * math.pi
                    hi = math.floor(two_pi * 2 ** 9) / 2 ** 9
                    for j in range(2):
                        a = wave[j]
                        link(nc.vector.tensor_scalar(a[:], angle[:], 0.5 * math.pi * j, None, ALU.add))
                        link(nc.vector.tensor_scalar(turn[:], a[:], 1 / two_pi, big, ALU.mult, ALU.add))
                        link(nc.vector.tensor_scalar(turn[:], turn[:], big, None, ALU.subtract))
                        link(nc.vector.scalar_tensor_tensor(a[:], turn[:], -hi, a[:], ALU.mult, ALU.add))
                        link(nc.vector.scalar_tensor_tensor(a[:], turn[:], hi - two_pi, a[:], ALU.mult, ALU.add))
                        link(nc.vector.tensor_scalar(a[:], a[:], PI, -PI, ALU.min, ALU.max))
                    dve.wait_ge(s["waved"], 2)
                    link(tt(m.h[:], m.h[:], wave[0][:].to_broadcast([P, NT, D]), ALU.mult))
                    link(tt(m.own[:], m.own[:], wave[1][:].to_broadcast([P, NT, D]), ALU.mult))
                link(tt(m.h[:], m.h[:], m.own[:], ALU.add))
                link(tt(m.h[:], m.h[:], m.x[:], ALU.add))

            @block.scalar
            def _(act):
                with act.Fori(0, NT) as t:
                    act.wait_ge(s["turned"], t + 2)
                    act.wait_ge(s["mapped"], t + 1)
                    nc.scalar.copy(midT[:], pT[:]).then_inc(s["turned_copied"], 1)
                if with_angle:
                    act.wait_ge(s["linked2"], 12)
                    for j in range(2):
                        nc.scalar.activation(wave[j][:], wave[j][:], ACT.Sin).then_inc(s["waved"], 1)

            @block.tensor
            def _(pe):
                pe.sem_inc(s["turned"], 1)
                pe.sem_inc(s["mapped"], 1)
                with pe.Fori(0, NT) as t:
                    pe.wait_ge(s["gathered_mid"], 3 * t + 3)
                    pe.wait_ge(s["linked"], 2 * t + 2)
                    for k in range(4):
                        mm = nc.tensor.transpose(pT[:, k * P:(k + 1) * P], mid[:, k, :], m.ident[:])
                    mm.then_inc(s["turned"], 1)
                    pe.wait_ge(s["turned_copied"], t + 1)
                    pe.wait_ge(s["done"], 2 * t + 2)
                    at = lambda k: midT[:, k * P:(k + 1) * P]
                    nc.tensor.matmul(po[:, 0:S], at(3), m.out_s[:, 0:S], start=True, stop=True)
                    if with_angle:
                        nc.tensor.matmul(po[:, D:D + 1], at(3), m.out_s[:, S:S + 1], start=True, stop=True)
                    for k in range(3):
                        mm = nc.tensor.matmul(po[:, S + k * V:S + (k + 1) * V], at(k), m.out_v[:], start=True, stop=True)
                    mm.then_inc(s["mapped"], 1)
    phase_end(nc, m)


def layernorm_phase(nc, m):
    s = names(m, "linked squared rooted")
    with ExitStack() as ctx:
        sb = lambda name, shape: ctx.enter_context(nc.sbuf_tensor(m.tag + "ln_" + name, shape, F32))
        mean, var = sb("mean", [P, NT]), sb("var", [P, NT])
        square = sb("square", [P, NT, D])
        wide = lambda a: a[:].unsqueeze(2).to_broadcast([P, NT, D])
        with nc.Block() as block:
            @block.vector
            def _(dve):
                link = linker(dve, s["linked"])
                link(nc.vector.tensor_reduce(mean[:], m.h[:], AX.X, ALU.add))
                link(nc.vector.tensor_scalar(mean[:], mean[:], 1.0 / D, None, ALU.mult))
                link(nc.vector.tensor_tensor(m.h[:], m.h[:], wide(mean), ALU.subtract))
                dve.wait_ge(s["squared"], 1)
                link(nc.vector.tensor_reduce(var[:], square[:], AX.X, ALU.add))
                dve.wait_ge(s["rooted"], 1)
                link(nc.vector.reciprocal(var[:], var[:]))
                nc.vector.tensor_tensor(m.x[:], m.h[:], wide(var), ALU.mult)

            @block.scalar
            def _(act):
                act.wait_ge(s["linked"], 3)
                nc.scalar.activation(square[:], m.h[:], ACT.Square).then_inc(s["squared"], 1)
                act.wait_ge(s["linked"], 4)
                nc.scalar.activation(var[:], var[:], ACT.Sqrt, bias=m.eps[:, 0:1], scale=1.0 / D).then_inc(s["rooted"], 1)
    phase_end(nc, m)


def conv_layer(nc, m, io, w, scal, sc_scale, mid_scale, angle_scale, rounds):
    with ExitStack() as ctx:
        sb = lambda name, shape: ctx.enter_context(nc.sbuf_tensor(m.tag + "cl_" + name, shape, F32))
        m.lin_a, m.lin_b = sb("lin_a", [P, 2 * D]), sb("lin_b", [V, 2 * D])
        m.fc1, m.fc2 = sb("fc1", [16, S]), sb("fc2", [S, 192])
        m.out_s, m.out_v = sb("out_s", [96, S + 1]), sb("out_v", [96, V])
        m.own = sb("own", [P, NT, D])
        conv_weights_phase(nc, m, w, sc_scale, mid_scale, angle_scale)
        node_linear_phase(nc, m, m.x, m.attr)
        clear_phase(nc, m, 4)
        with nc.Fori(0, rounds):
            window_phase(nc, m)
            edge_phase(nc, m, m.table, (scal, w.K, m.fc1[0:w.K, :], m.fc2[:]))
        m.h = sb("h", [P, NT, D])
        conv_node_phase(nc, m, w.angle is not None)
        layernorm_phase(nc, m)


class Memory:
    pass


KX, KDIST, KONE = (3, 0, 1), 2, 4


def update_weights_phase(nc, m, io):
    s = names(m, "loaded", "g0")
    c_msg, c_u0, c_u1 = (S + V) ** -0.5, (S * S + V * V) ** -0.5, (2 * S * V) ** -0.5
    parts = [(m.ms[:, 0:S], io["L3_gnn_lm0"], S ** -0.5), (m.ms[:, S:2 * S], io["L3_gnn_wm000"], c_msg),
             (m.ms[:, 2 * S:], io["L3_gnn_wm011"], c_msg),
             (m.mv[:, 0:V], io["L3_gnn_lm1"], V ** -0.5), (m.mv[:, V:2 * V], io["L3_gnn_wm101"], c_msg),
             (m.mv[:, 2 * V:], io["L3_gnn_wm110"], c_msg * 3 ** -0.5),
             (m.u000[:], io["L3_gnn_wu000"].rearrange("(n r) w -> r n w", r=P), c_u0),
             (m.u110[:], io["L3_gnn_wu110"].rearrange("(n r) w -> r n w", r=P), c_u0 * 3 ** -0.5),
             (m.u011[:], io["L3_gnn_wu011"], c_u1), (m.u101[:], io["L3_gnn_wu101"], c_u1),
             (m.lu0[:], io["L3_gnn_lu0"], S ** -0.5), (m.lu1[:], io["L3_gnn_lu1"], V ** -0.5)]
    with nc.Block() as block:
        @block.gpsimd
        def _(pool):
            pool.dma_start(m.lower[:], io["lower"]).then_inc(s["g0"], 16)
            pool.wait_ge(s["g0"], 16)

        @block.sync
        def _(sp):
            for to, what, _ in parts:
                sp.dma_start(to, what).then_inc(s["loaded"], 16)

        @block.scalar
        def _(act):
            act.wait_ge(s["loaded"], 16 * len(parts))
            for to, _, c in parts:
                nc.scalar.mul(to, to, c)
    phase_end(nc, m)


def update_tables_phase(nc, m):
    s = names(m, "zeroed x_copied turned turned_copied mapped kept stored")
    with ExitStack() as ctx:
        sb = lambda name, shape: ctx.enter_context(nc.sbuf_tensor(m.tag + "ut_" + name, shape, F32))
        ps = lambda name: ctx.enter_context(nc.psum_tensor(m.tag + "ut_" + name, [P, 512], F32))
        tables, x1, xT = sb("tables", [P, NY, NT, D]), sb("x", [P, D]), sb("xT", [S, 4 * P])
        pT, p_s, p_v = ps("pT"), ps("s"), ps("v")
        with nc.Block() as block:
            @block.gpsimd
            def _(pool):
                nc.gpsimd.memset(tables[:], 0.0).then_inc(s["zeroed"], 1)

            @block.scalar
            def _(act):
                with act.Fori(0, NT) as t:
                    act.wait_ge(s["turned"], 2 * t + 2)
                    nc.scalar.copy(x1[:].unsqueeze(1), m.x[:, bass.ds(t, 1), :]).then_inc(s["x_copied"], 1)
                    act.wait_ge(s["turned"], 2 * t + 4)
                    act.wait_ge(s["mapped"], t + 1)
                    nc.scalar.copy(xT[:, 0:P], pT[0:S, 0:P]).then_inc(s["turned_copied"], 1)
                    nc.scalar.copy(xT[0:V, P:4 * P], pT[0:V, P:4 * P]).then_inc(s["turned_copied"], 1)

            @block.tensor
            def _(pe):
                pe.sem_inc(s["turned"], 2)
                pe.sem_inc(s["mapped"], 1)
                with pe.Fori(0, NT) as t:
                    pe.wait_ge(s["x_copied"], t + 1)
                    pe.sem_inc(s["turned"], 1)
                    nc.tensor.transpose(pT[0:S, 0:P], x1[:, 0:S], m.ident[:])
                    for d in range(3):
                        mm = nc.tensor.transpose(pT[0:V, (1 + d) * P:(2 + d) * P], x1[:, S + d * V:S + (d + 1) * V],
                                                 m.ident[:])
                    mm.then_inc(s["turned"], 1)
                    pe.wait_ge(s["turned_copied"], 2 * t + 2)
                    pe.wait_ge(s["kept"], 8 * t + 1)
                    nc.tensor.matmul(p_s[:, 0:D], xT[:, 0:P], m.ms[:], start=True, stop=True)
                    for d in range(3):
                        mm = nc.tensor.matmul(p_v[:, d * P:(d + 1) * P], xT[0:V, (1 + d) * P:(2 + d) * P], m.mv[:],
                                              start=True, stop=True)
                    mm.then_inc(s["mapped"], 1)

            @block.vector
            def _(dve):
                dve.sem_inc(s["kept"], 1)
                dve.wait_ge(s["zeroed"], 1)
                with dve.Fori(0, NT) as t:
                    dve.wait_ge(s["mapped"], t + 2)
                    for n, k in enumerate((KONE, KDIST)):
                        nc.vector.tensor_copy(tables[:, k, bass.ds(t, 1), 0:S], p_s[:, n * S:(n + 1) * S].unsqueeze(1)
                                              ).then_inc(s["kept"], 1)
                        nc.vector.tensor_copy(
                            tables[:, k, bass.ds(t, 1), S:D].rearrange("p o (d c) -> p (o d) c", d=3),
                            p_v[:, 0:3 * P].rearrange("p (d c) -> p d c", d=3)[:, :, n * V:(n + 1) * V],
                        ).then_inc(s["kept"], 1)
                    for d in range(3):
                        nc.vector.tensor_copy(tables[:, KX[d], bass.ds(t, 1), 0:S],
                                              p_v[:, d * P + 2 * V:(d + 1) * P].unsqueeze(1)).then_inc(s["kept"], 1)
                    for d in range(3):
                        ins = nc.vector.tensor_copy(tables[:, KX[d], bass.ds(t, 1), S + d * V:S + (d + 1) * V],
                                                    p_s[:, 2 * S:D].unsqueeze(1))
                        if d == 2:
                            ins.then_inc(s["kept"], 1)

            @block.sync
            def _(sp):
                sp.wait_ge(s["kept"], 8 * NT + 1)
                for k in range(NY):
                    sp.dma_start(m.sums[k * NP:(k + 1) * NP, :].rearrange("(p t) f -> p t f", t=NT),
                                 tables[:, k, :, :]).then_inc(s["stored"], 16)
                sp.wait_ge(s["stored"], 16 * NY)
    phase_end(nc, m)


def update_clear_phase(nc, m):
    s = names(m, "cleared src_made")
    with nc.Block() as block:
        @block.sync
        def _(sp):
            for t in range(TPC):
                sp.dma_start(m.by_src[t][0:NP, :].rearrange("(p t) f -> p (t f)", t=NT), m.zero[:]).then_inc(s["cleared"], 16)
                sp.dma_start(m.by_src[t][NP:NP + P, :], m.zero[:, 0:D]).then_inc(s["cleared"], 16)
            sp.wait_ge(s["cleared"], 16 * 2 * TPC)

        @block.vector
        def _(dve):
            nc.vector.tensor_copy(m.base[:], m.base0[:])
            nc.vector.tensor_copy(m.src_f[:], m.src[:, 0:CH * TPC]).then_inc(s["src_made"], 1)
            dve.wait_ge(s["src_made"], 1)
            nc.vector.tensor_scalar(m.to_spare[:], m.src_f[:], m.rows[:, 2:3], -1.0, ALU.subtract, ALU.mult)
    phase_end(nc, m)


def edge_phase_3(nc, m, io):
    KW = NY * W
    s = names(m, "rows_copied landed turns used weighted_ready same_ready row0 row1 row2 row3 mixed mixed_copied "
                 "messages_psum messages_ready chained index_ready",
              "t0 t1 t2 t3 w0 w1 w2 w3 w4 w5 w6 w7")
    row_loaded = [s["row0"], s["row1"], s["row2"], s["row3"]]
    gathered = [s["t0"], s["t1"], s["t2"], s["t3"]]
    scattered = [[s["w0"], s["w1"], s["w2"], s["w3"]], [s["w4"], s["w5"], s["w6"], s["w7"]]]
    with ExitStack() as ctx:
        sb = lambda name, shape, dt=F32, n=NB: [ctx.enter_context(nc.sbuf_tensor(m.tag + f"e3_{name}{b}", shape, dt))
                                                for b in range(n)]
        ps = lambda name, shape: [ctx.enter_context(nc.psum_tensor(m.tag + f"e3_{name}{b}", shape, F32)) for b in range(2)]
        window_rows = sb("window_rows", [P, 1], I32)
        window = sb("window", [P, D])
        src_row = sb("src_row", [P, TPC * P], I32)
        onehot = sb("onehot", [P, TPC, W], n=2)
        weighted = sb("weighted", [P, TPC, NY, W], n=2)
        same = sb("same", [P, TPC, P], n=2)
        before = sb("before", [P, TPC, P], n=1)[0]
        count, moved = sb("count", [P, TPC], n=1)[0], sb("moved", [P, TPC], n=1)[0]
        index = sb("index", [P, TPC], I32)
        mixed_sb = sb("mixed_sb", [P, TPC * P], n=2)
        message = sb("message", [P, TPC, D])
        mixed_ps = ps("mixed", [P, TPC * P])
        mess_ps = ps("mess", [P, TPC, 256])
        with nc.Block() as block:
            @block.sync
            def _(sp):
                def load(c, b):
                    sp.dma_start(src_row[b][:], io["src_rows"][bass.ds(c, 1), :].to_broadcast([P, TPC * P])
                                 ).then_inc(row_loaded[b], 16)

                for b in range(NB):
                    load(b, b)
                with sp.Fori(0, ITERS) as i:
                    for b in range(NB):
                        sp.wait_ge(s["same_ready"], i * NB + b + 1)
                        load((i + 1) * NB + b, b)
                for b in range(NB):
                    sp.wait_ge(row_loaded[b], (ITERS + 1) * 16)

            @block.scalar
            def _(act):
                def rows(c, b):
                    nc.scalar.copy(window_rows[b][:], m.window_rows[:, 1, bass.ds(c, 1)]).then_inc(s["rows_copied"], 1)

                def mixed(c, b):
                    act.wait_ge(s["mixed"], c + 1 + 2)
                    act.wait_ge(s["messages_psum"], c + 3)
                    nc.scalar.copy(mixed_sb[b % 2][0:KW, :], mixed_ps[b % 2][0:KW, :]).then_inc(s["mixed_copied"], 1)

                def messages(c, i, b):
                    act.wait_ge(s["messages_psum"], c + 1 + NB)
                    act.wait_ge(s["landed"], c + 1)
                    nc.scalar.copy(message[b][:], mess_ps[b % 2][:, :, 0:D]).then_inc(s["messages_ready"], 1)
                    act.wait_ge(gathered[b], (i + 1) * 16)
                    rows(c + NB, b)

                act.sem_inc(s["mixed_copied"], 2)
                act.sem_inc(s["messages_ready"], 2)
                for b in range(NB):
                    rows(b, b)
                mixed(0, 0)
                for b in range(1, NB):
                    mixed(b, b)
                    messages(b - 1, 0, b - 1)
                with act.Fori(1, ITERS) as i:
                    for b in range(NB):
                        mixed(i * NB + b, b)
                        messages(i * NB + b - 1, *((i, b - 1) if b else (i - 1, NB - 1)))
                messages(CH - 1, ITERS - 1, NB - 1)

            @block.gpsimd
            def _(pool):
                def gather(c, b):
                    pool.wait_ge(s["rows_copied"], c + 1)
                    pool.wait_ge(s["messages_psum"], c + 1)
                    pool.sem_inc(s["turns"], 1)
                    nc.gpsimd.indirect_dma_start(
                        out=window[b][0:KW, :], out_offset=None, in_=m.sums,
                        in_offset=IndirectOffsetOnAxis(ap=window_rows[b][0:KW, :], axis=0),
                    ).then_inc(gathered[b], 16)

                def scatter(c, b, turns_before):
                    pool.wait_ge(s["messages_ready"], c + 1 + 2)
                    pool.wait_ge(s["index_ready"], c + 1)
                    for t in range(TPC):
                        if turns_before is not None:
                            pool.wait_ge(scattered[(b + 1) % 2][t], turns_before * 16)
                        pool.sem_inc(s["turns"], 1)
                        nc.gpsimd.indirect_dma_start(
                            out=m.by_src[t], out_offset=IndirectOffsetOnAxis(ap=index[b][:, t:t + 1], axis=0),
                            in_=message[b][:, t, :], in_offset=None, compute_op=ALU.add,
                        ).then_inc(scattered[b % 2][t], 16)
                    pool.sem_inc(s["landed"], 1)

                def turn(i, first):
                    for b in range(NB):
                        before_b = (i * 2 if b == 0 else i * 2 + 1 if b in (1, 2) else i * 2 + 2)
                        scatter(i * NB + b, b, None if first and b == 0 else before_b)
                        yield b

                pool.sem_inc(s["landed"], NB - 1)
                for b in range(NB):
                    pool.wait_ge(s["rows_copied"], b + 1)
                    nc.gpsimd.indirect_dma_start(
                        out=window[b][0:KW, :], out_offset=None, in_=m.sums,
                        in_offset=IndirectOffsetOnAxis(ap=window_rows[b][0:KW, :], axis=0),
                    ).then_inc(gathered[b], 16)
                for b in turn(0, True):
                    gather(NB + b, b)
                with pool.Fori(1, ITERS - 1) as i:
                    for b in turn(i, False):
                        gather((i + 1) * NB + b, b)
                for b in turn(ITERS - 1, False):
                    pass
                for parity in range(2):
                    for t in range(TPC):
                        pool.wait_ge(scattered[parity][t], 16 * CH // 2)

            @block.vector
            def _(dve):
                with dve.Fori(0, ITERS) as i:
                    for b in range(NB):
                        c, b2 = i * NB + b, b % 2
                        dve.wait_ge(s["mixed"], c + 1)
                        nc.vector.tensor_tensor(
                            onehot[b2][:], m.iota[:, 0:W].unsqueeze(1).to_broadcast([P, TPC, W]),
                            m.rel[:, bass.ds(c * TPC, TPC)].unsqueeze(2).to_broadcast([P, TPC, W]),
                            ALU.is_equal).then_inc(s["chained"], 1)
                        dve.wait_ge(row_loaded[b], (i + 1) * 16)
                        src = m.src_f[:, bass.ds(c * TPC, TPC)]
                        nc.vector.tensor_tensor(
                            same[b2][:], src_row[b][:].rearrange("p (t e) -> p t e", t=TPC),
                            src.unsqueeze(2).to_broadcast([P, TPC, P]), ALU.is_equal).then_inc(s["same_ready"], 1)
                        dve.wait_ge(s["chained"], c * 4 + 1)
                        y = m.y[:, bass.ds(c * TPC * NY, TPC * NY)].rearrange("p (t k) -> p t k", k=NY)
                        nc.vector.tensor_tensor(
                            weighted[b2][:], onehot[b2][:].unsqueeze(2).to_broadcast([P, TPC, NY, W]),
                            y.unsqueeze(3).to_broadcast([P, TPC, NY, W]), ALU.mult).then_inc(s["weighted_ready"], 1)
                        dve.wait_ge(s["same_ready"], c + 1)
                        nc.vector.tensor_tensor(before[:], same[b2][:], m.lower[:].unsqueeze(1).to_broadcast([P, TPC, P]),
                                                ALU.mult).then_inc(s["chained"], 1)
                        dve.wait_ge(s["chained"], c * 4 + 2)
                        nc.vector.tensor_reduce(count[:], before[:], AX.X, ALU.add).then_inc(s["chained"], 1)
                        dve.wait_ge(s["chained"], c * 4 + 3)
                        nc.vector.scalar_tensor_tensor(moved[:], count[:], 0.5, m.to_spare[:, bass.ds(c * TPC, TPC)],
                                                       ALU.is_gt, ALU.mult).then_inc(s["chained"], 1)
                        dve.wait_ge(s["chained"], c * 4 + 4)
                        dve.wait_ge(s["landed"], c + 1)
                        nc.vector.tensor_tensor(index[b][:], moved[:], src, ALU.add).then_inc(s["index_ready"], 1)

            @block.tensor
            def _(pe):
                def mix(c, b):
                    pe.wait_ge(s["weighted_ready"], c + 1)
                    pe.wait_ge(s["same_ready"], c + 1)
                    pe.wait_ge(s["mixed_copied"], c + 1)
                    for t in range(TPC):
                        mm = nc.tensor.matmul(mixed_ps[b % 2][0:KW, t * P:(t + 1) * P],
                                              weighted[b % 2][:, t, :, :].rearrange("p k n -> p (k n)"),
                                              same[b % 2][:, t, :], start=True, stop=True)
                    mm.then_inc(s["mixed"], 1)

                def messages(c, i, b):
                    pe.wait_ge(s["mixed_copied"], c + 1 + 2)
                    pe.wait_ge(gathered[b], (i + 1) * 16)
                    pe.wait_ge(s["messages_ready"], c + 1)
                    for t in range(TPC):
                        mm = nc.tensor.matmul(mess_ps[b % 2][:, t, 0:D], mixed_sb[b % 2][0:KW, t * P:(t + 1) * P],
                                              window[b][0:KW, :], start=True, stop=True)
                    mm.then_inc(s["messages_psum"], 1)

                pe.sem_inc(s["mixed"], 2)
                pe.sem_inc(s["messages_psum"], NB)
                mix(0, 0)
                for b in range(1, NB):
                    mix(b, b)
                    messages(b - 1, 0, b - 1)
                with pe.Fori(1, ITERS) as i:
                    for b in range(NB):
                        mix(i * NB + b, b)
                        messages(i * NB + b - 1, *((i, b - 1) if b else (i - 1, NB - 1)))
                messages(CH - 1, ITERS - 1, NB - 1)
    phase_end(nc, m)


def update_node_phase(nc, m):
    s = names(m, "l0 l1 a_made xs_ready x_turned x_copied a_turned a_turned_copied y_psum products reduced "
                 "outer_ready turned turned_copied multiplied kept linked pe_turns")
    loaded = [s["l0"], s["l1"]]
    N0, N1 = S * S // P, V * V // P
    G, NY1 = (N0 + N1) // 4, 4
    assert NT % 2 == 1 and G % 2 == 0
    with ExitStack() as ctx:
        sb = lambda name, shape, n=2: [ctx.enter_context(nc.sbuf_tensor(m.tag + f"un_{name}{b}", shape, F32))
                                       for b in range(n)]
        ps = lambda name: ctx.enter_context(nc.psum_tensor(m.tag + "un_ps_" + name, [P, 512], F32))
        sums, xs, a = sb("sums", [P, TPC, D]), sb("xs", [P, D]), sb("a", [P, D])
        x_T, a0T = sb("x_T", [S, 4 * P]), sb("a0T", [S, P])
        q0, q1 = sb("q0", [P, S, S]), sb("q1", [P, V, V])
        qT = sb("qT", [P, 4 * P])
        halves, parts, prod1 = [sb(name, shape, 1)[0] for name, shape in
                                (("halves", [P, 2, D]), ("parts", [P, 3, V, V]), ("prod1", [P, 3, S, V]))]
        vectors = ctx.enter_context(nc.sbuf_tensor(m.tag + "un_vectors", [P, NT, 3 * V], F32))
        p_x, p_a, p_out = ps("x"), ps("a"), ps("out")
        p_y, p_t = [ps(f"y{n}") for n in range(3)], [ps(f"t{n}") for n in range(2)]
        tt = nc.vector.tensor_tensor

        def turns(eng, body):
            with eng.Fori(0, NT // 2) as i:
                body(i * 2, 0, (1, i))
                body(i * 2 + 1, 1, (0, i + 1))
            body(NT - 1, 0, None)

        with nc.Block() as block:
            @block.sync
            def _(sp):
                rows = [one[0:NP, :].rearrange("(p t) f -> p t f", t=NT) for one in m.by_src]

                def load(t, b, following):
                    sp.wait_ge(s["a_made"], t + 1)
                    for k in range(TPC):
                        sp.dma_start(sums[b][:, k, :].unsqueeze(1), rows[k][:, bass.ds(t, 1), :]).then_inc(loaded[b], 16)
                turns(sp, load)

            @block.scalar
            def _(act):
                def copy_x(t, b):
                    act.wait_ge(s["reduced"], t + 1)
                    nc.scalar.copy(xs[b][:].unsqueeze(1), m.x[:, bass.ds(t, 1), :]).then_inc(s["xs_ready"], 1)

                def copy_turned(t, b):
                    act.wait_ge(s["x_turned"], t + 1)
                    nc.scalar.copy(x_T[b][:, 0:P], p_x[0:S, 0:P]).then_inc(s["x_copied"], 1)
                    nc.scalar.copy(x_T[b][0:V, P:4 * P], p_x[0:V, P:4 * P]).then_inc(s["x_copied"], 1)
                    act.wait_ge(s["a_turned"], t + 1)
                    nc.scalar.copy(a0T[b][:], p_a[0:S, 0:P]).then_inc(s["a_turned_copied"], 1)

                def body(t, b, following):
                    if following:
                        copy_x(t + 1, following[0])
                    for n in range(G):
                        act.wait_ge(s["turned"], t * G + n + 1 + 2 * G)
                        act.wait_ge(s["multiplied"], t * G + n + 1)
                        nc.scalar.copy(qT[n % 2][:], p_t[n % 2][:]).then_inc(s["turned_copied"], 1)
                    act.wait_ge(s["multiplied"], (t + 1) * G + 2)
                    nc.scalar.copy(m.h[:, bass.ds(t, 1), :], p_out[:, 0:D].unsqueeze(1)).then_inc(s["kept"], 1)
                    if following:
                        copy_turned(t + 1, following[0])

                act.sem_inc(s["turned_copied"], 2)
                act.sem_inc(s["kept"], 1)
                copy_x(0, 0)
                copy_turned(0, 0)
                turns(act, body)

            @block.tensor
            def _(pe):
                turn, mm = nc.tensor.transpose, nc.tensor.matmul

                def turn_inputs(t, b):
                    pe.wait_ge(s["xs_ready"], t + 1)
                    pe.sem_inc(s["pe_turns"], 1)
                    turn(p_x[0:S, 0:P], xs[b][:, 0:S], m.ident[:])
                    for d in range(3):
                        last = turn(p_x[0:V, (1 + d) * P:(2 + d) * P], xs[b][:, S + d * V:S + (d + 1) * V], m.ident[:])
                    last.then_inc(s["x_turned"], 1)
                    pe.wait_ge(s["a_made"], t + 1 + 2)
                    pe.sem_inc(s["pe_turns"], 1)
                    turn(p_a[0:S, 0:P], a[b][:, 0:S], m.ident[:]).then_inc(s["a_turned"], 1)

                def for_vectors(t, b, n):
                    pe.wait_ge(s["products"], t * NY1 + (3, 1, 2, 4)[n])
                    if n == 2:
                        pe.wait_ge(s["a_turned_copied"], t + 1)
                    fixed, u = (x_T[b][:, 0:P], m.u011) if n < 2 else (a0T[b][:], m.u101)
                    mm(p_y[n % 3][:], fixed, u[:, (n % 2) * 512:(n % 2 + 1) * 512], start=True,
                       stop=True).then_inc(s["y_psum"], 1)

                def body(t, b, following):
                    pe.wait_ge(s["x_copied"], 2 * t + 2)
                    for n in range(3):
                        for_vectors(t, b, n)
                    pe.wait_ge(s["kept"], t + 1)
                    for d in range(3):
                        mm(p_out[:, S + d * V:S + (d + 1) * V], x_T[b][0:V, (d + 1) * P:(d + 2) * P], m.lu1[:],
                           start=True, stop=True)
                    mm(p_out[:, 0:S], x_T[b][:, 0:P], m.lu0[:], start=True, stop=False)

                    def turn_group(n):
                        pe.wait_ge(s["turned_copied"], t * G + n + 1)
                        if n == 0:
                            pe.wait_ge(s["outer_ready"], 2 * t + 1 + 1)
                        if n == N0 // 4:
                            pe.wait_ge(s["outer_ready"], 2 * t + 2 + 1)
                        q = q0 if n < N0 // 4 else q1
                        for k in range(4):
                            at = (4 * n + k) if q is q0 else (4 * n + k - N0)
                            flat = q[b][:].rearrange("p u v -> p (u v)")
                            last = turn(p_t[n % 2][:, k * P:(k + 1) * P], flat[:, at * P:(at + 1) * P], m.ident[:])
                        last.then_inc(s["turned"], 1)

                    turn_group(0)
                    for n in range(G):
                        if n + 1 < G:
                            turn_group(n + 1)
                        pe.wait_ge(s["turned_copied"], t * G + n + 1 + 2)
                        for k in range(4):
                            at = 4 * n + k
                            w = m.u000[:, at, :] if at < N0 else m.u110[:, at - N0, :]
                            last = mm(p_out[:, 0:S], qT[n % 2][:, k * P:(k + 1) * P], w, start=False,
                                      stop=(at == N0 + N1 - 1))
                        last.then_inc(s["multiplied"], 1)
                        if n == 1:
                            for_vectors(t, b, 3)
                    if following:
                        turn_inputs(t + 1, following[0])

                pe.sem_inc(s["turned"], 2 * G)
                pe.sem_inc(s["multiplied"], 2)
                turn_inputs(0, 0)
                turns(pe, body)

            @block.vector
            def _(dve):
                def add_up(t, b, pair):
                    dve.wait_ge(loaded[b], (pair + 1) * 16 * TPC)
                    tt(halves[:], sums[b][:, 0:2, :], sums[b][:, 2:4, :], ALU.add).then_inc(s["linked"], 1)
                    dve.wait_ge(s["linked"], 3 * t + 1)
                    tt(a[b][:], halves[:, 0, :], halves[:, 1, :], ALU.add).then_inc(s["a_made"], 1)

                def outer(t, b):
                    dve.wait_ge(s["a_made"], t + 1 + 2)
                    dve.wait_ge(s["xs_ready"], t + 1)
                    dve.wait_ge(s["turned"], t * G + G)
                    tt(q0[b][:], xs[b][:, 0:S].unsqueeze(2).to_broadcast([P, S, S]),
                       a[b][:, 0:S].unsqueeze(1).to_broadcast([P, S, S]), ALU.mult).then_inc(s["outer_ready"], 1)
                    dve.wait_ge(s["outer_ready"], 2 * t + 1)
                    v = lambda f: f[b][:, S:D].rearrange("p (d v) -> p d v", d=3)
                    tt(parts[:], v(xs).unsqueeze(3).to_broadcast([P, 3, V, V]),
                       v(a).unsqueeze(2).to_broadcast([P, 3, V, V]), ALU.mult).then_inc(s["linked"], 1)
                    dve.wait_ge(s["linked"], 3 * t + 2)
                    tt(q1[b][:], parts[:, 0], parts[:, 1], ALU.add).then_inc(s["linked"], 1)
                    dve.wait_ge(s["linked"], 3 * t + 3)
                    tt(q1[b][:], q1[b][:], parts[:, 2], ALU.add).then_inc(s["outer_ready"], 1)

                def body(t, b, following):
                    dve.wait_ge(s["reduced"], t + 2)
                    for n in range(NY1):
                        dve.wait_ge(s["y_psum"], t * NY1 + n + 1)
                        other, j = (a, n) if n < 2 else (xs, n - 2)
                        f = other[b][:, S:D].rearrange("p (d v) -> p d v", d=3)[:, :, 16 * j:16 * j + 16]
                        at = 16 * j + (0 if other is a else V)
                        tt(prod1[:, :, at:at + 16, :],
                           p_y[n % 3][:].rearrange("p (v w) -> p v w", w=V).unsqueeze(1).to_broadcast([P, 3, 16, V]),
                           f.unsqueeze(3).to_broadcast([P, 3, 16, V]), ALU.mult).then_inc(s["products"], 1)
                    if following:
                        add_up(t + 1, *following)
                        outer(t + 1, following[0])
                    dve.wait_ge(s["products"], (t + 1) * NY1 + 3)
                    nc.vector.tensor_reduce(vectors[:, bass.ds(t, 1), :].rearrange("p o (d w) -> p (o d) w", d=3),
                                            prod1[:].rearrange("p d v w -> p d w v"), AX.X, ALU.add
                                            ).then_inc(s["reduced"], 1)

                dve.sem_inc(s["products"], 3)
                dve.sem_inc(s["a_made"], 2)
                dve.sem_inc(s["reduced"], 2)
                dve.sem_inc(s["outer_ready"], 1)
                add_up(0, 0, 0)
                outer(0, 0)
                turns(dve, body)
                dve.wait_ge(s["kept"], NT + 1)
                dve.wait_ge(s["reduced"], NT + 2)
                nc.vector.scalar_tensor_tensor(m.h[:], m.x[:], 2.0, m.h[:], ALU.mult, ALU.add).then_inc(s["linked"], 1)
                dve.wait_ge(s["linked"], 3 * NT + 1)
                tt(m.h[:, :, S:D], m.h[:, :, S:D], vectors[:], ALU.add)
    phase_end(nc, m)


def update_layer(nc, m, io, rounds):
    with ExitStack() as ctx:
        sb = lambda name, shape: ctx.enter_context(nc.sbuf_tensor(m.tag + "ul_" + name, shape, F32))
        m.ms, m.mv = sb("ms", [S, D]), sb("mv", [V, P])
        m.u000, m.u110 = sb("u000", [P, S * S // P, S]), sb("u110", [P, V * V // P, S])
        m.u011, m.u101 = sb("u011", [S, V * V]), sb("u101", [S, V * V])
        m.lu0, m.lu1 = sb("lu0", [S, S]), sb("lu1", [V, V])
        with ExitStack() as inner:
            edges = lambda name, shape: inner.enter_context(nc.sbuf_tensor(m.tag + "ul_" + name, shape, F32))
            m.lower, m.src_f, m.to_spare = [edges(name, [P, n]) for name, n in
                                            (("lower", P), ("src_f", CH * TPC), ("to_spare", CH * TPC))]
            update_weights_phase(nc, m, io)
            update_tables_phase(nc, m)
            update_clear_phase(nc, m)
            with nc.Fori(0, rounds):
                window_phase(nc, m)
                edge_phase_3(nc, m, io)
        m.h = sb("h", [P, NT, D])
        update_node_phase(nc, m)
        layernorm_phase(nc, m)


H, AS, AV = 4, 16, 8
BIG = 1e30
ROW0 = H * D + H


def attention_weights_phase(nc, m, io):
    s = names(m, "zeroed loaded scaled gate_psum gate_kept head_psum head_kept")
    with ExitStack() as ctx:
        sb = lambda name, shape: ctx.enter_context(nc.sbuf_tensor(m.tag + "aw_" + name, shape, F32))
        valT, wg = sb("valT", [S, 96]), sb("wg", [S, V])
        slT, ps_w = sb("slT", [AS, H * 96]), sb("ps_w", [AS, H * S])
        vlT, pv_w = sb("vlT", [AV, H * P]), sb("pv_w", [AV, H * V])
        w2 = sb("w2", [P, 2])
        p_gate = ctx.enter_context(nc.psum_tensor(m.tag + "aw_pg", [P, 512], F32))
        p_s = ctx.enter_context(nc.psum_tensor(m.tag + "aw_ps", [P, 512], F32))
        p_v = ctx.enter_context(nc.psum_tensor(m.tag + "aw_pv", [P, 512], F32))
        loads = [(m.rbf[:, a:b], io["L0_gnn_W_rbf"][:, c:d]) for a, b, c, d in
                 ((0, 64, 0, 64), (64, 96, 160, 192), (96, 160, 64, 128), (160, 192, 128, 160), (192, 224, 192, 224))]
        loads += [(m.att[0:96, 0:S], io["L0_gnn_W_alpha"]), (m.att[0:96, S:2 * S], io["L0_gnn_Ws_val"]),
                  (m.val_v[:], io["L0_gnn_Wv_val"]), (m.alpha[:], io["alpha_rows"]),
                  (m.gamma_s[:], io["gamma_s_rows"]), (m.beta_s[:], io["beta_s_rows"]), (m.gamma_v[:], io["gamma_v_rows"]),
                  (m.head_mask[:], io["head_mask"]), (m.repeat[:], io["repeat"]),
                  (valT[:], io["valT"]), (wg[:], io["L0_gnn_Wg"]), (slT[:], io["slT"]), (ps_w[:], io["ps_w"]),
                  (vlT[:], io["vlT"]), (pv_w[:], io["pv_w"]),
                  (w2[0:S, 0:1], io["w2_ss"]), (w2[S:96, 0:1], io["w2_vv0"]),
                  (w2[0:S, 1:2], io["w2_sv"]), (w2[S:96, 1:2], io["w2_vs"]), (w2[96:P, 1:2], io["w2_vv1"])]
        for j, (ws, wv) in enumerate([(io["L0_gnn_Ws_dst"], io["L0_gnn_Wv_dst"]), (io["L0_gnn_Ws_src"], io["L0_gnn_Wv_src"])]):
            loads += [(m.lin_a[0:S, j * D:j * D + S], ws),
                      (m.lin_a[S:S + V, j * D + S:j * D + S + V], wv),
                      (m.lin_a[S + V:P, j * D + S + V:j * D + P], wv),
                      (m.lin_b[:, j * D + P:(j + 1) * D], wv)]
        with nc.Block() as block:
            @block.vector
            def _(dve):
                nc.vector.memset(m.lin_a[:], 0.0).then_inc(s["zeroed"], 1)
                nc.vector.memset(m.lin_b[:], 0.0).then_inc(s["zeroed"], 1)
                nc.vector.memset(m.att[:], 0.0).then_inc(s["zeroed"], 1)
                nc.vector.memset(m.out_s[:], 0.0).then_inc(s["zeroed"], 1)
                nc.vector.memset(w2[:], 0.0).then_inc(s["zeroed"], 1)
                nc.vector.memset(m.ones[:], 1.0)

            @block.sync
            def _(sp):
                sp.wait_ge(s["zeroed"], 5)
                for to, what in loads:
                    sp.dma_start(to, what).then_inc(s["loaded"], 16)

            @block.tensor
            def _(pe):
                pe.wait_ge(s["loaded"], 16 * len(loads))
                nc.tensor.matmul(p_gate[0:96, 0:V], valT[:], wg[:], start=True, stop=True).then_inc(s["gate_psum"], 1)
                for h in range(H):
                    nc.tensor.matmul(p_s[0:96, h * S:(h + 1) * S], slT[:, h * 96:(h + 1) * 96],
                                     ps_w[:, h * S:(h + 1) * S], start=True, stop=True)
                    mm = nc.tensor.matmul(p_v[:, h * V:(h + 1) * V], vlT[:, h * P:(h + 1) * P],
                                          pv_w[:, h * V:(h + 1) * V], start=True, stop=True)
                mm.then_inc(s["head_psum"], 1)

            @block.scalar
            def _(act):
                act.wait_ge(s["loaded"], 16 * len(loads))
                nc.scalar.mul(m.rbf[:, 64:96], m.rbf[:, 64:96], 3 ** -0.5)
                nc.scalar.mul(m.rbf[:, 192:224], m.rbf[:, 192:224], 2 ** -0.5)
                nc.scalar.mul(w2[S:96, 0:1], w2[S:96, 0:1], 3 ** -0.5).then_inc(s["scaled"], 1)
                nc.scalar.mul(w2[96:P, 1:2], w2[96:P, 1:2], 2 ** -0.5).then_inc(s["scaled"], 1)
                act.wait_ge(s["gate_psum"], 1)
                nc.scalar.copy(m.att[0:96, 2 * S:D], p_gate[0:96, 0:V])
                act.wait_ge(s["scaled"], 2)
                act.wait_ge(s["head_psum"], 1)
                nc.scalar.activation(m.out_s[0:96, :], p_s[0:96, 0:H * S], ACT.Copy, scale=w2[0:96, 0:1])
                nc.scalar.activation(m.out_v[:], p_v[:, 0:H * V], ACT.Copy, scale=w2[:, 1:2])
    phase_end(nc, m)


def equivariant_norm_phase(nc, m):
    s = names(m, "linked squared rooted vec_squared vec_rooted")
    with ExitStack() as ctx:
        sb = lambda name, shape: ctx.enter_context(nc.sbuf_tensor(m.tag + "en_" + name, shape, F32))
        mean, var, power = sb("mean", [P, NT]), sb("var", [P, NT]), sb("power", [P, NT])
        square, vsquare = sb("square", [P, NT, S]), sb("vsquare", [P, NT, 3 * V])
        wide = lambda a, n: a[:].unsqueeze(2).to_broadcast([P, NT, n])
        over = lambda a, n: a[:].unsqueeze(1).to_broadcast([P, NT, n])
        sn = m.xn[:, :, 0:S]
        with nc.Block() as block:
            @block.vector
            def _(dve):
                link = linker(dve, s["linked"])
                tt = nc.vector.tensor_tensor
                link(nc.vector.tensor_reduce(mean[:], m.x[:, :, 0:S], AX.X, ALU.add))
                link(nc.vector.tensor_scalar(mean[:], mean[:], 1.0 / S, None, ALU.mult))
                link(tt(sn, m.x[:, :, 0:S], wide(mean, S), ALU.subtract))
                dve.wait_ge(s["squared"], 1)
                link(nc.vector.tensor_reduce(var[:], square[:], AX.X, ALU.add))
                dve.wait_ge(s["vec_squared"], 1)
                link(nc.vector.tensor_reduce(power[:], vsquare[:], AX.X, ALU.add))
                dve.wait_ge(s["rooted"], 2)
                link(nc.vector.reciprocal(var[:], var[:]))
                link(nc.vector.reciprocal(power[:], power[:]))
                link(tt(sn, sn, wide(var, S), ALU.mult))
                link(tt(sn, sn, over(m.gamma_s, S), ALU.mult))
                link(tt(sn, sn, over(m.beta_s, S), ALU.add))
                for d in range(3):
                    v = slice(S + d * V, S + (d + 1) * V)
                    link(tt(m.xn[:, :, v], m.x[:, :, v], wide(power, V), ALU.mult))
                    link(tt(m.xn[:, :, v], m.xn[:, :, v], over(m.gamma_v, V), ALU.mult))

            @block.scalar
            def _(act):
                nc.scalar.activation(vsquare[:], m.x[:, :, S:D], ACT.Square).then_inc(s["vec_squared"], 1)
                act.wait_ge(s["linked"], 3)
                nc.scalar.activation(square[:], sn, ACT.Square).then_inc(s["squared"], 1)
                act.wait_ge(s["linked"], 5)
                nc.scalar.activation(var[:], var[:], ACT.Sqrt, bias=m.eps[:, 0:1], scale=1.0 / S).then_inc(s["rooted"], 1)
                nc.scalar.activation(power[:], power[:], ACT.Sqrt, bias=m.eps[:, 0:1], scale=1.0 / V).then_inc(s["rooted"], 1)
    phase_end(nc, m)


def attention_clear_phase(nc, m, io):
    s = names(m, "low_ready cleared")
    with ExitStack() as ctx:
        low = ctx.enter_context(nc.sbuf_tensor(m.tag + "ac_low", [P, NT * D], F32))
        with nc.Block() as block:
            @block.vector
            def _(dve):
                nc.vector.memset(low[:], -BIG).then_inc(s["low_ready"], 1)
                nc.vector.tensor_copy(m.base[:], m.base0[:])
                nc.vector.memset(m.node_rows[:], 0)
                nc.vector.memset(m.maxima_rows[:], 0)
                nc.vector.memset(m.all_max[:], 0.0)

            @block.sync
            def _(sp):
                sp.dma_start(m.chunk_rows[:], io["chunk_rows"]).then_inc(s["cleared"], 16)
                n = 1
                flat = m.att_sums.rearrange("r f -> (r f)").rearrange("(p x) -> p x", p=P)
                width = flat.shape[1]
                for a in range(0, width, NT * D):
                    b = min(a + NT * D, width)
                    sp.dma_start(flat[:, a:b], m.zero[:, 0:b - a]).then_inc(s["cleared"], 16)
                    n += 1
                sp.wait_ge(s["low_ready"], 1)
                flat = m.maxima.rearrange("r h -> (r h)").rearrange("(p x) -> p x", p=P)
                width = flat.shape[1]
                for a in range(0, width, NT * D):
                    b = min(a + NT * D, width)
                    sp.dma_start(flat[:, a:b], low[:, 0:b - a]).then_inc(s["cleared"], 16)
                    n += 1
                sp.wait_ge(s["cleared"], 16 * n)
    phase_end(nc, m)


def attention_window_phase(nc, m):
    s = names(m, "made")
    with nc.Block() as block:
        @block.vector
        def _(dve):
            nc.vector.tensor_scalar(m.node_rows_f[:], m.base[:], m.rows[:, 3:4], -float(W), ALU.add,
                                    ALU.add).then_inc(s["made"], 1)
            dve.wait_ge(s["made"], 1)
            nc.vector.tensor_copy(m.node_rows[:, 0:CH], m.node_rows_f[:])
            nc.vector.tensor_tensor(m.maxima_rows[:, 0:CH], m.node_rows_f[:], m.chunk_rows[:], ALU.add)
    phase_end(nc, m)


class Chain:

    def __init__(self, eng, sem):
        self.eng, self.sem, self.base, self.n = eng, sem, 0, 0

    def add(self, ins):
        self.n += 1
        ins.then_inc(self.sem, 1)

    def wait(self):
        self.eng.wait_ge(self.sem, self.base + self.n)

    def start(self):
        self.prologue = self.n

    def turn(self, c, each):
        self.base, self.n, self.each = c * each + self.prologue, 0, each

    def end(self):
        assert self.n == self.each, self.n


def attention_edge_phase(nc, m, io):
    NV = 24
    s = names(m, "cols_ready turns onehot_ready onehotT_psum onehotT_ready dst_psum dst_added weights_psum "
                 "products_ready turned turned_copied values_psum leak_ready values_ready mask_ready mask_psum "
                 "max_taken max_spread repeat_psum shift_psum shifted exp_ready attended_ready summed "
                 "staged chained scal0 scal1 scal2 scal3 stored0 stored1 maxima_ready keeping maxima_landed turns_pe",
              "g0 g1 g2 g3 w0 w1 w2 w3")
    gathered, scal_loaded = [s["g0"], s["g1"], s["g2"], s["g3"]], [s["scal0"], s["scal1"], s["scal2"], s["scal3"]]
    maxima_out, stored = [s["w0"], s["w1"], s["w2"], s["w3"]], [s["stored0"], s["stored1"]]
    with ExitStack() as ctx:
        sb = lambda name, shape, n=1, dt=F32: [ctx.enter_context(nc.sbuf_tensor(m.tag + f"ae_{name}{b}", shape, dt))
                                               for b in range(n)]
        ps = lambda name, shape: ctx.enter_context(nc.psum_tensor(m.tag + "ae_ps_" + name, shape, F32))
        src_cols, win_col, max_col = sb("src_cols", [P, TPC], NB, I32), sb("win", [P, 1], NB, I32), sb("maxc", [P, 1], NB, I32)
        xj = sb("xj", [P, TPC, D], NB)
        dst_win = sb("dst_win", [WS, D], NB)
        scal = sb("scal", [16, TPC * P], NB)
        onehot, onehotT = sb("onehot", [P, TPC, WS], NB), sb("onehotT", [WS, TPC * P], NB)
        msg, xs, tmp = sb("msg", [P, TPC, D])[0], sb("x", [P, TPC, 4, P], 2), sb("tmp", [P, TPC, 3, V])[0]
        xT = sb("xT", [P, 4 * P], 2)
        leak, leak2 = sb("leak", [P, TPC, S], 2), sb("leak2", [P, TPC, S])[0]
        score, low = sb("score", [P, TPC, H], 2), sb("low", [P, TPC, WS])[0]
        masked = sb("masked", [P, TPC, H, WS])[0]
        mx, by_head = sb("mx", [P, 1])[0], sb("by_head", [P, H])[0]
        win_max = sb("win_max", [P, H], NB)
        ex_in, ex = sb("ex_in", [P, TPC, H])[0], sb("ex", [P, TPC, H], 2)
        z, gate, vv = sb("z", [P, TPC, D], 2), sb("gate", [P, TPC, V], 2), sb("vv", [P, TPC, 3, V], 2)
        ye, attended = sb("ye", [P, TPC, H, 4])[0], sb("attended", [P, TPC, H * 4, WS], 2)
        stage = sb("stage", [P, ROW0], 2)
        p_dst, p_w, p_val = ps("dst", [P, 512]), ps("w", [P, TPC, 256]), ps("val", [P, TPC, 256])
        p_turn, p_a, p_b = ps("turn", [P, 512]), ps("a", [P, 512]), ps("b", [P, 512])
        p_onehotT, p_den, p_repeat, p_shift = p_turn[0:WS, :], p_b[0:WS, 320:324], p_dst[:, 320:324], p_dst[:, 324:340]
        tt, ts, red = nc.vector.tensor_tensor, nc.vector.tensor_scalar, nc.vector.tensor_reduce
        with nc.Block() as block:
            @block.sync
            def _(sp):
                def load(c, b):
                    sp.dma_start(scal[b][:], io["a16"][:, bass.ds(c * TPC * P, TPC * P)]).then_inc(scal_loaded[b], 16)

                def store(turn, b):
                    sp.wait_ge(s["staged"], turn + 1 + 1)
                    sp.dma_start(m.chunk_sums[bass.ds(turn, 1), :, :].rearrange("o p f -> p (o f)"),
                                 stage[b % 2][:]).then_inc(stored[b % 2], 16)

                for one in stored:
                    sp.sem_inc(one, 16)
                for b in range(NB):
                    load(b, b)
                with sp.Fori(0, ITERS) as i:
                    for b in range(NB):
                        c = i * NB + b
                        sp.wait_ge(s["weights_psum"], c + 1)
                        load(c + NB, b)
                        store(c, b)
                store(CH, 0)
                for b in range(NB):
                    sp.wait_ge(scal_loaded[b], (ITERS + 1) * 16)
                sp.wait_ge(stored[0], (ITERS * 2 + 2) * 16)
                sp.wait_ge(stored[1], (ITERS * 2 + 1) * 16)

            @block.gpsimd
            def _(pool):
                def gather(c, b):
                    pool.wait_ge(s["cols_ready"], c * 3 + 3)
                    pool.wait_ge(s["products_ready"], c + 1)
                    pool.sem_inc(s["turns"], 1)
                    nc.gpsimd.indirect_dma_start(
                        out=dst_win[b][:], out_offset=None, in_=m.dst_table,
                        in_offset=IndirectOffsetOnAxis(ap=win_col[b][0:WS, :], axis=0)).then_inc(gathered[b], 16)
                    for t in range(TPC):
                        nc.gpsimd.indirect_dma_start(
                            out=xj[b][:, t, :], out_offset=None, in_=m.table,
                            in_offset=IndirectOffsetOnAxis(ap=src_cols[b][:, t:t + 1], axis=0)).then_inc(gathered[b], 16)

                pool.sem_inc(s["maxima_landed"], NB)
                for b in range(NB):
                    gather(b, b)
                with pool.Fori(0, ITERS) as i:
                    for b in range(NB):
                        c = i * NB + b
                        pool.wait_ge(s["maxima_ready"], c + 1)
                        pool.sem_inc(s["turns"], 1)
                        nc.gpsimd.indirect_dma_start(
                            out=m.maxima, out_offset=IndirectOffsetOnAxis(ap=max_col[b][0:WS, :], axis=0),
                            in_=win_max[b][0:WS, :], in_offset=None).then_inc(maxima_out[b], 16)
                        pool.wait_ge(maxima_out[b], (i + 1) * 16)
                        pool.sem_inc(s["maxima_landed"], 1)
                        gather(c + NB, b)
                for b in range(NB):
                    pool.wait_ge(gathered[b], (ITERS + 1) * 16 * 5)

            @block.scalar
            def _(act):
                def columns(c, b):
                    nc.scalar.copy(src_cols[b][:], m.src[:, bass.ds(c * TPC, TPC)]).then_inc(s["cols_ready"], 1)
                    nc.scalar.copy(win_col[b][:], m.node_rows[:, bass.ds(c, 1)]).then_inc(s["cols_ready"], 1)
                    nc.scalar.copy(max_col[b][:], m.maxima_rows[:, bass.ds(c, 1)]).then_inc(s["cols_ready"], 1)

                def turn_onehot(c, b, first=False):
                    act.wait_ge(s["onehotT_psum"], c + 1)
                    if not first:
                        act.wait_ge(s["shift_psum"], c - 1)
                    nc.scalar.copy(onehotT[b % NB][:], p_onehotT).then_inc(s["onehotT_ready"], 1)

                def products(c, b):
                    for t in range(TPC):
                        act.wait_ge(s["turned"], c * TPC + t + 1)
                        act.wait_ge(s["values_psum"], c * TPC + t + 1)
                        nc.scalar.copy(xT[t % 2][:], p_turn[:]).then_inc(s["turned_copied"], 1)

                def values(c, b):
                    act.wait_ge(s["values_psum"], (c + 1) * TPC + 2)
                    act.wait_ge(s["summed"], c + 1)
                    nc.scalar.copy(leak[b % 2][:], p_val[:, :, 0:S]).then_inc(s["leak_ready"], 1)
                    nc.scalar.activation(z[b % 2][:, :, 0:S], p_val[:, :, S:2 * S], ACT.Tanh, scale=0.5
                                         ).then_inc(s["values_ready"], 1)
                    nc.scalar.activation(gate[b % 2][:], p_val[:, :, 2 * S:D], ACT.Tanh, scale=0.5
                                         ).then_inc(s["values_ready"], 1)
                    nc.scalar.copy(vv[b % 2][:].rearrange("p t d c -> p t (d c)"), p_val[:, :, D:256]
                                   ).then_inc(s["values_ready"], 1)

                def exponentials(c, b):
                    act.wait_ge(s["shifted"], c + 1)
                    nc.scalar.activation(ex[b % 2][:], ex_in[:], ACT.Exp).then_inc(s["exp_ready"], 1)

                def keep(c, i, b):
                    act.wait_ge(s["summed"], c + 1 + 1)
                    act.wait_ge(stored[b % 2], (i * 2 + b // 2 + 1) * 16)
                    st = stage[b % 2]
                    nc.scalar.copy(st[:, 0:2 * D], p_a[:, 0:2 * D]).then_inc(s["keeping"], 1)
                    nc.scalar.copy(st[:, 2 * D:4 * D], p_b[:, 0:2 * D]).then_inc(s["keeping"], 1)
                    nc.scalar.copy(st[0:WS, 4 * D:ROW0], p_den).then_inc(s["keeping"], 1)
                    act.wait_ge(s["keeping"], (c + 1) * 3)
                    act.sem_inc(s["staged"], 1)

                act.sem_inc(s["staged"], 1)
                for b in range(2):
                    nc.scalar.copy(stage[b][:, 4 * D:ROW0], m.zero[:, 0:H])
                for b in range(NB):
                    columns(b, b)
                turn_onehot(0, 0, first=True)
                turn_onehot(1, 1, first=True)
                products(0, 0)
                values(0, 0)
                with act.Fori(0, ITERS) as i:
                    for b in range(NB):
                        c = i * NB + b
                        turn_onehot(c + 2, b + 2)
                        exponentials(c, b)
                        products(c + 1, b + 1)
                        values(c + 1, b + 1)
                        keep(c, i, b)
                        act.wait_ge(gathered[b], (i + 1) * 16 * 5)
                        act.wait_ge(s["maxima_landed"], c + 1 + NB)
                        columns(c + NB, b)
                keep(CH, ITERS, 0)

            @block.vector
            def _(dve):
                link = Chain(dve, s["chained"])

                def y_of(c):
                    return m.y[:, bass.ds(c * TPC * NY, TPC * NY)].rearrange("p (t k) -> p t k", k=NY)

                def find(c, b, first=False):
                    if not first:
                        dve.wait_ge(s["summed"], c - 1)
                    tt(onehot[b % NB][:], m.iota[:].unsqueeze(1).to_broadcast([P, TPC, WS]),
                       m.rel[:, bass.ds(c * TPC, TPC)].unsqueeze(2).to_broadcast([P, TPC, WS]),
                       ALU.is_equal).then_inc(s["onehot_ready"], 1)

                def message(c, i, b, half):
                    dve.wait_ge(gathered[b], (i + 1) * 16 * 5)
                    dve.wait_ge(s["dst_psum"], 2 * c + half + 1)
                    tt(msg[:, 2 * half:2 * half + 2, :], xj[b][:, 2 * half:2 * half + 2, :],
                       p_dst[:, 0:2 * D].rearrange("p (t f) -> p t f", f=D), ALU.add).then_inc(s["dst_added"], 1)

                def scalars(c, b):
                    y, x = y_of(c), xs[b % 2]
                    dve.wait_ge(s["dst_added"], 2 * c + 2 + 1)
                    link.add(tt(x[:, :, 3, 0:S], msg[:, :, 0:S], y[:, :, 3:4].to_broadcast([P, TPC, S]), ALU.mult))
                    link.add(tt(tmp[:], msg[:, :, S:D].rearrange("p t (d c) -> p t d c", d=3),
                            y[:, :, 0:3].unsqueeze(3).to_broadcast([P, TPC, 3, V]), ALU.mult))
                    link.wait()
                    link.add(red(x[:, :, 3, S:96], tmp[:].rearrange("p t d c -> p t c d"), AX.X, ALU.add))

                def outer(c, b):
                    y, x = y_of(c), xs[b % 2]
                    link.add(tt(x[:, :, 0:3, 0:S], msg[:, :, 0:S].unsqueeze(2).to_broadcast([P, TPC, 3, S]),
                            y[:, :, 0:3].unsqueeze(3).to_broadcast([P, TPC, 3, S]), ALU.mult))
                    link.add(tt(x[:, :, 0:3, S:96], msg[:, :, S:D].rearrange("p t (d c) -> p t d c", d=3),
                            y[:, :, 3:4].unsqueeze(3).to_broadcast([P, TPC, 3, V]), ALU.mult))

                def cross(c, b):
                    y, x = y_of(c), xs[b % 2]
                    link.wait()
                    for d in range(3):
                        for to, v, w in ((x[:, :, d, 96:P], (d + 1) % 3, (d + 2) % 3), (tmp[:, :, d, :], (d + 2) % 3, (d + 1) % 3)):
                            link.add(tt(to, msg[:, :, S + v * V:S + (v + 1) * V],
                                    y[:, :, w:w + 1].to_broadcast([P, TPC, V]), ALU.mult))
                    link.wait()
                    link.add(tt(x[:, :, 0:3, 96:P], x[:, :, 0:3, 96:P], tmp[:], ALU.subtract))

                def weigh(c, b):
                    x = xs[b % 2]
                    link.wait()
                    dve.wait_ge(s["weights_psum"], c + 1)
                    link.add(tt(x[:, :, 0:3, :], x[:, :, 0:3, :], p_w[:, :, 96:224].unsqueeze(2).to_broadcast([P, TPC, 3, P]),
                            ALU.mult))
                    link.add(tt(x[:, :, 3, 0:96], x[:, :, 3, 0:96], p_w[:, :, 0:96], ALU.mult))
                    link.wait()
                    dve.sem_inc(s["products_ready"], 1)

                def scores(c, b):
                    dve.wait_ge(s["leak_ready"], c + 1)
                    link.add(nc.vector.scalar_tensor_tensor(leak2[:], leak[b % 2][:], 0.2, leak[b % 2][:], ALU.mult, ALU.max))
                    link.add(ts(low[:], onehot[b % NB][:], BIG, -BIG, ALU.mult, ALU.add))
                    link.wait()
                    link.add(tt(leak2[:], leak2[:], m.alpha[:].unsqueeze(1).to_broadcast([P, TPC, S]), ALU.mult))
                    link.wait()
                    link.add(red(score[b % 2][:], leak2[:].rearrange("p t (h a) -> p t h a", h=H), AX.X, ALU.add))
                    link.wait()
                    tt(masked[:], low[:].unsqueeze(2).to_broadcast([P, TPC, H, WS]),
                       score[b % 2][:].unsqueeze(3).to_broadcast([P, TPC, H, WS]), ALU.add).then_inc(s["mask_ready"], 1)

                def maxima(c):
                    dve.wait_ge(s["mask_psum"], c + 1)
                    red(mx[:], p_turn[:], AX.X, ALU.max).then_inc(s["max_taken"], 1)
                    dve.wait_ge(s["max_taken"], c + 1)
                    ts(by_head[:], m.head_mask[:], mx[:, 0:1], None, ALU.mult).then_inc(s["max_spread"], 1)

                def spread(c, b):
                    dve.wait_ge(s["repeat_psum"], c + 1)
                    dve.wait_ge(s["maxima_landed"], c + 1)
                    nc.vector.tensor_copy(win_max[b][:], p_repeat).then_inc(s["maxima_ready"], 1)
                    dve.wait_ge(s["maxima_ready"], c + 1)
                    link.add(nc.vector.tensor_copy(m.all_max[:, bass.ds(c, 1), :], win_max[b][:].unsqueeze(1)))

                def shift(c, b):
                    dve.wait_ge(s["shift_psum"], c + 1 + 2)
                    link.add(tt(ex_in[:], score[b % 2][:], p_shift.rearrange("p (t h) -> p t h", h=H), ALU.subtract))
                    link.wait()
                    ts(ex_in[:], ex_in[:], 0.0, None, ALU.min).then_inc(s["shifted"], 1)

                def attend(c, b):
                    zz = z[b % 2]
                    dve.wait_ge(s["values_ready"], 3 * c + 3)
                    link.add(ts(zz[:, :, 0:S], zz[:, :, 0:S], 0.5, 0.5, ALU.mult, ALU.add))
                    link.add(ts(gate[b % 2][:], gate[b % 2][:], 0.5, 0.5, ALU.mult, ALU.add))
                    link.wait()
                    link.add(tt(zz[:, :, S:D].rearrange("p t (d c) -> p t d c", d=3), vv[b % 2][:],
                            gate[b % 2][:].unsqueeze(2).to_broadcast([P, TPC, 3, V]), ALU.mult))
                    dve.wait_ge(s["exp_ready"], c + 1)
                    link.add(tt(ye[:], ex[b % 2][:].unsqueeze(3).to_broadcast([P, TPC, H, 4]),
                            y_of(c)[:, :, 0:4].unsqueeze(2).to_broadcast([P, TPC, H, 4]), ALU.mult))
                    link.wait()
                    tt(attended[b % 2][:], ye[:].rearrange("p t h k -> p t (h k)").unsqueeze(3).to_broadcast([P, TPC, 16, WS]),
                       onehot[b % NB][:].unsqueeze(2).to_broadcast([P, TPC, 16, WS]), ALU.mult).then_inc(s["attended_ready"], 1)

                for x in xs:
                    nc.vector.memset(x[:, :, 3, 96:P], 0.0)
                for buffer in (onehot[NB - 1], ex[1], z[1]):
                    link.add(nc.vector.memset(buffer[:], 0.0))
                nc.vector.memset(attended[1][:], 0.0).then_inc(s["attended_ready"], 1)
                dve.sem_inc(s["products_ready"], NB)
                dve.sem_inc(s["dst_added"], 1)
                find(0, 0, first=True)
                find(1, 1, first=True)
                for b in range(2):
                    message(b, 0, b, 0)
                    message(b, 0, b, 1)
                    scalars(b, b)
                    outer(b, b)
                    if b == 0:
                        cross(0, 0)
                        weigh(0, 0)
                link.start()
                with dve.Fori(0, ITERS) as i:
                    for b in range(NB):
                        c = i * NB + b
                        after_next = (c + 2, i, b + 2) if b + 2 < NB else (c + 2, i + 1, b + 2 - NB)
                        link.turn(c, NV)
                        find(c + 2, b + 2)
                        scores(c, b)
                        cross(c + 1, b + 1)
                        maxima(c)
                        weigh(c + 1, b + 1)
                        spread(c, b)
                        shift(c, b)
                        message(*after_next, 0)
                        attend(c, b)
                        message(*after_next, 1)
                        scalars(c + 2, b + 2)
                        outer(c + 2, b + 2)
                        link.end()

            @block.tensor
            def _(pe):
                turn, mm = nc.tensor.transpose, nc.tensor.matmul

                def turn_onehot(c, b, first=False):
                    pe.wait_ge(s["onehot_ready"], c + 1)
                    if not first:
                        pe.wait_ge(s["max_taken"], c - 1)
                    elif c:
                        pe.wait_ge(s["onehotT_ready"], c)
                    pe.sem_inc(s["turns_pe"], 1)
                    for t in range(TPC):
                        last = turn(p_onehotT[:, t * P:(t + 1) * P], onehot[b % NB][:, t, :], m.ident[:])
                    last.then_inc(s["onehotT_psum"], 1)

                def dst_part(c, i, b, half, first=False):
                    if half == 0:
                        pe.wait_ge(s["onehotT_ready"], c + 1)
                        pe.wait_ge(gathered[b % NB], (i + 1) * 16 * 5)
                        if not first:
                            pe.wait_ge(s["shifted"], c - 1)
                    pe.wait_ge(s["dst_added"], 2 * c + half + 1)
                    for j in range(2):
                        t = 2 * half + j
                        last = mm(p_dst[:, j * D:(j + 1) * D], onehotT[b % NB][:, t * P:(t + 1) * P], dst_win[b % NB][:],
                                  start=True, stop=True)
                    last.then_inc(s["dst_psum"], 1)

                def weights(c, i, b):
                    pe.wait_ge(scal_loaded[b % NB], (i + 1) * 16)
                    pe.wait_ge(s["products_ready"], c + NB)
                    for t in range(TPC):
                        last = mm(p_w[:, t, 0:224], scal[b % NB][:, t * P:(t + 1) * P], m.rbf[:], start=True, stop=True)
                    last.then_inc(s["weights_psum"], 1)

                def values(c, b, first=False):
                    pe.wait_ge(s["products_ready"], c + 1 + NB)
                    pe.wait_ge(s["onehotT_ready"], c + 2)
                    if not first:
                        pe.wait_ge(s["max_taken"], c)
                        pe.wait_ge(s["values_ready"], 3 * c)

                    def turn_tile(t):
                        for j in range(4):
                            last = turn(p_turn[:, j * P:(j + 1) * P], xs[b % 2][:, t, j, :], m.ident[:])
                        last.then_inc(s["turned"], 1)

                    turn_tile(0)
                    for t in range(TPC):
                        pe.wait_ge(s["turned_copied"], c * TPC + t + 1)
                        if t + 1 < TPC:
                            turn_tile(t + 1)
                        xt = xT[t % 2]
                        mm(p_val[:, t, 0:D], xt[:, 3 * P:4 * P], m.att[:], start=True, stop=True)
                        for d in range(3):
                            last = mm(p_val[:, t, D + d * V:D + (d + 1) * V], xt[:, d * P:(d + 1) * P], m.val_v[:],
                                      start=True, stop=True)
                        last.then_inc(s["values_psum"], 1)

                def turn_mask(c):
                    pe.wait_ge(s["mask_ready"], c + 1)
                    for t in range(TPC):
                        last = turn(p_turn[:, t * P:(t + 1) * P], masked[:, t, :, :].rearrange("p h n -> p (h n)"), m.ident[:])
                    last.then_inc(s["mask_psum"], 1)

                def repeat(c):
                    pe.wait_ge(s["max_spread"], c + 1)
                    mm(p_repeat, m.repeat[:], by_head[:], start=True, stop=True).then_inc(s["repeat_psum"], 1)

                def shifts(c, b):
                    pe.wait_ge(s["maxima_ready"], c + 1)
                    for t in range(TPC):
                        last = mm(p_shift[:, t * H:(t + 1) * H], onehotT[b % NB][:, t * P:(t + 1) * P],
                                  win_max[b][0:WS, :], start=True, stop=True)
                    last.then_inc(s["shift_psum"], 1)

                def sums(c, b, half):
                    b = (b - 1) % NB
                    if half == 0:
                        pe.wait_ge(s["attended_ready"], c + 1)
                        pe.wait_ge(s["staged"], c + 1)
                    for h in (2 * half, 2 * half + 1):
                        to = (p_b if half else p_a)[:, (h % 2) * D:(h % 2 + 1) * D]
                        for t in range(TPC):
                            mm(to, attended[b % 2][:, t, 4 * h:4 * h + 4, :].rearrange("p k n -> p (k n)"),
                               z[b % 2][:, t, :], start=(t == 0), stop=(t == TPC - 1))
                    if half == 1:
                        for t in range(TPC):
                            last = mm(p_den, onehot[b][:, t, :], ex[b % 2][:, t, :], start=(t == 0), stop=(t == TPC - 1))
                        last.then_inc(s["summed"], 1)

                pe.sem_inc(s["summed"], 1)
                pe.sem_inc(s["shift_psum"], 2)
                pe.sem_inc(s["values_psum"], 2)
                turn_onehot(0, 0, first=True)
                dst_part(0, 0, 0, 0, first=True)
                dst_part(0, 0, 0, 1, first=True)
                weights(0, 0, 0)
                turn_onehot(1, 1, first=True)
                dst_part(1, 0, 1, 0, first=True)
                dst_part(1, 0, 1, 1, first=True)
                values(0, 0, first=True)
                with pe.Fori(0, ITERS) as i:
                    for b in range(NB):
                        c = i * NB + b
                        after_next = (c + 2, i if b + 2 < NB else i + 1, b + 2)
                        weights(c + 1, i if b + 1 < NB else i + 1, b + 1)
                        turn_mask(c)
                        sums(c, b, 0)
                        repeat(c)
                        turn_onehot(c + 2, b + 2)
                        shifts(c, b)
                        dst_part(*after_next, 0)
                        sums(c, b, 1)
                        dst_part(*after_next, 1)
                        values(c + 1, b + 1)
                for half in range(2):
                    sums(CH, 0, half)
    phase_end(nc, m)


def attention_maximum_phase(nc, m):
    s = names(m, "piece0 piece1 reduced stored")
    PIECES = 4
    per = CH // PIECES
    with ExitStack() as ctx:
        sb = lambda name, shape: ctx.enter_context(nc.sbuf_tensor(m.tag + "am_" + name, shape, F32))
        piece = [sb(f"piece{b}", [P, per, NT * H]) for b in range(2)]
        best, top = sb("best", [P, PIECES, NT * H]), sb("top", [P, NT * H])
        loaded = [s["piece0"], s["piece1"]]
        with nc.Block() as block:
            @block.sync
            def _(sp):
                by_chunk = m.maxima.rearrange("(c p t) h -> p c (t h)", p=P, t=NT)
                for n in range(PIECES):
                    if n >= 2:
                        sp.wait_ge(s["reduced"], n - 1)
                    sp.dma_start(piece[n % 2][:], by_chunk[:, n * per:(n + 1) * per, :]).then_inc(loaded[n % 2], 16)
                sp.wait_ge(s["reduced"], PIECES + 1)
                sp.dma_start(m.amax.rearrange("(p t) h -> p (t h)", t=NT), top[:]).then_inc(s["stored"], 16)
                sp.wait_ge(s["stored"], 16)

            @block.vector
            def _(dve):
                for n in range(PIECES):
                    dve.wait_ge(loaded[n % 2], 16 * (n // 2 + 1))
                    nc.vector.tensor_reduce(best[:, n, :], piece[n % 2][:].rearrange("p c x -> p x c"), AX.X,
                                            ALU.max).then_inc(s["reduced"], 1)
                dve.wait_ge(s["reduced"], PIECES)
                nc.vector.tensor_reduce(top[:], best[:].rearrange("p n x -> p x n"), AX.X, ALU.max).then_inc(s["reduced"], 1)
    phase_end(nc, m)


def attention_add_phase(nc, m):
    s = names(m, "win_ready row_ready turns diffed shifted exp_ready scaled_ready landed l0 l1 l2 l3",
              "g0 g1 g2 g3 s0 s1 s2 s3")
    gathered, scattered = [s["g0"], s["g1"], s["g2"], s["g3"]], [s["s0"], s["s1"], s["s2"], s["s3"]]
    loaded = [s["l0"], s["l1"], s["l2"], s["l3"]]
    with ExitStack() as ctx:
        sb = lambda name, shape, dt=F32: [ctx.enter_context(nc.sbuf_tensor(m.tag + f"aa_{name}{b}", shape, dt)) for b in range(NB)]
        win_col, row_col = sb("win", [P, 1], I32), sb("row", [P, 1], I32)
        raw, scaled = sb("raw", [P, ROW0]), sb("scaled", [P, ROW0])
        top, diff, factor = sb("top", [P, H]), sb("diff", [P, H]), sb("factor", [P, H])
        with nc.Block() as block:
            @block.sync
            def _(sp):
                def load(c, b):
                    sp.dma_start(raw[b][:], m.chunk_sums[bass.ds(c + 1, 1), :, :].rearrange("o p f -> p (o f)")
                                 ).then_inc(loaded[b], 16)

                for b in range(NB):
                    load(b, b)
                with sp.Fori(0, ITERS - 1) as i:
                    for b in range(NB):
                        sp.wait_ge(s["scaled_ready"], (i * NB + b + 1) * 2 + 2 * NB)
                        load((i + 1) * NB + b, b)

            @block.scalar
            def _(act):
                def window_column(c, b):
                    nc.scalar.copy(win_col[b][:], m.node_rows[:, bass.ds(c, 1)]).then_inc(s["win_ready"], 1)

                for b in range(NB):
                    window_column(b, b)
                with act.Fori(0, ITERS) as i:
                    for b in range(NB):
                        c = i * NB + b
                        act.wait_ge(s["landed"], c + 1)
                        nc.scalar.copy(row_col[b][:], m.window_rows[:, 0, bass.ds(c, 1)]).then_inc(s["row_ready"], 1)
                        act.wait_ge(s["shifted"], c + 1)
                        act.wait_ge(s["scaled_ready"], (c + 1) * 2)
                        nc.scalar.activation(factor[b][:], diff[b][:], ACT.Exp).then_inc(s["exp_ready"], 1)
                        act.wait_ge(gathered[b], (i + 1) * 16)
                        window_column(c + NB, b)

            @block.gpsimd
            def _(pool):
                def gather(c, b):
                    pool.wait_ge(s["win_ready"], c + 1)
                    pool.wait_ge(s["diffed"], c + 1)
                    pool.sem_inc(s["turns"], 1)
                    nc.gpsimd.indirect_dma_start(
                        out=top[b][:], out_offset=None, in_=m.amax,
                        in_offset=IndirectOffsetOnAxis(ap=win_col[b][:], axis=0)).then_inc(gathered[b], 16)

                pool.sem_inc(s["landed"], NB)
                for b in range(NB):
                    gather(b, b)
                with pool.Fori(0, ITERS) as i:
                    for b in range(NB):
                        c = i * NB + b
                        pool.wait_ge(s["scaled_ready"], (c + 1) * 2 + 2 * NB)
                        pool.wait_ge(s["row_ready"], c + 1)
                        pool.sem_inc(s["turns"], 1)
                        nc.gpsimd.indirect_dma_start(
                            out=m.att_sums, out_offset=IndirectOffsetOnAxis(ap=row_col[b][:], axis=0),
                            in_=scaled[b][:], in_offset=None, compute_op=ALU.add).then_inc(scattered[b], 16)
                        gather(c + NB, b)
                        pool.wait_ge(scattered[b], (i + 1) * 16)
                        pool.sem_inc(s["landed"], 1)
                for b in range(NB):
                    pool.wait_ge(gathered[b], (ITERS + 1) * 16)

            @block.vector
            def _(dve):
                tt = nc.vector.tensor_tensor

                def shift(c, i, b):
                    dve.wait_ge(gathered[b], (i + 1) * 16)
                    tt(diff[b][:].unsqueeze(1), m.all_max[:, bass.ds(c, 1), :], top[b][:].unsqueeze(1),
                       ALU.subtract).then_inc(s["diffed"], 1)
                    dve.wait_ge(s["diffed"], c + 1 + NB)
                    nc.vector.tensor_scalar(diff[b][:], diff[b][:], -1e4, None, ALU.max).then_inc(s["shifted"], 1)

                dve.sem_inc(s["diffed"], NB)
                dve.sem_inc(s["scaled_ready"], 2 * NB)
                shift(0, 0, 0)
                with dve.Fori(0, ITERS) as i:
                    for b in range(NB):
                        c = i * NB + b
                        shift(c + 1, *((i, b + 1) if b + 1 < NB else (i + 1, 0)))
                        dve.wait_ge(s["exp_ready"], c + 1)
                        dve.wait_ge(loaded[b], (i + 1) * 16)
                        dve.wait_ge(s["landed"], c + 1)
                        tt(scaled[b][:, 0:H * D].rearrange("p (h f) -> p h f", h=H),
                           raw[b][:, 0:H * D].rearrange("p (h f) -> p h f", h=H),
                           factor[b][:].unsqueeze(2).to_broadcast([P, H, D]), ALU.mult).then_inc(s["scaled_ready"], 1)
                        tt(scaled[b][:, H * D:ROW0], raw[b][:, H * D:ROW0], factor[b][:], ALU.mult).then_inc(s["scaled_ready"], 1)
    phase_end(nc, m)


def attention_node_phase(nc, m):
    s = names(m, "l0 l1 assembled linked turned turned_copied projected kept")
    loaded = [s["l0"], s["l1"]]
    NL, NA = 8, 5
    with ExitStack() as ctx:
        sb = lambda name, shape: [ctx.enter_context(nc.sbuf_tensor(m.tag + f"an_{name}{b}", shape, F32)) for b in range(2)]
        sums, mid = sb("sums", [P, 4, ROW0]), sb("mid", [P, H, 4, P])
        rden = sb("rden", [P, H])
        midT = sb("midT", [P, H * P])
        p_turn = [ctx.enter_context(nc.psum_tensor(m.tag + f"an_pt{b}", [P, 512], F32)) for b in range(2)]
        p_out = ctx.enter_context(nc.psum_tensor(m.tag + "an_po", [P, 512], F32))
        tt, ts = nc.vector.tensor_tensor, nc.vector.tensor_scalar

        def tiles(eng, body):
            with eng.Fori(0, NT // 2) as i:
                for b in range(2):
                    body(i * 2 + b, b, i)
            body(NT - 1, 0, NT // 2)

        with nc.Block() as block:
            @block.sync
            def _(sp):
                rows = m.att_sums.rearrange("(k p t) f -> k p t f", k=4, t=NT)

                def load(t, b, i):
                    sp.wait_ge(s["assembled"], (t + 1) * NA)
                    for k in range(4):
                        sp.dma_start(sums[b][:, k, :].unsqueeze(1), rows[k][:, bass.ds(t, 1), :]).then_inc(loaded[b], 16)
                tiles(sp, load)

            @block.vector
            def _(dve):
                def assemble(t, b, i):
                    T, M = sums[b][:, :, 0:H * D].rearrange("p k (h f) -> p h k f", h=H), mid[b]
                    v = lambda k, d: T[:, :, k, S + d * V:S + (d + 1) * V]
                    r = lambda n: rden[b][:].unsqueeze(2).to_broadcast([P, H, n])
                    r3 = lambda n: rden[b][:].unsqueeze(2).unsqueeze(3).to_broadcast([P, H, 3, n])
                    dve.wait_ge(loaded[b], (i + 1) * 64)
                    dve.wait_ge(s["turned"], t * 4 + 4)
                    ts(rden[b][:], sums[b][:, 0, H * D:ROW0], 1e-16, None, ALU.add).then_inc(s["linked"], 1)
                    for d in range(3):
                        tt(M[:, :, d, 96:P], v((d + 2) % 3, (d + 1) % 3), v((d + 1) % 3, (d + 2) % 3),
                           ALU.subtract).then_inc(s["linked"], 1)
                    tt(M[:, :, 3, S:96], v(0, 0), v(1, 1), ALU.add).then_inc(s["linked"], 1)
                    dve.wait_ge(s["linked"], t * NL + 5)
                    tt(M[:, :, 3, S:96], M[:, :, 3, S:96], v(2, 2), ALU.add).then_inc(s["linked"], 1)
                    nc.vector.reciprocal(rden[b][:], rden[b][:]).then_inc(s["linked"], 1)
                    dve.wait_ge(s["linked"], t * NL + 7)
                    for d in range(3):
                        last = tt(M[:, :, d, 0:S], T[:, :, d, 0:S], r(S), ALU.mult)
                        last.then_inc(s["assembled"], 1) if d == 2 else None
                    for d in range(3):
                        last = tt(M[:, :, d, S:96], v(3, d), r(V), ALU.mult)
                        last.then_inc(s["assembled"], 1) if d == 2 else None
                    for d in range(3):
                        last = tt(M[:, :, d, 96:P], M[:, :, d, 96:P], r(V), ALU.mult)
                        last.then_inc(s["assembled"], 1) if d == 2 else None
                    tt(M[:, :, 3, 0:S], T[:, :, 3, 0:S], r(S), ALU.mult).then_inc(s["assembled"], 1)
                    tt(M[:, :, 3, S:96], M[:, :, 3, S:96], r(V), ALU.mult).then_inc(s["linked"], 1)
                    dve.wait_ge(s["linked"], t * NL + 8)
                    dve.sem_inc(s["assembled"], 1)

                dve.sem_inc(s["assembled"], 2 * NA)
                for b in range(2):
                    nc.vector.memset(mid[b][:, :, 3, 96:P], 0.0)
                tiles(dve, assemble)
                dve.wait_ge(s["kept"], NT + 1)
                h = m.h
                nc.vector.scalar_tensor_tensor(h[:], m.x[:], 2.0, h[:], ALU.mult, ALU.add)

            @block.tensor
            def _(pe):
                def project(t, b, i):
                    pe.wait_ge(s["assembled"], (t + 1) * NA + 2 * NA)

                    def turn(j):
                        pe.wait_ge(s["turned_copied"], t * 4 + j + 1)
                        for h in range(H):
                            last = nc.tensor.transpose(p_turn[j % 2][:, h * P:(h + 1) * P], mid[b][:, h, j, :], m.ident[:])
                        last.then_inc(s["turned"], 1)

                    turn(0)
                    pe.wait_ge(s["kept"], t + 1)
                    for j in range(4):
                        if j < 3:
                            turn(j + 1)
                        pe.wait_ge(s["turned_copied"], t * 4 + j + 3)
                        to, w, n = (p_out[:, 0:S], m.out_s, S) if j == 3 else (p_out[:, S + j * V:S + (j + 1) * V], m.out_v, V)
                        for h in range(H):
                            last = nc.tensor.matmul(to, midT[j % 2][:, h * P:(h + 1) * P], w[:, h * n:(h + 1) * n],
                                                    start=(h == 0), stop=(h == H - 1))
                        last.then_inc(s["projected"], 1)

                pe.sem_inc(s["turned"], 8)
                pe.sem_inc(s["projected"], 2)
                tiles(pe, project)

            @block.scalar
            def _(act):
                def keep(t, b, i):
                    for j in range(4):
                        act.wait_ge(s["turned"], t * 4 + j + 1 + 8)
                        act.wait_ge(s["projected"], t * 4 + j + 1)
                        nc.scalar.copy(midT[j % 2][:], p_turn[j % 2][:]).then_inc(s["turned_copied"], 1)
                    act.wait_ge(s["projected"], t * 4 + 4 + 2)
                    nc.scalar.copy(m.h[:, bass.ds(t, 1), :].rearrange("p o f -> p (o f)"), p_out[:, 0:D]).then_inc(s["kept"], 1)

                act.sem_inc(s["turned_copied"], 2)
                act.sem_inc(s["kept"], 1)
                tiles(act, keep)
    phase_end(nc, m)


def attention_layer(nc, m, io, rounds):
    with ExitStack() as ctx:
        sb = lambda name, shape, dt=F32: ctx.enter_context(nc.sbuf_tensor(m.tag + "al_" + name, shape, dt))
        m.rbf, m.att, m.val_v = sb("rbf", [16, 224]), sb("att", [P, D]), sb("val_v", [P, V])
        m.alpha, m.gamma_s, m.beta_s, m.gamma_v = [sb(name, [P, n]) for name, n in
                                                    (("alpha", S), ("gamma_s", S), ("beta_s", S), ("gamma_v", V))]
        m.head_mask, m.repeat = sb("head_mask", [P, H]), sb("repeat", [P, P])
        m.out_s, m.out_v = sb("out_s", [P, H * S]), sb("out_v", [P, H * V])
        m.lin_a, m.lin_b = sb("lin_a", [P, 2 * D]), sb("lin_b", [V, 2 * D])
        m.ones = sb("ones", [P, NT])
        attention_weights_phase(nc, m, io)
        with ExitStack() as inner:
            m.xn = inner.enter_context(nc.sbuf_tensor(m.tag + "al_xn", [P, NT, D], F32))
            m.own = inner.enter_context(nc.sbuf_tensor(m.tag + "al_own", [P, NT, D], F32))
            equivariant_norm_phase(nc, m)
            node_linear_phase(nc, m, m.xn, m.ones, m.dst_table)
        m.node_rows_f, m.node_rows = sb("node_rows_f", [P, CH]), sb("node_rows", [P, CH + NB], I32)
        m.maxima_rows, m.chunk_rows = sb("maxima_rows", [P, CH + NB], I32), sb("chunk_rows", [P, CH])
        m.all_max = sb("all_max", [P, CH + NB, H])
        attention_clear_phase(nc, m, io)
        with nc.Fori(0, rounds):
            window_phase(nc, m)
            attention_window_phase(nc, m)
            attention_edge_phase(nc, m, io)
            attention_maximum_phase(nc, m)
            attention_add_phase(nc, m)
        m.h = sb("h", [P, NT, D])
        attention_node_phase(nc, m)
        layernorm_phase(nc, m)


def build(nc, io, out, layers=(0, 1, 2, 3)):
    m = Memory()
    with ExitStack() as ctx:
        sb = lambda name, shape, dt=F32: ctx.enter_context(nc.sbuf_tensor(name, shape, dt))
        m.sems = [ctx.enter_context(nc.semaphore(f"phase{n}")) for n in range(36)]
        m.dma_sems = [ctx.enter_context(nc.semaphore(f"gpsimd_dma{n}")) for n in range(20)]
        nums = [sem.num for sem in m.sems + m.dma_sems]
        assert nums == list(range(nums[0], nums[0] + len(nums)))
        m.sem_range = range(nums[0], nums[-1] + 1)
        m.dma_range = range(m.dma_sems[0].num, nums[-1] + 1)
        m.dst_i = sb("dst_i", [P, CH * TPC], I32)
        m.src = sb("src", [P, (CH + NB) * TPC], I32)
        m.dst_f = sb("dst_f", [P, CH * TPC])
        m.rel = sb("rel", [P, (CH + NB) * TPC])
        m.y = sb("y", [P, (CH + NB) * TPC * NY])
        m.ident = sb("ident", [P, P])
        m.iota = sb("iota", [P, WS])
        m.rows = sb("rows", [P, 4])
        m.attr = sb("attr", [P, NT])
        m.x = sb("x", [P, NT, D])
        m.zero = sb("zero", [P, NT * D])
        m.eps = sb("eps", [P, 1])
        m.ends = sb("ends", [P, 2 * CH])
        m.span = sb("span", [P, 2 * CH])
        m.fits = sb("fits", [P, 1])
        m.base0 = sb("base0", [P, CH])
        m.base = sb("base", [P, CH])
        m.window_rows = sb("window_rows", [P, 2, CH + NB], I32)
        m.rounds_i = sb("rounds_i", [1, 1], I32)
        m.rounds_dram = nc.dram_tensor("rounds", (1, 1), I32, kind="Internal").ap()
        m.sums = nc.dram_tensor("sums", (NY * NP, D), F32, kind="Internal").ap()
        m.by_src = [nc.dram_tensor(f"by_src{t}", (NP + P, D), F32, kind="Internal").ap() for t in range(TPC)]
        m.table = nc.dram_tensor("table", (NP, D), F32, kind="Internal").ap()
        setup_phase(nc, m, io)
        rounds = nc.values_load(m.rounds_dram, min_val=1, max_val=ROUNDS)
        if 0 in layers:
            m.tag = "L0_"
            m.dst_table = nc.dram_tensor("dst_table", (NP, D), F32, kind="Internal").ap()
            m.maxima = nc.dram_tensor("maxima", (CH * NP, H), F32, kind="Internal").ap()
            m.amax = nc.dram_tensor("amax", (NP, H), F32, kind="Internal").ap()
            m.chunk_sums = nc.dram_tensor("chunk_sums", (CH + 1, P, ROW0), F32, kind="Internal").ap()
            m.att_sums = nc.dram_tensor("att_sums", (4 * NP, ROW0), F32, kind="Internal").ap()
            attention_layer(nc, m, io, rounds)
        if 1 in layers:
            m.tag = "L1_"
            w = Memory()
            w.K, w.fc1, w.fc2 = 8, io["L1_gnn_fc_w1"], io["L1_gnn_fc_w2"]
            w.sc_s, w.sc_v, w.lin_s, w.lin_v = io["L1_gnn_sc_w0"], io["L1_gnn_sc_w1"], io["L1_gnn_lin1_w0"], io["L1_gnn_lin1_w1"]
            w.out_s, w.out_v, w.angle = io["L1_gnn_lin2_w0"], io["L1_gnn_lin2_w1"], io["L1_gnn_lin3_w"]
            conv_layer(nc, m, io, w, io["a8"], 1.0, 0.25 * 96 ** -0.5, 0.1 * 0.25 * 96 ** -0.5, rounds)
        if 2 in layers:
            m.tag = "L2_"
            w = Memory()
            w.K, w.fc1, w.fc2 = 16, io["L2_gnn_fc_W1"], io["L2_gnn_fc_W2"]
            w.sc_s, w.sc_v, w.lin_s, w.lin_v = io["L2_gnn_W_sc0"], io["L2_gnn_W_sc1"], io["L2_gnn_W_l1_0"], io["L2_gnn_W_l1_1"]
            w.out_s, w.out_v, w.angle = io["L2_gnn_W_l2_0"], io["L2_gnn_W_l2_1"], None
            conv_layer(nc, m, io, w, io["a16"], math.sin(math.pi / 8), math.cos(math.pi / 8) * 10 ** -0.5 * 96 ** -0.5,
                       None, rounds)
        if 3 in layers:
            m.tag = "L3_"
            update_layer(nc, m, io, rounds)
        s = names(m, "stored")
        with nc.Block() as block:
            @block.sync
            def _(sp):
                sp.dma_start(out.rearrange("(p t) f -> p t f", t=NT), m.x[:]).then_inc(s["stored"], 16)
                sp.wait_ge(s["stored"], 16)


def kernel(**inputs):
    import numpy as np
    import concourse.bacc as _bacc
    from concourse import mybir as _mybir
    from concourse.bass_utils import run_bass_kernel_spmd as _run

    epad = CH * TPC * P - EDGES

    def by_edge(a, fill="edge"):
        a = np.pad(a, [(0, epad)] + [(0, 0)] * (a.ndim - 1), mode=fill)
        return np.ascontiguousarray(np.moveaxis(a.reshape(CH * TPC, P, *a.shape[1:]), 0, 1))

    def d_major(a):
        return np.concatenate([a[:, :S], a[:, S:].reshape(-1, V, 3).transpose(0, 2, 1).reshape(-1, 3 * V)], 1)

    g = {k: np.asarray(v) for k, v in inputs.items()}
    attr4 = by_edge(g["edge_attr_4"], "constant")
    valid = by_edge(np.ones((EDGES, 1), np.float32), "constant")
    n = np.arange(P)
    iota = np.where(np.arange(WS) < W, np.arange(WS), -1e6).astype(np.float32)
    arrays = {
        "x": np.pad(d_major(g["x"]), [(0, NP - NODES), (0, 0)]),
        "attr": np.pad(g["node_vec1"][:, 0], (0, NP - NODES)).reshape(P, NT),
        "src": np.pad(by_edge(g["src"]), [(0, 0), (0, NB * TPC)]),
        "dst": by_edge(g["dst"]),
        "y": np.pad(np.concatenate([attr4[:, :, 1:4], attr4[:, :, 0:1], valid], 2), [(0, 0), (0, NB * TPC), (0, 0)]).reshape(P, -1),
        "a8": np.pad(g["edge_attr_8"].T, [(0, 0), (0, epad + NB * TPC * P)]),
        "a16": np.pad(g["edge_attr_16"].T, [(0, 0), (0, epad + NB * TPC * P)]),
        "ident": np.eye(P, dtype=np.float32),
        "lower": np.tril(np.ones((P, P), np.float32), -1),
        "src_rows": np.pad(g["src"], (0, epad + NB * TPC * P), mode="edge").reshape(CH + NB, TPC * P),
        "iota": np.tile(iota, (P, 1)),
        "rows": np.stack([n // WS * NP + n % WS, np.minimum(n // W, NY - 1) * NP + n % W, NP + n, n % WS], 1).astype(np.float32),
    }
    arrays.update({k: v for k, v in g.items() if k.startswith("L")})
    for k in ("wm000", "wm011", "wm101", "wm110", "wu011"):
        arrays["L3_gnn_" + k] = g["L3_gnn_" + k].reshape(g["L3_gnn_" + k].shape[0], -1)
    for k in ("wu000", "wu110"):
        arrays["L3_gnn_" + k] = g["L3_gnn_" + k].reshape(-1, S)
    arrays["L3_gnn_wu101"] = g["L3_gnn_wu101"].transpose(1, 0, 2).reshape(S, -1)
    L0 = lambda k: g["L0_gnn_" + k]
    by_head = lambda a, n: a.reshape(a.shape[0], H, n)
    row = lambda a: np.tile(a.reshape(1, -1), (P, 1))
    arrays.update({
        "alpha_rows": row(L0("alpha_dot")), "gamma_s_rows": row(L0("gamma_s")), "beta_s_rows": row(L0("beta_s")),
        "gamma_v_rows": row(L0("gamma_v")),
        "head_mask": (n[:, None] // WS == np.arange(H)).astype(np.float32),
        "repeat": (n[:, None] % WS == n % WS).astype(np.float32),
        "chunk_rows": row(np.arange(CH) * NP).astype(np.float32),
        "valT": L0("Ws_val").T,
        "slT": by_head(L0("Ws_vlin"), AS).transpose(2, 1, 0).reshape(AS, -1),
        "ps_w": L0("Wps").reshape(H, AS, S).transpose(1, 0, 2).reshape(AS, -1),
        "vlT": by_head(L0("Wv_vlin"), AV).transpose(2, 1, 0).reshape(AV, -1),
        "pv_w": L0("Wpv").reshape(H, AV, V).transpose(1, 0, 2).reshape(AV, -1),
    })
    arrays.update({k: L0(k).reshape(-1, 1) for k in ("w2_ss", "w2_sv", "w2_vs", "w2_vv0", "w2_vv1")})
    nc = _bacc.Bacc("TRN2", target_bir_lowering=False, num_devices=1)
    arrays = {k: np.ascontiguousarray(v) for k, v in arrays.items()}
    io = {
        k: nc.dram_tensor(f"in_{k}", v.shape, _mybir.dt.from_np(v.dtype), kind="ExternalInput").ap()
        for k, v in arrays.items()}
    out = nc.dram_tensor("out", (NP, D), F32, kind="ExternalOutput").ap()
    build(nc, io, out, LAYERS)
    r = _run(nc, [{f"in_{k}": v for k, v in arrays.items()}], core_ids=[0]).results[0]["out"]
    r = r[:NODES]
    return np.concatenate([r[:, :S], r[:, S:].reshape(-1, 3, V).transpose(0, 2, 1).reshape(-1, 3 * V)], 1)
```
